# Optimizing a Trainium2 kernel written in Bass

```python
import numpy as np
import jax
import jax.numpy as jnp

def _softmax(x, axis=-1):
    return jax.nn.softmax(x, axis=axis)

def _gelu(x):
    return jax.nn.gelu(x, approximate=True)

def _silu(x):
    return jax.nn.silu(x)

def _sigmoid(x):
    return jax.nn.sigmoid(x)

def _layernorm(x, axis=-1, eps=1e-05):
    m = jnp.mean(x, axis=axis, keepdims=True)
    v = jnp.var(x, axis=axis, keepdims=True)
    return (x - m) / jnp.sqrt(v + eps)

def _scatter_add(tgt, idx, src, axis=0):
    return tgt.at[idx].add(src)

def _segment_sum(src, seg, n):
    return jax.ops.segment_sum(src, seg, n)
kernel_name = 'mk_seq_postln_d2_jaxref_r4_5e042b'

def setup_inputs(seed: int=0):
    np.random.seed(seed)
    _w = jnp.asarray

    def _L0_attn_setup():
        import jax, jax.numpy as jnp
        import numpy as np
        import math
        H = 16
        N_EMBD = 256
        EPS = 1e-05
        key = jax.random.key(seed)
        ks = jax.random.split(key, 6)
        B, T, C = (2, 512, 256)
        x = jax.random.normal(ks[0], (B, T, C), dtype=jnp.float32)
        s = 0.02
        Wq = jax.random.normal(ks[1], (C, N_EMBD), dtype=jnp.float32) * s
        Wk = jax.random.normal(ks[2], (C, N_EMBD), dtype=jnp.float32) * s
        Wv = jax.random.normal(ks[3], (C, N_EMBD), dtype=jnp.float32) * s
        Wo = jax.random.normal(ks[4], (N_EMBD, C), dtype=jnp.float32) * s
        return {'x': x, 'Wq': Wq, 'bq': jnp.zeros((N_EMBD,), jnp.float32), 'Wk': Wk, 'bk': jnp.zeros((N_EMBD,), jnp.float32), 'Wv': Wv, 'bv': jnp.zeros((N_EMBD,), jnp.float32), 'Wo': Wo, 'bo': jnp.zeros((C,), jnp.float32), 'gamma': jnp.ones((C,), jnp.float32), 'beta': jnp.zeros((C,), jnp.float32)}
    _L0_attn_in = _L0_attn_setup()

    def _L0_ffn_setup():
        import jax, jax.numpy as jnp
        import numpy as np
        EPS = 1e-05

        @jax.custom_vjp
        def ste_quantize(w):
            scale = jnp.maximum(jnp.mean(jnp.abs(w)), EPS)
            return jnp.clip(jnp.round(w / scale), -1.0, 1.0)

        def _ste_fwd(w):
            return (ste_quantize(w), None)

        def _ste_bwd(_, g):
            return (g,)
        ste_quantize.defvjp(_ste_fwd, _ste_bwd)
        key = jax.random.key(seed)
        k1, k2 = jax.random.split(key)
        x = jax.random.normal(k1, (8, 2048, 256), dtype=jnp.float32)
        weight = jax.random.normal(k2, (256, 256), dtype=jnp.float32) * 0.02
        return {'x': x, 'weight': weight}
    _L0_ffn_in = _L0_ffn_setup()

    def _L1_attn_setup():
        import jax, jax.numpy as jnp
        import numpy as np
        import math
        N_HEAD = 16
        N_KV_HEAD = 4
        WINDOW = 128
        EPS = 1e-06

        def _rotate_half(t):
            t1, t2 = jnp.split(t, 2, axis=-1)
            return jnp.concatenate([-t2, t1], axis=-1)

        def _rope_tables(T, head_dim):
            theta = 1.0 / 10000.0 ** (jnp.arange(0, head_dim, 2, dtype=jnp.float32) / head_dim)
            pos = jnp.arange(T, dtype=jnp.float32)
            freqs = jnp.outer(pos, theta)
            cos = jnp.concatenate([jnp.cos(freqs), jnp.cos(freqs)], axis=-1)
            sin = jnp.concatenate([jnp.sin(freqs), jnp.sin(freqs)], axis=-1)
            return (cos, sin)
        key = jax.random.key(seed)
        k1, k2, k3, k4 = jax.random.split(key, 4)
        B, T, C = (1, 512, 256)
        kv_out = 2 * N_KV_HEAD * (C // N_HEAD)
        x = jax.random.normal(k1, (B, T, C), dtype=jnp.float32)
        Wq = jax.random.normal(k2, (C, C), dtype=jnp.float32) * 0.02
        Wkv = jax.random.normal(k3, (kv_out, C), dtype=jnp.float32) * 0.02
        Wproj = jax.random.normal(k4, (C, C), dtype=jnp.float32) * 0.02
        return {'x': x, 'Wq': Wq, 'Wkv': Wkv, 'Wproj': Wproj}
    _L1_attn_in = _L1_attn_setup()

    def _L1_ffn_setup():
        import jax, jax.numpy as jnp
        import numpy as np
        B, S, D = (2, 512, 256)
        H, E, P, K = (8, 8, 128, 2)
        SCALE = 1.0 / np.sqrt(P)

        def _get_sel_gate(x, w, route_scale):
            logits = jnp.einsum('bsd,ed->bse', x, w).astype(jnp.float32)
            raw = logits.reshape(x.shape[0], x.shape[1], H, E)
            probs = jax.nn.sigmoid(raw)
            vals, idx = jax.lax.top_k(probs, K)
            vals = vals / jnp.clip(vals.sum(-1, keepdims=True), 1e-09)
            vals = vals * route_scale
            gate = (jax.nn.one_hot(idx, E, dtype=vals.dtype) * vals[..., None]).sum(-2)
            return gate
        key = jax.random.key(seed)
        ks = jax.random.split(key, 8)
        std = 1.0 / np.sqrt(D)
        return {'x': jax.random.normal(ks[0], (B, S, D), jnp.float32), 'q_w': jax.random.normal(ks[1], (H * P, D), jnp.float32) * std, 'k_w': jax.random.normal(ks[2], (H * P, D), jnp.float32) * std, 'v_w': jax.random.normal(ks[3], (H * E, D, P), jnp.float32) * std, 'o_w': jax.random.normal(ks[4], (H * E, P, D), jnp.float32) * (1.0 / np.sqrt(H * P)), 'sel_v_w': jax.random.normal(ks[5], (H * E, D), jnp.float32) * std, 'sel_o_w': jax.random.normal(ks[6], (H * E, D), jnp.float32) * std, 'route_scale': jnp.ones((1,), jnp.float32)}
    _L1_ffn_in = _L1_ffn_setup()
    _d = {'L0_attn_x': _L0_attn_in['x'], 'L0_attn_Wq': _L0_attn_in['Wq'], 'L0_attn_bq': _L0_attn_in['bq'], 'L0_attn_Wk': _L0_attn_in['Wk'], 'L0_attn_bk': _L0_attn_in['bk'], 'L0_attn_Wv': _L0_attn_in['Wv'], 'L0_attn_bv': _L0_attn_in['bv'], 'L0_attn_Wo': _L0_attn_in['Wo'], 'L0_attn_bo': _L0_attn_in['bo'], 'L0_attn_gamma': _L0_attn_in['gamma'], 'L0_attn_beta': _L0_attn_in['beta'], 'L0_ffn_weight': _L0_ffn_in['weight'], 'L1_attn_Wq': _L1_attn_in['Wq'], 'L1_attn_Wkv': _L1_attn_in['Wkv'], 'L1_attn_Wproj': _L1_attn_in['Wproj'], 'L1_ffn_q_w': _L1_ffn_in['q_w'], 'L1_ffn_k_w': _L1_ffn_in['k_w'], 'L1_ffn_v_w': _L1_ffn_in['v_w'], 'L1_ffn_o_w': _L1_ffn_in['o_w'], 'L1_ffn_sel_v_w': _L1_ffn_in['sel_v_w'], 'L1_ffn_sel_o_w': _L1_ffn_in['sel_o_w'], 'L1_ffn_route_scale': _L1_ffn_in['route_scale']}
    _x0 = _d['L0_attn_x']
    _d['L0_attn_x'] = jax.random.normal(jax.random.fold_in(jax.random.key(seed), 1), (8, 512, 256), dtype=_x0.dtype)
    del _x0
    return _d

def reference(L0_attn_x, L0_attn_Wq, L0_attn_bq, L0_attn_Wk, L0_attn_bk, L0_attn_Wv, L0_attn_bv, L0_attn_Wo, L0_attn_bo, L0_attn_gamma, L0_attn_beta, L0_ffn_weight, L1_attn_Wq, L1_attn_Wkv, L1_attn_Wproj, L1_ffn_q_w, L1_ffn_k_w, L1_ffn_v_w, L1_ffn_o_w, L1_ffn_sel_v_w, L1_ffn_sel_o_w, L1_ffn_route_scale):

    def _L0_attn_ref(x, Wq, bq, Wk, bk, Wv, bv, Wo, bo, gamma, beta):
        import jax, jax.numpy as jnp
        import numpy as np
        import math
        H = 16
        N_EMBD = 256
        EPS = 1e-05
        B, T, _ = x.shape
        Dh = N_EMBD // H

        def split_heads(y):
            return y.reshape(B, T, H, Dh).transpose(0, 2, 1, 3)
        q = split_heads(x @ Wq + bq)
        k = split_heads(x @ Wk + bk)
        v = split_heads(x @ Wv + bv)
        att = jnp.einsum('bhtd,bhsd->bhts', q, k) * (1.0 / math.sqrt(Dh))
        causal = jnp.tril(jnp.ones((T, T), dtype=bool))
        att = jnp.where(causal[None, None], att, -jnp.inf)
        att = jax.nn.softmax(att, axis=-1)
        o = jnp.einsum('bhts,bhsd->bhtd', att, v)
        o = o.transpose(0, 2, 1, 3).reshape(B, T, N_EMBD)
        y = o @ Wo + bo
        mu = jnp.mean(y, axis=-1, keepdims=True)
        var = jnp.var(y, axis=-1, keepdims=True)
        return (y - mu) * jax.lax.rsqrt(var + EPS) * gamma + beta

    def _L0_ffn_ref(x, weight):
        import jax, jax.numpy as jnp
        import numpy as np
        EPS = 1e-05

        @jax.custom_vjp
        def ste_quantize(w):
            scale = jnp.maximum(jnp.mean(jnp.abs(w)), EPS)
            return jnp.clip(jnp.round(w / scale), -1.0, 1.0)

        def _ste_fwd(w):
            return (ste_quantize(w), None)

        def _ste_bwd(_, g):
            return (g,)
        ste_quantize.defvjp(_ste_fwd, _ste_bwd)
        w_ternary = ste_quantize(weight)
        scale = jnp.maximum(jnp.mean(jnp.abs(weight)), EPS)
        return jnp.einsum('bsi,oi->bso', x, w_ternary * scale)

    def _L1_attn_ref(x, Wq, Wkv, Wproj):
        import jax, jax.numpy as jnp
        import numpy as np
        import math
        N_HEAD = 16
        N_KV_HEAD = 4
        WINDOW = 128
        EPS = 1e-06

        def _rotate_half(t):
            t1, t2 = jnp.split(t, 2, axis=-1)
            return jnp.concatenate([-t2, t1], axis=-1)

        def _rope_tables(T, head_dim):
            theta = 1.0 / 10000.0 ** (jnp.arange(0, head_dim, 2, dtype=jnp.float32) / head_dim)
            pos = jnp.arange(T, dtype=jnp.float32)
            freqs = jnp.outer(pos, theta)
            cos = jnp.concatenate([jnp.cos(freqs), jnp.cos(freqs)], axis=-1)
            sin = jnp.concatenate([jnp.sin(freqs), jnp.sin(freqs)], axis=-1)
            return (cos, sin)
        B, T, C = x.shape
        H, KV = (N_HEAD, N_KV_HEAD)
        d = C // H
        n_rep = H // KV
        q = (x @ Wq.T).reshape(B, T, H, d).transpose(0, 2, 1, 3)
        kv = x @ Wkv.T
        k, v = jnp.split(kv, 2, axis=2)
        k = k.reshape(B, T, KV, d).transpose(0, 2, 1, 3)
        v = v.reshape(B, T, KV, d).transpose(0, 2, 1, 3)
        q = q / (jnp.linalg.norm(q, axis=-1, keepdims=True) + EPS)
        k = k / (jnp.linalg.norm(k, axis=-1, keepdims=True) + EPS)
        cos, sin = _rope_tables(T, d)
        cos = cos[None, None]
        sin = sin[None, None]
        q = q * cos + _rotate_half(q) * sin
        k = k * cos + _rotate_half(k) * sin
        k = jnp.repeat(k, n_rep, axis=1)
        v = jnp.repeat(v, n_rep, axis=1)
        rows = jnp.arange(T)[:, None]
        cols = jnp.arange(T)[None, :]
        mask = (cols <= rows) & (cols > rows - WINDOW)
        scale = 1.0 / math.sqrt(d)
        scores = jnp.einsum('bhqd,bhkd->bhqk', q, k) * scale
        scores = jnp.where(mask[None, None], scores, -jnp.inf)
        attn = jax.nn.softmax(scores, axis=-1)
        y = jnp.einsum('bhqk,bhkd->bhqd', attn, v)
        y = y.transpose(0, 2, 1, 3).reshape(B, T, C)
        return y @ Wproj.T

    def _L1_ffn_ref(x, q_w, k_w, v_w, o_w, sel_v_w, sel_o_w, route_scale):
        import jax, jax.numpy as jnp
        import numpy as np
        B, S, D = (2, 512, 256)
        H, E, P, K = (8, 8, 128, 2)
        SCALE = 1.0 / np.sqrt(P)

        def _get_sel_gate(x, w, route_scale):
            logits = jnp.einsum('bsd,ed->bse', x, w).astype(jnp.float32)
            raw = logits.reshape(x.shape[0], x.shape[1], H, E)
            probs = jax.nn.sigmoid(raw)
            vals, idx = jax.lax.top_k(probs, K)
            vals = vals / jnp.clip(vals.sum(-1, keepdims=True), 1e-09)
            vals = vals * route_scale
            gate = (jax.nn.one_hot(idx, E, dtype=vals.dtype) * vals[..., None]).sum(-2)
            return gate
        rs = route_scale[0]
        gate_v = _get_sel_gate(x, sel_v_w, rs)
        gate_o = _get_sel_gate(x, sel_o_w, rs)
        q = jnp.einsum('bsd,hpd->bhsp', x, q_w.reshape(H, P, D))
        k = jnp.einsum('bsd,hpd->bhsp', x, k_w.reshape(H, P, D))
        xv = jnp.einsum('bsd,hedp->bshep', x, v_w.reshape(H, E, D, P))
        v = jnp.einsum('bshep,bshe->bhsp', xv, gate_v)
        att = jax.nn.softmax(jnp.einsum('bhqp,bhkp->bhqk', q, k) * SCALE, axis=-1)
        ctx = jnp.einsum('bhqk,bhkp->bqhp', att, v)
        weighted = ctx[:, :, :, None, :] * gate_o[..., None]
        out = jnp.einsum('bshep,hepd->bsd', weighted, o_w.reshape(H, E, P, D))
        return out
    x = L0_attn_x
    x = _layernorm(x + _L0_attn_ref(x, L0_attn_Wq, L0_attn_bq, L0_attn_Wk, L0_attn_bk, L0_attn_Wv, L0_attn_bv, L0_attn_Wo, L0_attn_bo, L0_attn_gamma, L0_attn_beta), axis=-1)
    x = _layernorm(x + _L0_ffn_ref(x, L0_ffn_weight), axis=-1)
    x = _layernorm(x + _L1_attn_ref(x, L1_attn_Wq, L1_attn_Wkv, L1_attn_Wproj), axis=-1)
    x = _layernorm(x + _L1_ffn_ref(x, L1_ffn_q_w, L1_ffn_k_w, L1_ffn_v_w, L1_ffn_o_w, L1_ffn_sel_v_w, L1_ffn_sel_o_w, L1_ffn_route_scale), axis=-1)
    return x

_drawn_inputs = setup_inputs


def setup_inputs(seed=0):
    import zlib

    import numpy as np

    out = dict(_drawn_inputs(seed))
    spreads = {'L0_attn_bq': (0.0, 0.626),
     'L0_attn_bk': (0.0, 0.8),
     'L0_attn_bv': (0.0, 0.1),
     'L0_attn_bo': (0.0, 0.1),
     'L0_attn_gamma': (1.0, 0.2),
     'L0_attn_beta': (0.0, 0.1)}
    factors = {'L0_attn_Wq': 2.722, 'L1_attn_Wq': 8.0, 'L1_ffn_q_w': 2.734, 'L1_ffn_k_w': 2.828}
    for name, (base, spread) in spreads.items():
        noise = np.random.default_rng([zlib.crc32(name.encode()), seed]).standard_normal(out[name].shape)
        drawn = base * np.exp(spread * noise) if base else spread * noise
        out[name] = jnp.asarray(drawn.astype(out[name].dtype))
    for name, factor in factors.items():
        out[name] = (out[name] * factor).astype(out[name].dtype)
    return out
```

```python
import concourse.bass as bass
from concourse import mybir
from contextlib import ExitStack

F32 = mybir.dt.float32
BF16 = mybir.dt.bfloat16
F32R = mybir.dt.float32r
ALU = mybir.AluOpType
ACT = mybir.ActivationFunctionType
AX = mybir.AxisListType

P = 128
B = 8
T = 512
NT = T // P
D = 256
DK = D // P
H = 16
HD = D // H
HP = 32
HG = P // HP
NG = H // HG
KV = 4
QKV = D + 2 * KV * HD
FH = 8
E = 8
FP = 128
SEL = FH * E
BANK = 512
LN_EPS = 1e-5
QK_EPS = 1e-6
MASKED = -1e30
ATT_SCALE = HD ** -0.5
FFN_SCALE = FP ** -0.5
UNITS = H * NT
LAG = 3


def layer0_and_layer1_attention(nc, dram, kept):
    ctx = ExitStack()
    with ctx:
        def sb(name, shape, dt=F32):
            return ctx.enter_context(nc.sbuf_tensor(name, shape, dt))

        def sem(name):
            return ctx.enter_context(nc.semaphore(name))

        wq = sb("wq", [P, DK, NG * P])
        wk = sb("wk", [P, DK, NG * P])
        wv = sb("wv", [P, DK, D])
        wo = sb("wo", [P, DK, D])
        bq = sb("bq", [P, NG])
        bk = sb("bk", [P, NG])
        bv = sb("bv", [P, D])
        bo = sb("bo", [P, D])
        gamma = sb("gamma", [P, D])
        beta = sb("beta", [P, D])
        wt = sb("wt", [P, DK, D])
        tern = sb("tern", [P, DK, D])
        w1 = sb("w1", [P, DK, QKV])
        wp = sb("wp", [P, DK, D])
        wsel = sb("wsel", [P, DK, 2 * SEL])
        cos = sb("cos", [P, NT, HD])
        sin = sb("sin", [P, NT, HD])
        rank = sb("rank", [P, E])
        rscale = sb("rscale", [P, 1])
        ident = sb("ident", [P, P])
        identb = sb("identb", [P, P], BF16)
        cmask = sb("cmask", [P, P], BF16)
        band = sb("band", [P, BANK], BF16)
        diag = sb("diag", [P, BANK], BF16)
        ones = sb("ones", [P, P])
        tscale = sb("tscale", [P, 2])
        tsum = sb("tsum", [P, 2])
        mhalf = sb("mhalf", [P, NT * (H + KV)])
        phalf = sb("phalf", [P, NT * (H + KV)])
        eps = sb("eps", [P, NT])
        pad = sb("pad", [P, 1])
        x_in = sb("x_in", [P, NT, D])
        xbeta = sb("xbeta", [P, NT, D])
        tT = [sb(f"tT{i}", [P, DK, T]) for i in range(2)]
        qT = sb("qT", [P, NG, T])
        kT = sb("kT", [P, NG, T])
        vaug = sb("vaug", [P, NT, H, HP])
        probs = sb("probs", [P, 4, T])
        nmax = sb("nmax", [P, 8])
        pT = sb("pT", [P, HG, NT, T])
        oTs = sb("oTs", [P, NG, T])
        o = sb("o", [P, NT, D])
        rden = sb("rden", [P, NT, H])
        z = sb("z", [P, NT, D])
        x1 = sb("x1", [P, NT, D])
        x2 = sb("x2", [P, NT, D])
        stats = sb("stats", [P, NT, 6])
        mv = sb("mv", [P, NT, 2])
        ve = sb("ve", [P, NT])
        rstd = sb("rstd", [P, NT])
        qkv = sb("qkv", [P, NT, QKV])
        v1aug = sb("v1aug", [P, NT, KV, HP])
        kpad = sb("kpad", [P, NT, P])
        ss = sb("ss", [P, NT * (H + KV)])
        nrm = sb("nrm", [P, NT * (H + KV)])
        xhl = sb("xhl", [P, 2, DK, T], F32R)
        QK = NT * (H + KV)
        sq = pT[:, 0, :, 0:(H + KV) * HD]
        rot = pT[:, 1, :, 0:(H + KV) * HD]
        qn = pT[:, 2, :, 0:(H + KV) * HD]
        qpad = qT
        q1T = kT
        k1T = pT[:, 3, 0, :]
        p1T = [pT[:, i, k:k + 2, :].rearrange("p k q -> p (k q)") for i in (1, 2, 0) for k in (0, 2)][0:KV + 1]
        gw = [pT[:, 0, i, :] for i in range(NT)]
        m12 = sb("m12", [P, 4, NT * 2 * FH])

        ps = ctx.enter_context(nc.psum_tensor("psA", [P, 8, BANK], F32))

        loaded = sem("loaded")
        const_v = sem("const_v")
        const_g = sem("const_g")
        const_p = sem("const_p")
        x_loaded = sem("x_loaded")
        x_free = sem("x_free")
        tr_ps = sem("tr_ps")
        tr_sb = sem("tr_sb")
        q_ps = sem("q_ps")
        k_ps = sem("k_ps")
        absum_ps = sem("absum_ps")
        v_ps = sem("v_ps")
        q_ready = sem("q_ready")
        k_ready = sem("k_ready")
        v_ready = sem("v_ready")
        s_ps = sem("s_ps")
        max_ready = sem("max_ready")
        exp_ready = sem("exp_ready")
        t_ps = sem("t_ps")
        pt_a = sem("pt_a")
        pt_v = sem("pt_v")
        ot_ps = sem("ot_ps")
        ot_ready = sem("ot_ready")
        on_ps = sem("on_ps")
        o_ready = sem("o_ready")
        y_ps = sem("y_ps")
        y_read = sem("y_read")
        var_ready = sem("var_ready")
        rstd_ready = sem("rstd_ready")
        xb_ready = sem("xb_ready")
        x_ready = sem("x_ready")
        qkv_ps = sem("qkv_ps")
        qkv_ready = sem("qkv_ready")
        ss_ready = sem("ss_ready")
        nrm_ready = sem("nrm_ready")
        rope_ready = sem("rope_ready")
        v1_ready = sem("v1_ready")
        qk1_ps = sem("qk1_ps")
        qk1_a = sem("qk1_a")
        qk1_v = sem("qk1_v")
        s1_ps = sem("s1_ps")
        exp1_ready = sem("exp1_ready")
        av1_done = sem("av1_done")
        logit_ps = sem("logit_ps")
        logit_read = sem("logit_read")
        xhi_ready = sem("xhi_ready")
        xlo_ready = sem("xlo_ready")
        store_sem = sem("store_sem")
        stored = sem("stored")
        dve_step = sem("dve_step")
        pool_step = sem("pool_step")
        act_step = sem("act_step")
        DVE_STEPS = 45
        POOL_STEPS = 4

        block = ctx.enter_context(nc.Block())

        LOADS = [(wq[:], dram["wq"]), (wk[:], dram["wk"]), (wv[:], dram["wv"]), (wo[:], dram["wo"]),
                 (bq[:], dram["bq"]), (bk[:], dram["bk"]), (bv[:], dram["bv"].partition_broadcast(P)),
                 (bo[:], dram["bo"].partition_broadcast(P)), (gamma[:], dram["gamma"].partition_broadcast(P)),
                 (beta[:], dram["beta"].partition_broadcast(P)), (wt[:], dram["wt"]), (w1[:], dram["w1"]),
                 (wp[:], dram["wp"]), (wsel[:], dram["wsel"]), (cos[:], dram["cos"]), (sin[:], dram["sin"]),
                 (rank[:], dram["rank"].partition_broadcast(P)),
                 (rscale[:], dram["route_scale"].partition_broadcast(P)), (ident[:], dram["ident"])]

        @block.sync
        def _(sp):
            sp.dma_start(x_in[:], dram["x"][0].rearrange("(t p) d -> p t d", p=P)).then_inc(x_loaded, 16)
            for dst, src in LOADS:
                sp.dma_start(dst, src).then_inc(loaded, 16)
            sp.sem_inc(stored, 1)

            def store(b):
                sp.wait_ge(xhi_ready, b + 1)
                sp.wait_ge(xlo_ready, b + 1)
                sp.dma_start(dram["xs"][bass.ds(b, 1)].rearrange("o p n -> p (o n)"),
                             xhl[:].rearrange("p a k t -> p (a k t)").bitcast(F32)).then_inc(store_sem, 16)
                sp.wait_ge(store_sem, b * 16 + 16)
                sp.sem_inc(stored, 1)

            with sp.Fori(0, B - 1) as b:
                sp.wait_ge(x_free, b + 1)
                sp.dma_start(x_in[:], dram["x"][bass.ds(b + 1, 1)].rearrange("o (t p) d -> p (o t) d", p=P)).then_inc(x_loaded, 16)
                store(b)
            store(B - 1)

        def all_loaded(eng):
            eng.wait_ge(loaded, 16 * len(LOADS))

        @block.gpsimd
        def _(pool):
            g = nc.gpsimd
            g.memset(mhalf[:], -0.5).then_inc(const_p, 1)
            g.memset(phalf[:], 0.5).then_inc(const_p, 1)
            g.memset(eps[:], LN_EPS).then_inc(const_p, 1)
            g.memset(cmask[:], 0.0).then_inc(const_p, 1)
            g.memset(band[:], 0.0).then_inc(const_p, 1)
            g.memset(diag[:], 0.0).then_inc(const_p, 1)
            pool.wait_ge(const_p, 6)
            g.affine_select(out=cmask[:], in_=cmask[:], compare_op=ALU.is_ge, fill=MASKED, base=0,
                            pattern=[[-1, P]], channel_multiplier=1).then_inc(const_g, 1)
            g.affine_select(out=band[:].rearrange("p (j q) -> p j q", j=2), in_=band[:].rearrange("p (j q) -> p j q", j=2),
                            compare_op=ALU.is_ge, fill=MASKED, base=0,
                            pattern=[[0, 2], [1, 2 * P]], channel_multiplier=-1).then_inc(const_p, 1)
            pool.wait_ge(const_p, 7)
            g.affine_select(out=band[:].rearrange("p (j q) -> p j q", j=2), in_=band[:].rearrange("p (j q) -> p j q", j=2),
                            compare_op=ALU.is_ge, fill=MASKED, base=P - 1,
                            pattern=[[0, 2], [-1, 2 * P]], channel_multiplier=1).then_inc(const_g, 1)
            g.affine_select(out=diag[:].rearrange("p (j q) -> p j q", j=4), in_=diag[:].rearrange("p (j q) -> p j q", j=4),
                            compare_op=ALU.is_ge, fill=MASKED, base=0,
                            pattern=[[0, 4], [1, P]], channel_multiplier=-1).then_inc(const_g, 1)
            all_loaded(pool)
            with pool.Fori(0, B) as b:
                step = [0]

                def link(ins):
                    step[0] += 1
                    ins.then_inc(pool_step, 1)
                    pool.wait_ge(pool_step, b * POOL_STEPS + step[0])

                pool.wait_ge(x_loaded, b * 16 + 16)
                pool.wait_ge(tr_ps, b * 12 + 2)
                g.tensor_tensor(out=xbeta[:], in0=x_in[:], in1=beta[:].unsqueeze(1).to_broadcast([P, NT, D]),
                                op=ALU.add).then_inc(x_free, 1)

                def root(n):
                    pool.wait_ge(var_ready, b * 4 + n)
                    link(g.tensor_tensor(out=ve[:], in0=mv[:, :, 1], in1=eps[:], op=ALU.add))
                    g.tensor_tensor(out=rstd[:], in0=ve[:], in1=mhalf[:, 0:NT], op=ALU.pow).then_inc(rstd_ready, 1)

                root(1)
                root(2)
                root(3)
                pool.wait_ge(ss_ready, b + 1)
                g.tensor_tensor(out=nrm[:], in0=ss[:], in1=phalf[:], op=ALU.pow).then_inc(nrm_ready, 1)
                root(4)
                assert step[0] == POOL_STEPS

        @block.scalar
        def _(act):
            a = nc.scalar
            all_loaded(act)
            a.activation(identb[:], ident[:], ACT.Copy).then_inc(act_step, 1)
            with act.Fori(0, B) as b:
                def tt_evac(n):
                    act.wait_ge(tr_ps, b * 12 + 2 * n + 1)
                    a.activation(tT[n % 2][:, 0, :], ps[:, 0, :], ACT.Copy).then_inc(tr_sb, 1)

                tt_evac(0)
                for G in range(NG):
                    act.wait_ge(k_ps, b * NG + G + 1)
                    a.activation(kT[:, G, :], ps[:, (6 + G) % 8, :], ACT.Identity, bias=bk[:, G:G + 1]).then_inc(k_ready, 1)
                for u in range(UNITS + LAG):
                    if u < UNITS:
                        n = (u % NT + 1) * P
                        act.wait_ge(max_ready, b * UNITS + u + 1)
                        a.activation(probs[:, u % 4, 0:n], ps[:, 4 + u % 4, 0:n], ACT.Exp,
                                     bias=nmax[:, u % 8:u % 8 + 1]).then_inc(exp_ready, 1)
                    w = u - LAG
                    if w >= 0 and (w % NT) % 2 == 0:
                        h, qt = divmod(w, NT)
                        act.wait_ge(t_ps, b * UNITS + w + 1)
                        if h % HG == 0 and qt == 0 and h:
                            act.wait_ge(ot_ps, b * NG + h // HG)
                        a.activation(pT[:, h % HG, 0:qt + 1, qt * P:(qt + 1) * P],
                                     ps[:, w % 2, 0:(qt + 1) * P].rearrange("p (k q) -> p k q", q=P), ACT.Copy).then_inc(pt_a, 1)
                tt_evac(1)
                tt_evac(2)
                tt_evac(3)
                for t in range(NT):
                    act.wait_ge(qkv_ps, b * NT + t + 1)
                    a.activation(qkv[:, t, :], ps[:, 4 + t, 0:QKV], ACT.Copy).then_inc(qkv_ready, 1)
                act.wait_ge(qkv_ready, b * NT + NT)
                for t in range(NT):
                    a.activation(v1aug[:, t, :, 0:HD], qkv[:, t, D + KV * HD:QKV].rearrange("p (g d) -> p g d", g=KV),
                                 ACT.Copy).then_inc(v1_ready, 1)
                for j in range(2):
                    act.wait_ge(qk1_ps, b * 5 + j + 1)
                    a.activation(q1T[:, j, :], ps[:, j, :], ACT.Copy).then_inc(qk1_a, 1)
                act.wait_ge(qk1_ps, b * 5 + 5)
                a.activation(k1T, ps[:, 4, :], ACT.Copy).then_inc(qk1_a, 1)
                for w in range(KV * NT):
                    kt = w // KV
                    act.wait_ge(s1_ps, b * KV * NT + w + 1)
                    if w >= KV + 1:
                        act.wait_ge(av1_done, b * NT + (w - KV - 1) // KV + 1)
                    bank = 4 + 2 * (w % 2)
                    n = 1024 if kt < NT - 1 else BANK
                    src = ps[:, bank:bank + 2, :].rearrange("p a n -> p (a n)") if n == 1024 else ps[:, bank, :]
                    a.activation(p1T[w % (KV + 1)][:, 0:n], src, ACT.Exp, scale=ATT_SCALE).then_inc(exp1_ready, 1)
                tt_evac(4)
                tt_evac(5)
                act.wait_ge(tr_sb, b * 12 + 12)
                act.wait_ge(stored, b + 1)
                a.activation(xhl[:, 0], tT[1][:], ACT.Copy).then_inc(xhi_ready, 1)
                act.wait_ge(logit_ps, b + 1)
                a.activation(gw[0], ps[:, 6, :], ACT.Exp, scale=-1.0).then_inc(logit_read, 1)

        @block.vector
        def _(dve):
            v = nc.vector
            v.memset(vaug[:], 0.0).then_inc(const_v, 1)
            v.memset(v1aug[:], 0.0).then_inc(const_v, 1)
            v.memset(kpad[:], 0.0).then_inc(const_v, 1)
            v.memset(ones[:], 1.0).then_inc(const_v, 1)
            dve.wait_ge(const_v, 4)
            v.memset(vaug[:, :, :, HD:HD + 1], 1.0).then_inc(const_v, 1)
            v.memset(v1aug[:, :, :, HD:HD + 1], 1.0).then_inc(const_v, 1)
            all_loaded(dve)
            v.tensor_reduce(out=tsum[:, 0:1], in_=wt[:].rearrange("p k n -> p (k n)"), axis=AX.X, op=ALU.add,
                            apply_absolute_value=True).then_inc(const_v, 1)
            dve.wait_ge(absum_ps, 1)
            v.tensor_scalar(out=tscale[:, 1:2], in0=ps[:, 7, 0:1], scalar1=1.0 / (D * D), scalar2=LN_EPS,
                            op0=ALU.mult, op1=ALU.max).then_inc(const_v, 1)
            dve.wait_ge(const_v, 8)
            v.tensor_scalar(out=tscale[:, 0:1], in0=tscale[:, 1:2], scalar1=0.5, scalar2=None, op0=ALU.mult).then_inc(const_v, 1)
            v.tensor_scalar(out=tsum[:, 1:2], in0=tscale[:, 1:2], scalar1=-0.5, scalar2=None, op0=ALU.mult).then_inc(const_v, 1)
            dve.wait_ge(const_v, 10)
            v.tensor_scalar(out=tern[:], in0=wt[:], scalar1=tsum[:, 1:2], scalar2=None, op0=ALU.is_lt).then_inc(const_v, 1)
            dve.wait_ge(const_v, 11)
            v.scalar_tensor_tensor(out=tern[:], in0=wt[:], scalar=tscale[:, 0:1], in1=tern[:], op0=ALU.is_gt,
                                   op1=ALU.subtract).then_inc(const_v, 1)

            with dve.Fori(0, B) as b:
                step = [0]

                def link(ins):
                    step[0] += 1
                    ins.then_inc(dve_step, 1)
                    dve.wait_ge(dve_step, b * DVE_STEPS + step[0])

                def tt_evac(n):
                    dve.wait_ge(tr_ps, b * 12 + 2 * n + 2)
                    v.tensor_copy(tT[n % 2][:, 1, :], ps[:, 1, :]).then_inc(tr_sb, 1)

                def layer_norm(n, src, out, done):
                    for t in range(NT):
                        last = v.bn_stats(out=stats[:, t, :], in_=src[:, t, :])
                    link(last)
                    v.memset(pad[:], 0.0)
                    for t in range(NT):
                        last = v.bn_aggr(out=mv[:, t, :], in_=stats[:, t, :])
                    last.then_inc(var_ready, 1)
                    dve.wait_ge(rstd_ready, b * 4 + n)
                    for t in range(NT):
                        last = v.tensor_scalar(out=out[:, t, :], in0=src[:, t, :], scalar1=mv[:, t, 0:1], scalar2=rstd[:, t:t + 1],
                                               op0=ALU.subtract, op1=ALU.mult)
                    done(last)

                def token_ready(n):
                    def done(ins):
                        ins.then_inc(x_ready, 1)
                        dve.wait_ge(x_ready, b * 3 + n)
                    return done

                tt_evac(0)
                for G in range(NG):
                    dve.wait_ge(q_ps, b * NG + G + 1)
                    v.tensor_scalar(out=qT[:, G, :], in0=ps[:, 2 + G, :], scalar1=bq[:, G:G + 1], scalar2=ATT_SCALE,
                                    op0=ALU.add, op1=ALU.mult).then_inc(q_ready, 1)
                for i in range(2):
                    dve.wait_ge(v_ps, b * 2 + i + 1)
                    for t in range(2):
                        last = v.tensor_tensor(out=vaug[:, 2 * i + t, :, 0:HD],
                                        in0=ps[:, 2 + i, t * D:(t + 1) * D].rearrange("p (h d) -> p h d", h=H),
                                        in1=bv[:].rearrange("p (h d) -> p h d", h=H), op=ALU.add)
                    last.then_inc(v_ready, 1)
                for u in range(UNITS + LAG):
                    if u < UNITS:
                        n = (u % NT + 1) * P
                        dve.wait_ge(s_ps, b * UNITS + u + 1)
                        if u >= 8:
                            dve.wait_ge(exp_ready, b * UNITS + u - 7)
                        v.tensor_reduce(out=nmax[:, u % 8:u % 8 + 1], in_=ps[:, 4 + u % 4, 0:n], axis=AX.X, op=ALU.max,
                                        negate=True).then_inc(max_ready, 1)
                    w = u - LAG
                    if w >= 0 and (w % NT) % 2 == 1:
                        h, qt = divmod(w, NT)
                        dve.wait_ge(t_ps, b * UNITS + w + 1)
                        if h % HG == 0 and qt == 1 and h:
                            dve.wait_ge(ot_ps, b * NG + h // HG)
                        v.tensor_copy(pT[:, h % HG, 0:qt + 1, qt * P:(qt + 1) * P],
                                      ps[:, w % 2, 0:(qt + 1) * P].rearrange("p (k q) -> p k q", q=P)).then_inc(pt_v, 1)
                    if w >= 0 and w % (NT * HG) == 2 and w > 2:
                        G = w // (NT * HG) - 1
                        dve.wait_ge(ot_ps, b * NG + G + 1)
                        v.tensor_copy(oTs[:, G, :], ps[:, 2 + G % 2, :]).then_inc(ot_ready, 1)
                dve.wait_ge(ot_ps, b * NG + NG)
                v.tensor_copy(oTs[:, NG - 1, :], ps[:, 2 + (NG - 1) % 2, :]).then_inc(ot_ready, 1)

                def normalised(layer):
                    for t in range(NT):
                        dve.wait_ge(on_ps, b * 2 * NT + layer * NT + t + 1)
                        heads = ps[:, 4 + t, :].rearrange("p (c a d) -> p c a d", c=NG, a=HG)
                        link(v.reciprocal(out=rden[:, t, :].rearrange("p (c a) -> p c a", c=NG), in_=heads[:, :, :, HD]))
                        dst = o[:, t, :].rearrange("p (c a d) -> p c a d", c=NG, a=HG) if layer == 0 else \
                            o[:, t, :].rearrange("p (a c d) -> p c a d", c=NG, a=HG)
                        scale = rden[:, t, :].rearrange("p (c a) -> p c a", c=NG).unsqueeze(3).to_broadcast([P, NG, HG, HD])
                        v.tensor_tensor(out=dst, in0=heads[:, :, :, 0:HD], in1=scale, op=ALU.mult).then_inc(o_ready, 1)

                normalised(0)
                tt_evac(1)
                dve.wait_ge(y_ps, b * 3 * NT + NT)
                link(v.tensor_tensor(out=z[:], in0=ps[:, 2:4, :].rearrange("p a (t n) -> p (a t) n", t=2),
                                     in1=bo[:].unsqueeze(1).to_broadcast([P, NT, D]), op=ALU.add))
                layer_norm(1, z, z, link)
                link(v.tensor_tensor(out=z[:], in0=z[:], in1=gamma[:].unsqueeze(1).to_broadcast([P, NT, D]), op=ALU.mult))
                dve.wait_ge(x_free, b + 1)
                link(v.tensor_tensor(out=z[:], in0=z[:], in1=xbeta[:], op=ALU.add))
                layer_norm(2, z, x1, token_ready(1))
                tt_evac(2)
                dve.wait_ge(y_ps, b * 3 * NT + 2 * NT)
                link(v.scalar_tensor_tensor(out=z[:].rearrange("p t n -> p (t n)"), in0=ps[:, 2:4, :].rearrange("p a n -> p (a n)"),
                                            scalar=tscale[:, 1:2], in1=x1[:].rearrange("p t n -> p (t n)"),
                                            op0=ALU.mult, op1=ALU.add))
                layer_norm(3, z, x2, token_ready(2))
                tt_evac(3)
                dve.wait_ge(qkv_ready, b * NT + NT)
                qk = qkv[:, :, 0:D + KV * HD]
                link(v.tensor_tensor(out=sq, in0=qk, in1=qk, op=ALU.mult))
                v.tensor_reduce(out=ss[:].rearrange("p (t h) -> p t h", t=NT), in_=sq.rearrange("p t (h d) -> p t h d", d=HD),
                                axis=AX.X, op=ALU.add).then_inc(ss_ready, 1)
                dve.wait_ge(nrm_ready, b + 1)
                link(v.tensor_scalar(out=nrm[:], in0=nrm[:], scalar1=QK_EPS, scalar2=None, op0=ALU.add))
                link(v.reciprocal(out=ss[:], in_=nrm[:]))
                heads = H + KV
                for t in range(NT):
                    last = v.tensor_tensor(out=qn[:, t, :].rearrange("p (h d) -> p h d", d=HD),
                                           in0=qkv[:, t, 0:D + KV * HD].rearrange("p (h d) -> p h d", d=HD),
                                           in1=ss[:, t * heads:(t + 1) * heads].unsqueeze(2).to_broadcast([P, heads, HD]),
                                           op=ALU.mult)
                link(last)
                half = HD // 2
                qnh = qn.rearrange("p t (h d) -> p t h d", d=HD)
                roth = rot.rearrange("p t (h d) -> p t h d", d=HD)
                for t in range(NT):
                    v.tensor_tensor(out=roth[:, t, :, 0:half], in0=qnh[:, t, :, half:HD],
                                    in1=sin[:, t, 0:half].unsqueeze(1).to_broadcast([P, heads, half]), op=ALU.mult)
                    last = v.tensor_tensor(out=roth[:, t, :, half:HD], in0=qnh[:, t, :, 0:half],
                                           in1=sin[:, t, half:HD].unsqueeze(1).to_broadcast([P, heads, half]), op=ALU.mult)
                link(last)
                for t in range(NT):
                    last = v.tensor_tensor(out=qnh[:, t], in0=qnh[:, t],
                                           in1=cos[:, t, :].unsqueeze(1).to_broadcast([P, heads, HD]), op=ALU.mult)
                link(last)
                for t in range(NT):
                    v.tensor_tensor(out=qpad[:, t, :].rearrange("p (j g d) -> p j g d", j=HG, g=KV)[:, :, :, 0:HD],
                                    in0=qn[:, t, 0:D].rearrange("p (g j d) -> p j g d", g=KV, j=HG),
                                    in1=rot[:, t, 0:D].rearrange("p (g j d) -> p j g d", g=KV, j=HG), op=ALU.add)
                    last = v.tensor_tensor(out=kpad[:, t, :].rearrange("p (g d) -> p g d", g=KV)[:, :, 0:HD],
                                           in0=qn[:, t, D:D + KV * HD].rearrange("p (g d) -> p g d", g=KV),
                                           in1=rot[:, t, D:D + KV * HD].rearrange("p (g d) -> p g d", g=KV), op=ALU.add)
                last.then_inc(rope_ready, 1)
                for j in range(2, 4):
                    dve.wait_ge(qk1_ps, b * 5 + j + 1)
                    v.tensor_copy(q1T[:, j, :], ps[:, j, :]).then_inc(qk1_v, 1)
                for c in range(NG):
                    dve.wait_ge(av1_done, b * NT + NT)
                    v.tensor_copy(oTs[:, c, :], ps[:, c, :]).then_inc(ot_ready, 1)
                normalised(1)
                tt_evac(4)
                dve.wait_ge(y_ps, b * 3 * NT + 3 * NT)
                link(v.tensor_tensor(out=z[:], in0=ps[:, 2:4, :].rearrange("p a (t n) -> p (a t) n", t=2), in1=x2[:], op=ALU.add))
                layer_norm(4, z, x1, token_ready(3))
                tt_evac(5)
                link(v.tensor_copy(kept["acc"][:, bass.ds(b, 1)].rearrange("p o t d -> p (o t) d"), x1[:]))
                dve.wait_ge(xhi_ready, b + 1)
                v.tensor_tensor(out=xhl[:, 1], in0=tT[1][:], in1=xhl[:, 0].bitcast(F32), op=ALU.subtract).then_inc(xlo_ready, 1)
                dve.wait_ge(logit_read, b + 2)
                NGR = NT * 2 * FH
                g3 = [x.rearrange("p (c e) -> p c e", e=E) for x in gw]
                wide = [P, NGR, E]
                ranks = rank[:].unsqueeze(1).to_broadcast(wide)
                link(v.tensor_scalar(out=gw[1], in0=gw[0], scalar1=1.0, scalar2=None, op0=ALU.add))
                link(v.reciprocal(out=gw[0], in_=gw[1]))

                def first_largest(src, top, hot, tmp):
                    link(v.tensor_reduce(out=m12[:, top, :], in_=g3[src], axis=AX.X, op=ALU.max))
                    link(v.tensor_tensor(out=g3[tmp], in0=g3[src], in1=m12[:, top, :].unsqueeze(2).to_broadcast(wide), op=ALU.is_equal))
                    link(v.tensor_tensor(out=g3[tmp], in0=g3[tmp], in1=ranks, op=ALU.mult))
                    link(v.tensor_reduce(out=m12[:, 3, :], in_=g3[tmp], axis=AX.X, op=ALU.max))
                    link(v.tensor_tensor(out=g3[hot], in0=g3[tmp], in1=m12[:, 3, :].unsqueeze(2).to_broadcast(wide), op=ALU.is_equal))

                first_largest(0, 0, 1, 2)
                link(v.scalar_tensor_tensor(out=gw[2], in0=gw[1], scalar=-2.0, in1=gw[0], op0=ALU.mult, op1=ALU.add))
                first_largest(2, 1, 3, 3)
                link(v.tensor_tensor(out=gw[1], in0=gw[1], in1=gw[3], op=ALU.add))
                link(v.tensor_tensor(out=gw[0], in0=gw[0], in1=gw[1], op=ALU.mult))
                link(v.tensor_tensor(out=m12[:, 2, :], in0=m12[:, 0, :], in1=m12[:, 1, :], op=ALU.add))
                link(v.tensor_scalar(out=m12[:, 2, :], in0=m12[:, 2, :], scalar1=1e-9, scalar2=None, op0=ALU.max))
                link(v.reciprocal(out=m12[:, 3, :], in_=m12[:, 2, :]))
                link(v.tensor_scalar(out=m12[:, 3, :], in0=m12[:, 3, :], scalar1=rscale[:, 0:1], scalar2=None, op0=ALU.mult))
                for t in range(NT):
                    n = 2 * FH
                    last = v.tensor_tensor(out=kept["gates"][:, bass.ds(b, 1), :, :, t, :].rearrange("p o h c e -> p c (o h) e"),
                                           in0=g3[0][:, t * n:(t + 1) * n, :].rearrange("p (c h) e -> p c h e", c=2),
                                           in1=m12[:, 3, t * n:(t + 1) * n].rearrange("p (c h) -> p c h", c=2).unsqueeze(3).to_broadcast([P, 2, FH, E]),
                                           op=ALU.mult)
                link(last)
                assert step[0] == DVE_STEPS, step[0]

        @block.tensor
        def _(pe):
            mm = nc.tensor.matmul
            all_loaded(pe)
            pe.wait_ge(const_v, 7)
            mm(ps[:, 7, 0:1], ones[:], tsum[:, 0:1], start=True, stop=True).then_inc(absum_ps, 1)
            pe.wait_ge(const_v, 12)
            pe.wait_ge(const_g, 3)
            pe.wait_ge(act_step, 1)
            pe.sem_inc(logit_read, 1)
            with pe.Fori(0, B) as b:
                def transposition(n, src, per_tile=None):
                    for k in range(DK):
                        for t in range(NT):
                            if per_tile:
                                per_tile(t)
                            last = nc.tensor.transpose(ps[:, k, t * P:(t + 1) * P], src[:, t, k * P:(k + 1) * P], ident[:])
                        last.then_inc(tr_ps, 1)

                def project(n, out, rhs, width, t, done=None):
                    for k in range(DK):
                        last = mm(out, tT[n % 2][:, k, t * P:(t + 1) * P], rhs[:, k, 0:width], start=(k == 0), stop=(k == DK - 1))
                    if done is not None:
                        last.then_inc(done, 1)

                pe.wait_ge(x_loaded, b * 16 + 16)
                transposition(0, x_in)
                pe.wait_ge(tr_sb, b * 12 + 2)
                pe.wait_ge(logit_read, b + 1)
                for w, first, done in ((wq, 2, q_ps), (wk, 6, k_ps)):
                    for G in range(NG):
                        for k in range(DK):
                            last = mm(ps[:, (first + G) % 8, :], w[:, k, G * P:(G + 1) * P], tT[0][:, k, :],
                                      start=(k == 0), stop=(k == DK - 1))
                        last.then_inc(done, 1)
                for i in range(2):
                    pe.wait_ge(q_ready, b * NG + i + 1)
                    for t in range(2):
                        project(0, ps[:, 2 + i, t * D:(t + 1) * D], wv, D, 2 * i + t, v_ps if t else None)
                pe.wait_ge(q_ready, b * NG + NG)
                pe.wait_ge(k_ready, b * NG + NG)
                pe.wait_ge(v_ready, b * 2 + 2)

                def weighted(G):
                    pe.wait_ge(pt_a, b * 2 * H + 2 * HG * (G + 1))
                    pe.wait_ge(pt_v, b * 2 * H + 2 * HG * (G + 1))
                    if G >= 2:
                        pe.wait_ge(ot_ready, b * 2 * NG + G - 1)
                    for kt in range(NT):
                        for j in range(HG):
                            last = mm(ps[j * HP:(j + 1) * HP, 2 + G % 2, kt * P:T], vaug[:, kt, G * HG + j, :],
                                      pT[:, j, kt, kt * P:T], start=(kt == 0), stop=(kt == NT - 1), skip_group_check=True)
                    last.then_inc(ot_ps, 1)

                for u in range(UNITS + LAG):
                    if u < UNITS:
                        h, qt = divmod(u, NT)
                        G, j = divmod(h, HG)
                        if u >= 4:
                            pe.wait_ge(exp_ready, b * UNITS + u - 3)
                        rows = slice(j * HP, j * HP + HD)
                        bank = ps[:, 4 + u % 4, :]
                        mm(bank[:, 0:(qt + 1) * P], qT[rows, G, qt * P:(qt + 1) * P], kT[rows, G, 0:(qt + 1) * P],
                           start=True, stop=False)
                        mm(bank[:, qt * P:(qt + 1) * P], identb[:], cmask[:], start=False, stop=True).then_inc(s_ps, 1)
                    w = u - LAG
                    if w >= 0:
                        qt = w % NT
                        pe.wait_ge(exp_ready, b * UNITS + w + 1)
                        if w >= 2:
                            pe.wait_ge(pt_v if qt % 2 else pt_a, b * 2 * H + (w - 2) // NT * 2 + (w - 2) % NT // 2 + 1)
                        for k in range(qt + 1):
                            last = nc.tensor.transpose(ps[:, w % 2, k * P:(k + 1) * P], probs[:, w % 4, k * P:(k + 1) * P], ident[:])
                        last.then_inc(t_ps, 1)
                        if w % (NT * HG) == NT * HG - 1:
                            weighted(w // (NT * HG))

                def back(layer):
                    pe.wait_ge(ot_ready, b * 2 * NG + layer * NG + NG)
                    for t in range(NT):
                        for c in range(NG):
                            last = nc.tensor.transpose(ps[:, 4 + t, c * P:(c + 1) * P], oTs[:, c, t * P:(t + 1) * P], ident[:])
                        last.then_inc(on_ps, 1)

                def to_width(n, rhs):
                    pe.wait_ge(tr_sb, b * 12 + 2 * n + 2)
                    for t in range(NT):
                        project(n, ps[:, 2 + t // 2, (t % 2) * D:(t % 2 + 1) * D], rhs, D, t, y_ps)

                back(0)
                transposition(1, o, lambda t: pe.wait_ge(o_ready, b * 2 * NT + t + 1))
                to_width(1, wo)
                pe.wait_ge(x_ready, b * 3 + 1)
                transposition(2, x1)
                to_width(2, tern)
                pe.wait_ge(x_ready, b * 3 + 2)
                transposition(3, x2)
                pe.wait_ge(tr_sb, b * 12 + 8)
                for t in range(NT):
                    project(3, ps[:, 4 + t, 0:QKV], w1, QKV, t, qkv_ps)
                pe.wait_ge(rope_ready, b + 1)
                pe.wait_ge(tr_sb, b * 12 + 8)
                pe.wait_ge(qkv_ready, b * NT + NT)
                for j in range(HG):
                    for t in range(NT):
                        last = nc.tensor.transpose(ps[:, j, t * P:(t + 1) * P], qpad[:, t, j * P:(j + 1) * P], ident[:])
                    last.then_inc(qk1_ps, 1)
                for t in range(NT):
                    last = nc.tensor.transpose(ps[:, 4, t * P:(t + 1) * P], kpad[:, t, :], ident[:])
                last.then_inc(qk1_ps, 1)
                pe.wait_ge(qk1_a, b * 3 + 3)
                pe.wait_ge(qk1_v, b * 2 + 2)
                pe.wait_ge(v1_ready, b * NT + NT)

                def weighted1(kt):
                    pe.wait_ge(exp1_ready, b * KV * NT + (kt + 1) * KV)
                    nq = 2 * P if kt < NT - 1 else P
                    for j in range(HG):
                        for g in range(KV):
                            last = mm(ps[g * HP:(g + 1) * HP, j, kt * P:kt * P + nq], v1aug[:, kt, g, :],
                                      p1T[(kt * KV + g) % (KV + 1)][:, j * nq:(j + 1) * nq],
                                      start=(kt == 0), stop=(kt == NT - 1), skip_group_check=True)
                    last.then_inc(av1_done, 1)

                for w in range(KV * NT + 1):
                    if w < KV * NT:
                        kt, g = divmod(w, KV)
                        if w >= 2:
                            pe.wait_ge(exp1_ready, b * KV * NT + w - 1)
                        rows = slice(g * HP, g * HP + HD)
                        bank = 4 + 2 * (w % 2)
                        keys = k1T[rows, kt * P:(kt + 1) * P]
                        if kt < NT - 1:
                            for i in range(2):
                                mm(ps[:, bank + i, :], keys, q1T[rows, 2 * i:2 * i + 2, kt * P:(kt + 2) * P], start=True, stop=False)
                                last = mm(ps[:, bank + i, :], identb[:], band[:], start=False, stop=True)
                        else:
                            mm(ps[:, bank, :], keys, q1T[rows, :, kt * P:T], start=True, stop=False)
                            last = mm(ps[:, bank, :], identb[:], diag[:], start=False, stop=True)
                        last.then_inc(s1_ps, 1)
                    if w and w % KV == 0:
                        weighted1(w // KV - 1)

                back(1)
                transposition(4, o, lambda t: pe.wait_ge(o_ready, b * 2 * NT + NT + t + 1))
                to_width(4, wp)
                pe.wait_ge(x_ready, b * 3 + 3)
                transposition(5, x1)
                pe.wait_ge(tr_sb, b * 12 + 12)
                for t in range(NT):
                    project(5, ps[:, 6, t * P:(t + 1) * P], wsel, 2 * SEL, t, logit_ps if t == NT - 1 else None)


def layouts(inputs):
    import numpy as np

    def rows(w):
        return np.ascontiguousarray(w.reshape(-1, P, w.shape[1]).transpose(1, 0, 2))

    def padded(w):
        out = np.zeros((w.shape[0], H, HP), w.dtype)
        out[:, :, 0:HD] = w.reshape(-1, H, HD)
        return out.reshape(-1, H * HP)

    i = {k: np.asarray(v) for k, v in inputs.items()}
    f = np.float32
    theta = 1.0 / 10000.0 ** (np.arange(0, HD, 2, dtype=f) / HD)
    freqs = np.outer(np.arange(T, dtype=f), theta).astype(f)
    cos = np.concatenate([np.cos(freqs)] * 2, 1).astype(f)
    sin = np.concatenate([-np.sin(freqs), np.sin(freqs)], 1).astype(f)
    table = lambda x: np.ascontiguousarray(x.reshape(NT, P, HD).transpose(1, 0, 2))
    return {
        "x": i["L0_attn_x"],
        "wq": rows(padded(i["L0_attn_Wq"])), "wk": rows(padded(i["L0_attn_Wk"])),
        "wv": rows(i["L0_attn_Wv"]), "wo": rows(i["L0_attn_Wo"]),
        "bq": np.ascontiguousarray(padded(i["L0_attn_bq"][None]).reshape(NG, P).T),
        "bk": np.ascontiguousarray(padded(i["L0_attn_bk"][None]).reshape(NG, P).T),
        "bv": i["L0_attn_bv"], "bo": i["L0_attn_bo"],
        "gamma": i["L0_attn_gamma"], "beta": i["L0_attn_beta"],
        "wt": rows(i["L0_ffn_weight"].T),
        "w1": rows(np.concatenate([i["L1_attn_Wq"].T, i["L1_attn_Wkv"].T], 1)),
        "wp": rows(i["L1_attn_Wproj"].T),
        "wsel": rows(np.concatenate([i["L1_ffn_sel_v_w"].T, i["L1_ffn_sel_o_w"].T], 1)),
        "cos": table(cos), "sin": table(sin),
        "rank": np.arange(E, 0, -1).astype(f),
        "route_scale": i["L1_ffn_route_scale"],
        "ident": np.eye(P, dtype=f),
        "wf": np.concatenate([
            i["L1_ffn_q_w"].reshape(FH, FP, DK, P).transpose(0, 3, 2, 1).reshape(FH, P, -1),
            i["L1_ffn_k_w"].reshape(FH, FP, DK, P).transpose(0, 3, 2, 1).reshape(FH, P, -1),
            i["L1_ffn_v_w"].reshape(FH, E, DK, P, FP).transpose(0, 3, 2, 1, 4).reshape(FH, P, -1),
            i["L1_ffn_o_w"].reshape(FH, E, FP, D).transpose(0, 2, 1, 3).reshape(FH, P, -1)], 2),
    }


def routed_heads(nc, dram, kept):
    ctx = ExitStack()
    with ctx:
        def sb(name, shape, dt=F32):
            return ctx.enter_context(nc.sbuf_tensor(name, shape, dt))

        def sem(name):
            return ctx.enter_context(nc.semaphore(name))

        acc, gates = kept["acc"], kept["gates"]
        QW, VW = DK * FP, DK * E * FP
        WCOLS = 2 * QW + VW + E * D
        SLICE = WCOLS // B
        stage = sb("stage", [P, WCOLS])
        whl = [sb(f"whl{i}", [P, 2, WCOLS], F32R) for i in range(2)]
        xhl = sb("xhlB", [P, 2, DK, T], F32R)
        gs = sb("gs", [P, 2, NT, E])
        go = sb("go", [P, NT, E])
        qhl = sb("qhl", [P, 2, T], F32R)
        khl = sb("khl", [P, 2, T], F32R)
        vacc = sb("vacc", [P, NT, FP])
        vhl = sb("vhl", [P, 2, NT, FP], F32R)
        probs = sb("probsB", [P, 2, T])
        nmax = sb("nmaxB", [P, NT])
        rowsum = sb("rowsum", [P, NT])
        rinv = sb("rinv", [P, NT])
        pT = sb("pTB", [P, 2, NT, T], F32R)
        cT = sb("cT", [P, 2, T], F32R)
        part = sb("part", [P, NT, D])
        ident = sb("identB", [P, P])
        ps = ctx.enter_context(nc.psum_tensor("psB", [P, 8, BANK], F32))
        PROJ, TR, CTX, RING = 0, 2, 4, 5
        CHUNKS = NT * 2 + NT * E // 2
        NRING = 3

        ident_loaded = sem("ident_loadedB")
        w_loaded = sem("w_loaded")
        w_hi0 = sem("w_hi0")
        w_split = sem("w_split")
        w_hi = sem("w_hi")
        x_loaded = sem("x_loadedB")
        gates_ready = sem("gates_ready")
        proj_ps = sem("proj_ps")
        qk_hi = sem("qk_hi")
        qk_lo = sem("qk_lo")
        chunk_ps = sem("chunk_ps")
        chunk_used = sem("chunk_used")
        v_hi = sem("v_hi")
        v_lo = sem("v_lo")
        s_ps = sem("s_psB")
        max_ready = sem("max_readyB")
        exp_ready = sem("exp_readyB")
        t_ps = sem("t_psB")
        pt_hi = sem("pt_hi")
        pt_lo = sem("pt_lo")
        ctx_ps = sem("ctx_ps")
        ctx_hi = sem("ctx_hi")
        ctx_lo = sem("ctx_lo")
        added = sem("added")
        dve_step = sem("dve_stepB")
        DVE_STEPS = NT * (E - 2) + 2 + NT * (E - 4)

        block = ctx.enter_context(nc.Block())
        TERMS = ((0, 0), (0, 1), (1, 0))

        @block.sync
        def _(sp):
            sp.dma_start(stage[:], dram["wf"][0]).then_inc(w_loaded, 16)
            sp.dma_start(ident[:], dram["ident"]).then_inc(ident_loaded, 16)
            sp.dma_start(xhl[:].rearrange("p a k t -> p (a k t)").bitcast(F32), dram["xs"][0]).then_inc(x_loaded, 16)
            with sp.Fori(0, FH) as h:
                sp.wait_ge(w_split, h * B + 1)
                sp.dma_start(stage[:], dram["wf"][bass.ds((h + 1) % FH, 1)].rearrange("o p n -> p (o n)")).then_inc(w_loaded, 16)
                with sp.Fori(0, B) as b:
                    sp.wait_ge(chunk_ps, h * (B * CHUNKS) + b * CHUNKS + 2 * NT)
                    sp.dma_start(xhl[:].rearrange("p a k t -> p (a k t)").bitcast(F32),
                                 dram["xs"][bass.ds((b + 1) % B, 1)].rearrange("o p n -> p (o n)")).then_inc(x_loaded, 16)
            sp.wait_ge(x_loaded, 16 * (FH * B + 1))
            sp.wait_ge(w_loaded, 16 * (FH + 1))

        def heads(eng, body):
            with eng.Fori(0, FH // 2) as hh:
                for parity in range(2):
                    h = hh * 2 + parity
                    with eng.Fori(0, B) as b:
                        body(parity, h, b, hh * (2 * B) + b + parity * B)

        @block.gpsimd
        def _(pool):
            g = nc.gpsimd
            pool.sem_inc(added, NT)

            def iteration(parity, h, b, i):
                g.tensor_copy(gs[:].rearrange("p c t e -> p (c t e)"),
                              gates[:, bass.ds(b, 1), bass.ds(h, 1)].rearrange("p o a c t e -> p (o a c t e)")).then_inc(gates_ready, 1)
                pool.wait_ge(w_loaded, h * 16 + 32)
                part_in = stage[:, bass.ds(b * SLICE, SLICE)]
                hi = whl[1 - parity][:, 0, bass.ds(b * SLICE, SLICE)]
                g.tensor_copy(hi, part_in).then_inc(w_hi, 1)
                pool.wait_ge(w_hi, i + 1)
                g.tensor_tensor(out=whl[1 - parity][:, 1, bass.ds(b * SLICE, SLICE)], in0=part_in, in1=hi.bitcast(F32),
                                op=ALU.subtract).then_inc(w_split, 1)
                for t in range(NT):
                    pool.wait_ge(chunk_used, i * CHUNKS + NRING + 2 * NT + (t + 1) * E // 2)
                    dst = acc[:, bass.ds(b, 1), t, :].rearrange("p o n -> p (o n)")
                    g.tensor_tensor(out=dst, in0=dst, in1=part[:, t, :], op=ALU.add).then_inc(added, 1)

            heads(pool, iteration)

        @block.scalar
        def _(act):
            a = nc.scalar
            act.wait_ge(w_loaded, 16)
            a.activation(whl[0][:, 0, :], stage[:], ACT.Copy).then_inc(w_hi0, 1)

            def iteration(parity, h, b, i):
                for n, (dst, scale) in enumerate(((qhl, FFN_SCALE), (khl, 1.0))):
                    act.wait_ge(proj_ps, i * 2 + n + 1)
                    a.activation(dst[:, 0, :], ps[:, PROJ + n, :], ACT.Copy, scale=scale).then_inc(qk_hi, 1)

                def value_hi(t):
                    act.wait_ge(chunk_used, i * CHUNKS + NRING + 2 * t + 2)
                    a.activation(vhl[:, 0, t, :], vacc[:, t, :], ACT.Copy).then_inc(v_hi, 1)

                def exp(qt):
                    act.wait_ge(max_ready, i * NT + qt + 1)
                    a.activation(probs[:, qt % 2, :], ps[:, PROJ + qt % 2, :], ACT.Exp, bias=nmax[:, qt:qt + 1],
                                 accum_out=rowsum[:, qt:qt + 1]).then_inc(exp_ready, 1)

                def probs_hi(qt):
                    act.wait_ge(t_ps, i * NT + qt + 1)
                    a.activation(pT[:, 0, :, qt * P:(qt + 1) * P], ps[:, TR + qt % 2, :].rearrange("p (k q) -> p k q", q=P),
                                 ACT.Copy).then_inc(pt_hi, 1)

                exp(0)
                exp(1)
                value_hi(0)
                probs_hi(0)
                exp(2)
                probs_hi(1)
                exp(3)
                value_hi(1)
                probs_hi(2)
                probs_hi(3)
                value_hi(2)
                value_hi(3)
                act.wait_ge(ctx_ps, i + 1)
                a.activation(cT[:, 0, :], ps[:, CTX, :], ACT.Copy).then_inc(ctx_hi, 1)

            heads(act, iteration)

        @block.vector
        def _(dve):
            v = nc.vector
            dve.wait_ge(w_hi0, 1)
            v.tensor_tensor(out=whl[0][:, 1, :], in0=stage[:], in1=whl[0][:, 0, :].bitcast(F32), op=ALU.subtract).then_inc(w_split, 1)

            def iteration(parity, h, b, i):
                step = [0]

                def link(ins):
                    step[0] += 1
                    ins.then_inc(dve_step, 1)
                    dve.wait_ge(dve_step, i * DVE_STEPS + step[0])

                def gated(out, gate, first_chunk, experts, width):
                    for c in range(E // experts):
                        n = first_chunk + c
                        dve.wait_ge(chunk_ps, i * CHUNKS + n + 1)
                        for e in range(experts):
                            src = ps[:, RING + n % NRING, e * width:(e + 1) * width]
                            scale = gate[:, c * experts + e:c * experts + e + 1]
                            if c == 0 and e == 0:
                                ins = v.tensor_scalar(out=out, in0=src, scalar1=scale, scalar2=None, op0=ALU.mult)
                            else:
                                ins = v.scalar_tensor_tensor(out=out, in0=src, scalar=scale, in1=out, op0=ALU.mult, op1=ALU.add)
                            if e < experts - 1:
                                link(ins)
                        ins.then_inc(chunk_used, 1)
                        dve.wait_ge(chunk_used, i * CHUNKS + NRING + n + 1)

                def values(t):
                    gated(vacc[:, t, :], gs[:, 0, t, :], 2 * t, E // 2, FP)

                def value_lo(t):
                    dve.wait_ge(v_hi, i * NT + t + 1)
                    v.tensor_tensor(out=vhl[:, 1, t, :], in0=vacc[:, t, :], in1=vhl[:, 0, t, :].bitcast(F32), op=ALU.subtract).then_inc(v_lo, 1)

                def row_max(qt):
                    dve.wait_ge(s_ps, i * NT + qt + 1)
                    v.tensor_reduce(out=nmax[:, qt:qt + 1], in_=ps[:, PROJ + qt % 2, :], axis=AX.X, op=ALU.max,
                                    negate=True).then_inc(max_ready, 1)

                def probs_lo(qt):
                    dve.wait_ge(pt_hi, i * NT + qt + 1)
                    cols = slice(qt * P, (qt + 1) * P)
                    v.tensor_tensor(out=pT[:, 1, :, cols], in0=ps[:, TR + qt % 2, :].rearrange("p (k q) -> p k q", q=P),
                                    in1=pT[:, 0, :, cols].bitcast(F32), op=ALU.subtract).then_inc(pt_lo, 1)

                dve.wait_ge(qk_hi, i * 2 + 1)
                v.scalar_tensor_tensor(out=qhl[:, 1, :], in0=ps[:, PROJ, :], scalar=FFN_SCALE, in1=qhl[:, 0, :].bitcast(F32),
                                       op0=ALU.mult, op1=ALU.subtract).then_inc(qk_lo, 1)
                dve.wait_ge(qk_hi, i * 2 + 2)
                v.tensor_tensor(out=khl[:, 1, :], in0=ps[:, PROJ + 1, :], in1=khl[:, 0, :].bitcast(F32), op=ALU.subtract).then_inc(qk_lo, 1)
                dve.wait_ge(gates_ready, i + 1)
                values(0)
                row_max(0)
                row_max(1)
                value_lo(0)
                values(1)
                probs_lo(0)
                row_max(2)
                probs_lo(1)
                row_max(3)
                value_lo(1)
                values(2)
                probs_lo(2)
                probs_lo(3)
                value_lo(2)
                values(3)
                value_lo(3)
                dve.wait_ge(exp_ready, i * NT + NT)
                link(v.reciprocal(out=rinv[:], in_=rowsum[:]))
                link(v.tensor_tensor(out=go[:], in0=gs[:, 1], in1=rinv[:].unsqueeze(2).to_broadcast([P, NT, E]), op=ALU.mult))
                dve.wait_ge(ctx_hi, i + 1)
                v.tensor_tensor(out=cT[:, 1, :], in0=ps[:, CTX, :], in1=cT[:, 0, :].bitcast(F32), op=ALU.subtract).then_inc(ctx_lo, 1)
                for t in range(NT):
                    dve.wait_ge(added, i * NT + t + 1)
                    gated(part[:, t, :], go[:, t, :], 2 * NT + t * E // 2, 2, D)
                assert step[0] == DVE_STEPS, step[0]

            heads(dve, iteration)

        @block.tensor
        def _(pe):
            mm = nc.tensor.matmul
            pe.sem_inc(chunk_used, NRING)
            pe.wait_ge(ident_loaded, 16)

            def split_product(out, pairs):
                n = len(pairs) * len(TERMS)
                k = 0
                for stationary, moving in pairs:
                    for s, m in TERMS:
                        last = mm(out, stationary(s), moving(m), start=(k == 0), stop=(k == n - 1))
                        k += 1
                return last

            def iteration(parity, h, b, i):
                w = whl[parity]

                def weight(s, first, width):
                    return w[:, s, first:first + width]

                pe.wait_ge(w_split, h * B + 1)
                pe.wait_ge(x_loaded, i * 16 + 16)
                for n in range(2):
                    split_product(ps[:, PROJ + n, :],
                                  [(lambda s, k=k: weight(s, n * QW + k * FP, FP), lambda m, k=k: xhl[:, m, k, :])
                                   for k in range(DK)]).then_inc(proj_ps, 1)

                def values(t):
                    for half in range(2):
                        c = 2 * t + half
                        pe.wait_ge(chunk_used, i * CHUNKS + c + 1)
                        split_product(ps[:, RING + c % NRING, :],
                                      [(lambda s, k=k: xhl[:, s, k, t * P:(t + 1) * P],
                                        lambda m, k=k: weight(m, 2 * QW + k * E * FP + half * BANK, BANK))
                                       for k in range(DK)]).then_inc(chunk_ps, 1)

                def scores(qt):
                    if qt >= 2:
                        pe.wait_ge(exp_ready, i * NT + qt - 1)
                    split_product(ps[:, PROJ + qt % 2, :],
                                  [(lambda s: qhl[:, s, qt * P:(qt + 1) * P], lambda m: khl[:, m, :])]).then_inc(s_ps, 1)

                def transposes(qt):
                    pe.wait_ge(exp_ready, i * NT + qt + 1)
                    if qt >= 2:
                        pe.wait_ge(pt_lo, i * NT + qt - 1)
                    for k in range(NT):
                        last = nc.tensor.transpose(ps[:, TR + qt % 2, k * P:(k + 1) * P], probs[:, qt % 2, k * P:(k + 1) * P], ident[:])
                    last.then_inc(t_ps, 1)

                values(0)
                pe.wait_ge(qk_lo, i * 2 + 2)
                scores(0)
                scores(1)
                values(1)
                transposes(0)
                scores(2)
                transposes(1)
                scores(3)
                values(2)
                transposes(2)
                transposes(3)
                values(3)
                pe.wait_ge(pt_lo, i * NT + NT)
                pe.wait_ge(v_lo, i * NT + NT)
                split_product(ps[:, CTX, :],
                              [(lambda s, k=k: vhl[:, s, k, :], lambda m, k=k: pT[:, m, k, :]) for k in range(NT)]).then_inc(ctx_ps, 1)
                pe.wait_ge(ctx_lo, i + 1)
                for t in range(NT):
                    for pair in range(E // 2):
                        c = 2 * NT + t * E // 2 + pair
                        pe.wait_ge(chunk_used, i * CHUNKS + c + 1)
                        split_product(ps[:, RING + c % NRING, :],
                                      [(lambda s: cT[:, s, t * P:(t + 1) * P],
                                        lambda m: weight(m, 2 * QW + VW + pair * BANK, BANK))]).then_inc(chunk_ps, 1)

            heads(pe, iteration)


def last_norm(nc, dram, kept):
    ctx = ExitStack()
    with ctx:
        acc = kept["acc"]
        stats = ctx.enter_context(nc.sbuf_tensor("statsC", [P, B, NT, 6], F32))
        mv = ctx.enter_context(nc.sbuf_tensor("mvC", [P, B, NT, 2], F32))
        ve = ctx.enter_context(nc.sbuf_tensor("veC", [P, B, NT], F32))
        rstd = ctx.enter_context(nc.sbuf_tensor("rstdC", [P, B, NT], F32))
        mhalf = ctx.enter_context(nc.sbuf_tensor("mhalfC", [P, NT], F32))
        stats_ready = ctx.enter_context(nc.semaphore("stats_readyC"))
        var_ready = ctx.enter_context(nc.semaphore("var_readyC"))
        pool_step = ctx.enter_context(nc.semaphore("pool_stepC"))
        rstd_ready = ctx.enter_context(nc.semaphore("rstd_readyC"))
        out_ready = ctx.enter_context(nc.semaphore("out_ready"))
        stored = ctx.enter_context(nc.semaphore("storedC"))
        block = ctx.enter_context(nc.Block())

        @block.vector
        def _(dve):
            v = nc.vector

            def normalise(b):
                dve.wait_ge(rstd_ready, b + 1)
                for t in range(NT):
                    last = v.tensor_scalar(out=acc[:, b, t, :], in0=acc[:, b, t, :], scalar1=mv[:, b, t, 0:1],
                                           scalar2=rstd[:, b, t:t + 1], op0=ALU.subtract, op1=ALU.mult)
                last.then_inc(out_ready, 1)

            for b in range(B):
                for t in range(NT):
                    last = v.bn_stats(out=stats[:, b, t, :], in_=acc[:, b, t, :])
                last.then_inc(stats_ready, 1)
                dve.wait_ge(stats_ready, b + 1)
                for t in range(NT):
                    last = v.bn_aggr(out=mv[:, b, t, :], in_=stats[:, b, t, :])
                last.then_inc(var_ready, 1)
                if b:
                    normalise(b - 1)
            normalise(B - 1)

        @block.gpsimd
        def _(pool):
            g = nc.gpsimd
            g.memset(mhalf[:], -0.5).then_inc(pool_step, 1)
            for b in range(B):
                pool.wait_ge(var_ready, b + 1)
                g.tensor_scalar(out=ve[:, b, :], in0=mv[:, b, :, 1], scalar1=LN_EPS, scalar2=None, op0=ALU.add).then_inc(pool_step, 1)
                pool.wait_ge(pool_step, b + 2)
                g.tensor_tensor(out=rstd[:, b, :], in0=ve[:, b, :], in1=mhalf[:], op=ALU.pow).then_inc(rstd_ready, 1)

        @block.sync
        def _(sp):
            for b in range(B):
                sp.wait_ge(out_ready, b + 1)
                sp.dma_start(dram["out"][b].rearrange("(t p) d -> p t d", p=P), acc[:, b]).then_inc(stored, 16)
            sp.wait_ge(stored, 16 * B)


def build(nc, dram):
    with nc.sbuf_tensor("acc", [P, B, NT, D], F32) as acc, nc.sbuf_tensor("gates", [P, B, FH, 2, NT, E], F32) as gates:
        kept = {"acc": acc, "gates": gates}
        layer0_and_layer1_attention(nc, dram, kept)
        routed_heads(nc, dram, kept)
        last_norm(nc, dram, kept)


def kernel(**inputs):
    import concourse.bacc as bacc
    from concourse.bass_utils import run_bass_kernel_spmd

    nc = bacc.Bacc("TRN2", target_bir_lowering=False, num_devices=1)
    arrays = {f"in_{name}": a for name, a in layouts(inputs).items()}
    dram = {name[3:]: nc.dram_tensor(name, a.shape, mybir.dt.from_np(a.dtype), kind="ExternalInput").ap()
            for name, a in arrays.items()}
    dram["xs"] = nc.dram_tensor("routed_input", [B, P, 2 * DK * T], F32, kind="Internal").ap()
    dram["out"] = nc.dram_tensor("out_0", [B, T, D], F32, kind="ExternalOutput").ap()
    build(nc, dram)
    return run_bass_kernel_spmd(nc, [arrays], core_ids=[0]).results[0]["out_0"]
```

```python
import concourse.bass as bass
from concourse import mybir
from contextlib import ExitStack

F32 = mybir.dt.float32
BF16 = mybir.dt.bfloat16
F32R = mybir.dt.float32r
ALU = mybir.AluOpType
ACT = mybir.ActivationFunctionType
AX = mybir.AxisListType

P = 128
B = 8
T = 512
NT = T // P
D = 256
DK = D // P
H = 16
HD = D // H
HP = 32
HG = P // HP
NG = H // HG
KV = 4
QKV = D + 2 * KV * HD
FH = 8
E = 8
FP = 128
SEL = FH * E
BANK = 512
LN_EPS = 1e-5
QK_EPS = 1e-6
MASKED = -1e30
ATT_SCALE = HD ** -0.5
FFN_SCALE = FP ** -0.5
UNITS = H * NT
LAG = 3


def layer0_and_layer1_attention(nc, dram, kept):
    ctx = ExitStack()
    with ctx:
        def sb(name, shape, dt=F32):
            return ctx.enter_context(nc.sbuf_tensor(name, shape, dt))

        def sem(name):
            return ctx.enter_context(nc.semaphore(name))

        def in_turn(first, then):
            with ExitStack() as early:
                a = [early.enter_context(nc.sbuf_tensor(*x)) for x in first]
            return a, [sb(*x) for x in then]

        wq = sb("wq", [P, DK, NG * P])
        wk = sb("wk", [P, DK, NG * P])
        wv = sb("wv", [P, DK, D])
        wo = sb("wo", [P, DK, D])
        bq = sb("bq", [P, NG])
        bk = sb("bk", [P, NG])
        bv = sb("bv", [P, D])
        bo = sb("bo", [P, D])
        gamma = sb("gamma", [P, D])
        beta = sb("beta", [P, D])
        wt = sb("wt", [P, DK, D])
        tern = sb("tern", [P, DK, D])
        w1 = sb("w1", [P, DK, QKV])
        wp = sb("wp", [P, DK, D])
        wsel = sb("wsel", [P, DK, 2 * SEL])
        cos = sb("cos", [P, NT, HD])
        sin = sb("sin", [P, NT, HD])
        rank = sb("rank", [P, E])
        rscale = sb("rscale", [P, 1])
        ident = sb("ident", [P, P])
        identb = sb("identb", [P, P], BF16)
        cmask = sb("cmask", [P, P], BF16)
        band = sb("band", [P, BANK], BF16)
        diag = sb("diag", [P, BANK], BF16)
        ones = sb("ones", [P, P])
        tscale = sb("tscale", [P, 2])
        tsum = sb("tsum", [P, 2])
        mhalf = sb("mhalf", [P, NT * (H + KV)])
        phalf = sb("phalf", [P, NT * (H + KV)])
        eps = sb("eps", [P, NT])
        pad = sb("pad", [P, 1])
        x_in = sb("x_in", [P, NT, D])
        tT = [sb(f"tT{i}", [P, DK, T]) for i in range(2)]
        (kT,), (o, z, x1, x2) = in_turn([("kT", [P, 2, NG, T], F32R)], [(n, [P, NT, D], F32) for n in ("o", "z", "x1", "x2")])
        (q1lo,), (probs,) = in_turn([("q1lo", [P, HG, T], F32R)], [("probs", [P, 4, T], F32)])
        (xhl,), (oTs,) = in_turn([("xhl", [P, 2, DK, T], F32R)], [("oTs", [P, NG, T], F32)])
        (xbeta,), (qkv,) = in_turn([("xbeta", [P, NT, D], F32)], [("qkv", [P, NT, QKV], F32)])
        (qst,), (qpad,) = in_turn([("qst", [P, NG, T], F32)], [("qpad", [P, NT, HG * P], F32)])
        (q1hi,), (qs,) = in_turn([("q1hi", [P, HG, T], F32R)], [("qs", [P, NG, T], F32)])
        alone = sb("alone", [P, 2 * HG, T], F32R)
        vaug = sb("vaug", [P, NT, H, HP])
        nmax = sb("nmax", [P, 8])
        pT = sb("pT", [P, HG, NT, T])
        rden = sb("rden", [P, NT, H])
        stats = sb("stats", [P, NT, 6])
        mv = sb("mv", [P, NT, 2])
        ve = sb("ve", [P, NT])
        rstd = sb("rstd", [P, NT])
        v1aug = sb("v1aug", [P, NT, KV, HP])
        kpad = sb("kpad", [P, NT, P])
        ss = sb("ss", [P, NT * (H + KV)])
        nrm = sb("nrm", [P, NT * (H + KV)])
        rowsel = sb("rowsel", [P, 2])
        qf = pT[:, 0]
        sq = pT[:, 0, :, 0:(H + KV) * HD]
        rot = pT[:, 1, :, 0:(H + KV) * HD]
        qn = pT[:, 2, :, 0:(H + KV) * HD]
        p1T = [pT[:, i, k:k + 2, :].rearrange("p k q -> p (k q)") for i in (1, 2, 0) for k in (0, 2)][0:KV + 1]
        gw = [pT[:, 0, i, :] for i in range(NT)]
        m12 = sb("m12", [P, 4, NT * 2 * FH])

        ps = ctx.enter_context(nc.psum_tensor("psA", [P, 8, BANK], F32))

        loaded = sem("loaded")
        const_v = sem("const_v")
        const_g = sem("const_g")
        const_p = sem("const_p")
        x_loaded = sem("x_loaded")
        x_free = sem("x_free")
        tr_ps = sem("tr_ps")
        tr_sb = sem("tr_sb")
        q_ps = sem("q_ps")
        k_ps = sem("k_ps")
        absum_ps = sem("absum_ps")
        v_ps = sem("v_ps")
        q_ready = sem("q_ready")
        k_ready = sem("k_ready")
        qf_ready = sem("qf_ready")
        qs_ready = sem("qs_ready")
        khi_ready = sem("khi_ready")
        alone_ready = sem("alone_ready")
        v_ready = sem("v_ready")
        s_ps = sem("s_ps")
        max_ready = sem("max_ready")
        exp_ready = sem("exp_ready")
        t_ps = sem("t_ps")
        pt_a = sem("pt_a")
        pt_v = sem("pt_v")
        ot_ps = sem("ot_ps")
        ot_ready = sem("ot_ready")
        on_ps = sem("on_ps")
        o_ready = sem("o_ready")
        y_ps = sem("y_ps")
        y_read = sem("y_read")
        var_ready = sem("var_ready")
        rstd_ready = sem("rstd_ready")
        xb_ready = sem("xb_ready")
        x_ready = sem("x_ready")
        qkv_ps = sem("qkv_ps")
        qkv_ready = sem("qkv_ready")
        ss_ready = sem("ss_ready")
        nrm_ready = sem("nrm_ready")
        rope_ready = sem("rope_ready")
        v1_ready = sem("v1_ready")
        qk1_ps = sem("qk1_ps")
        qk1_a = sem("qk1_a")
        qk1_v = sem("qk1_v")
        s1_ps = sem("s1_ps")
        exp1_ready = sem("exp1_ready")
        av1_done = sem("av1_done")
        logit_ps = sem("logit_ps")
        logit_read = sem("logit_read")
        xhi_ready = sem("xhi_ready")
        xlo_ready = sem("xlo_ready")
        store_sem = sem("store_sem")
        stored = sem("stored")
        dve_step = sem("dve_step")
        pool_step = sem("pool_step")
        act_step = sem("act_step")
        DVE_STEPS = 45
        POOL_STEPS = 4

        block = ctx.enter_context(nc.Block())

        LOADS = [(wq[:], dram["wq"]), (wk[:], dram["wk"]), (wv[:], dram["wv"]), (wo[:], dram["wo"]),
                 (bq[:], dram["bq"]), (bk[:], dram["bk"]), (bv[:], dram["bv"].partition_broadcast(P)),
                 (bo[:], dram["bo"].partition_broadcast(P)), (gamma[:], dram["gamma"].partition_broadcast(P)),
                 (beta[:], dram["beta"].partition_broadcast(P)), (wt[:], dram["wt"]), (w1[:], dram["w1"]),
                 (wp[:], dram["wp"]), (wsel[:], dram["wsel"]), (cos[:], dram["cos"]), (sin[:], dram["sin"]),
                 (rank[:], dram["rank"].partition_broadcast(P)), (rowsel[:], dram["rowsel"]),
                 (rscale[:], dram["route_scale"].partition_broadcast(P)), (ident[:], dram["ident"])]

        @block.sync
        def _(sp):
            sp.dma_start(x_in[:], dram["x"][0].rearrange("(t p) d -> p t d", p=P)).then_inc(x_loaded, 16)
            for dst, src in LOADS:
                sp.dma_start(dst, src).then_inc(loaded, 16)
            sp.sem_inc(stored, 1)

            def store(b):
                sp.wait_ge(xhi_ready, b + 1)
                sp.wait_ge(xlo_ready, b + 1)
                sp.dma_start(dram["xs"][bass.ds(b, 1)].rearrange("o p n -> p (o n)"),
                             xhl[:].rearrange("p a k t -> p (a k t)").bitcast(F32)).then_inc(store_sem, 16)
                sp.wait_ge(store_sem, b * 16 + 16)
                sp.sem_inc(stored, 1)

            with sp.Fori(0, B - 1) as b:
                sp.wait_ge(x_free, b + 1)
                sp.dma_start(x_in[:], dram["x"][bass.ds(b + 1, 1)].rearrange("o (t p) d -> p (o t) d", p=P)).then_inc(x_loaded, 16)
                store(b)
            store(B - 1)

        def all_loaded(eng):
            eng.wait_ge(loaded, 16 * len(LOADS))

        @block.gpsimd
        def _(pool):
            g = nc.gpsimd
            g.memset(mhalf[:], -0.5).then_inc(const_p, 1)
            g.memset(phalf[:], 0.5).then_inc(const_p, 1)
            g.memset(alone[:].bitcast(F32), 0.0).then_inc(const_g, 1)
            g.memset(eps[:], LN_EPS).then_inc(const_p, 1)
            g.memset(cmask[:], 0.0).then_inc(const_p, 1)
            g.memset(band[:], 0.0).then_inc(const_p, 1)
            g.memset(diag[:], 0.0).then_inc(const_p, 1)
            pool.wait_ge(const_p, 6)
            g.affine_select(out=cmask[:], in_=cmask[:], compare_op=ALU.is_ge, fill=MASKED, base=0,
                            pattern=[[-1, P]], channel_multiplier=1).then_inc(const_g, 1)
            g.affine_select(out=band[:].rearrange("p (j q) -> p j q", j=2), in_=band[:].rearrange("p (j q) -> p j q", j=2),
                            compare_op=ALU.is_ge, fill=MASKED, base=0,
                            pattern=[[0, 2], [1, 2 * P]], channel_multiplier=-1).then_inc(const_p, 1)
            pool.wait_ge(const_p, 7)
            g.affine_select(out=band[:].rearrange("p (j q) -> p j q", j=2), in_=band[:].rearrange("p (j q) -> p j q", j=2),
                            compare_op=ALU.is_ge, fill=MASKED, base=P - 1,
                            pattern=[[0, 2], [-1, 2 * P]], channel_multiplier=1).then_inc(const_g, 1)
            g.affine_select(out=diag[:].rearrange("p (j q) -> p j q", j=4), in_=diag[:].rearrange("p (j q) -> p j q", j=4),
                            compare_op=ALU.is_ge, fill=MASKED, base=0,
                            pattern=[[0, 4], [1, P]], channel_multiplier=-1).then_inc(const_g, 1)
            all_loaded(pool)
            pool.wait_ge(const_g, 4)
            with pool.Fori(0, B) as b:
                step = [0]

                def link(ins):
                    step[0] += 1
                    ins.then_inc(pool_step, 1)
                    pool.wait_ge(pool_step, b * POOL_STEPS + step[0])

                pool.wait_ge(x_loaded, b * 16 + 16)
                pool.wait_ge(tr_ps, b * 12 + 2)
                g.tensor_tensor(out=xbeta[:], in0=x_in[:], in1=beta[:].unsqueeze(1).to_broadcast([P, NT, D]),
                                op=ALU.add).then_inc(x_free, 1)

                def root(n):
                    pool.wait_ge(var_ready, b * 4 + n)
                    link(g.tensor_tensor(out=ve[:], in0=mv[:, :, 1], in1=eps[:], op=ALU.add))
                    g.tensor_tensor(out=rstd[:], in0=ve[:], in1=mhalf[:, 0:NT], op=ALU.pow).then_inc(rstd_ready, 1)

                for G in range(NG):
                    pool.wait_ge(q_ready, b * NG + G + 1)
                    pool.wait_ge(qs_ready, b * NG + G + 1)
                    if G >= 2:
                        pool.wait_ge(s_ps, b * UNITS + (G - 1) * HG * NT)
                    if G:
                        pool.wait_ge(alone_ready, b * H + G * HG)
                    else:
                        pool.wait_ge(x_free, b + 1)
                    for j in range(HG):
                        rows = slice(j * HP, (j + 1) * HP)
                        g.tensor_tensor(out=alone[rows, G % 2 * HG + j, :], in0=qst[rows, G, :], in1=qs[rows, G, :],
                                        op=ALU.add).then_inc(alone_ready, 1)
                pool.wait_ge(alone_ready, b * H + H)
                root(1)
                root(2)
                root(3)
                pool.wait_ge(ss_ready, b + 1)
                g.tensor_tensor(out=nrm[:], in0=ss[:], in1=phalf[:], op=ALU.pow).then_inc(nrm_ready, 1)
                root(4)
                assert step[0] == POOL_STEPS

        @block.scalar
        def _(act):
            a = nc.scalar
            all_loaded(act)
            a.activation(identb[:], ident[:], ACT.Copy).then_inc(act_step, 1)
            with act.Fori(0, B) as b:
                def tt_evac(n):
                    act.wait_ge(tr_ps, b * 12 + 2 * n + 1)
                    a.activation(tT[n % 2][:, 0, :], ps[:, 0, :], ACT.Copy).then_inc(tr_sb, 1)

                tt_evac(0)
                for G in range(NG):
                    act.wait_ge(qf_ready, b * NG + G + 1)
                    a.activation(qs[:, G, :].bitcast(F32R), qf[:, G, :], ACT.Copy, scale=rowsel[:, 1:2]).then_inc(qs_ready, 1)
                for G in range(NG):
                    act.wait_ge(k_ps, b * NG + G + 1)
                    a.activation(kT[:, 0, G, :], ps[:, (6 + G) % 8, :], ACT.Identity, bias=bk[:, G:G + 1]).then_inc(khi_ready, 1)
                for u in range(UNITS + LAG):
                    if u < UNITS:
                        n = (u % NT + 1) * P
                        act.wait_ge(max_ready, b * UNITS + u + 1)
                        a.activation(probs[:, u % 4, 0:n], ps[:, 4 + u % 4, 0:n], ACT.Exp,
                                     bias=nmax[:, u % 8:u % 8 + 1]).then_inc(exp_ready, 1)
                    w = u - LAG
                    if w >= 0 and (w % NT) % 2 == 0:
                        h, qt = divmod(w, NT)
                        act.wait_ge(t_ps, b * UNITS + w + 1)
                        if h % HG == 0 and qt == 0 and h:
                            act.wait_ge(ot_ps, b * NG + h // HG)
                        a.activation(pT[:, h % HG, 0:qt + 1, qt * P:(qt + 1) * P],
                                     ps[:, w % 2, 0:(qt + 1) * P].rearrange("p (k q) -> p k q", q=P), ACT.Copy).then_inc(pt_a, 1)
                tt_evac(1)
                tt_evac(2)
                tt_evac(3)
                for t in range(NT):
                    act.wait_ge(qkv_ps, b * NT + t + 1)
                    a.activation(qkv[:, t, :], ps[:, 4 + t, 0:QKV], ACT.Copy).then_inc(qkv_ready, 1)
                act.wait_ge(qkv_ready, b * NT + NT)
                for t in range(NT):
                    a.activation(v1aug[:, t, :, 0:HD], qkv[:, t, D + KV * HD:QKV].rearrange("p (g d) -> p g d", g=KV),
                                 ACT.Copy).then_inc(v1_ready, 1)
                for j in range(HG):
                    act.wait_ge(qk1_ps, b * 5 + j + 1)
                    a.activation(q1hi[:, j, :], ps[:, j, :], ACT.Copy).then_inc(qk1_a, 1)
                act.wait_ge(qk1_ps, b * 5 + 5)
                for g in range(KV):
                    rows = slice(g * HP, (g + 1) * HP)
                    a.activation(alone[rows, g, :], ps[rows, 4, :], ACT.Copy).then_inc(qk1_a, 1)
                for w in range(KV * NT):
                    kt = w // KV
                    act.wait_ge(s1_ps, b * KV * NT + w + 1)
                    if w >= KV + 1:
                        act.wait_ge(av1_done, b * NT + (w - KV - 1) // KV + 1)
                    bank = 4 + 2 * (w % 2)
                    n = 1024 if kt < NT - 1 else BANK
                    src = ps[:, bank:bank + 2, :].rearrange("p a n -> p (a n)") if n == 1024 else ps[:, bank, :]
                    a.activation(p1T[w % (KV + 1)][:, 0:n], src, ACT.Exp, scale=ATT_SCALE).then_inc(exp1_ready, 1)
                tt_evac(4)
                tt_evac(5)
                act.wait_ge(tr_sb, b * 12 + 12)
                act.wait_ge(stored, b + 1)
                a.activation(xhl[:, 0], tT[1][:], ACT.Copy).then_inc(xhi_ready, 1)
                act.wait_ge(logit_ps, b + 1)
                a.activation(gw[0], ps[:, 6, :], ACT.Exp, scale=-1.0).then_inc(logit_read, 1)

        @block.vector
        def _(dve):
            v = nc.vector
            v.memset(vaug[:], 0.0).then_inc(const_v, 1)
            v.memset(v1aug[:], 0.0).then_inc(const_v, 1)
            v.memset(kpad[:], 0.0).then_inc(const_v, 1)
            v.memset(ones[:], 1.0).then_inc(const_v, 1)
            dve.wait_ge(const_v, 4)
            v.memset(vaug[:, :, :, HD:HD + 1], 1.0).then_inc(const_v, 1)
            v.memset(v1aug[:, :, :, HD:HD + 1], 1.0).then_inc(const_v, 1)
            all_loaded(dve)
            v.tensor_reduce(out=tsum[:, 0:1], in_=wt[:].rearrange("p k n -> p (k n)"), axis=AX.X, op=ALU.add,
                            apply_absolute_value=True).then_inc(const_v, 1)
            dve.wait_ge(absum_ps, 1)
            v.tensor_scalar(out=tscale[:, 1:2], in0=ps[:, 7, 0:1], scalar1=1.0 / (D * D), scalar2=LN_EPS,
                            op0=ALU.mult, op1=ALU.max).then_inc(const_v, 1)
            dve.wait_ge(const_v, 8)
            v.tensor_scalar(out=tscale[:, 0:1], in0=tscale[:, 1:2], scalar1=0.5, scalar2=None, op0=ALU.mult).then_inc(const_v, 1)
            v.tensor_scalar(out=tsum[:, 1:2], in0=tscale[:, 1:2], scalar1=-0.5, scalar2=None, op0=ALU.mult).then_inc(const_v, 1)
            dve.wait_ge(const_v, 10)
            v.tensor_scalar(out=tern[:], in0=wt[:], scalar1=tsum[:, 1:2], scalar2=None, op0=ALU.is_lt).then_inc(const_v, 1)
            dve.wait_ge(const_v, 11)
            v.scalar_tensor_tensor(out=tern[:], in0=wt[:], scalar=tscale[:, 0:1], in1=tern[:], op0=ALU.is_gt,
                                   op1=ALU.subtract).then_inc(const_v, 1)

            with dve.Fori(0, B) as b:
                step = [0]

                def link(ins):
                    step[0] += 1
                    ins.then_inc(dve_step, 1)
                    dve.wait_ge(dve_step, b * DVE_STEPS + step[0])

                def tt_evac(n):
                    dve.wait_ge(tr_ps, b * 12 + 2 * n + 2)
                    v.tensor_copy(tT[n % 2][:, 1, :], ps[:, 1, :]).then_inc(tr_sb, 1)

                def layer_norm(n, src, out, done):
                    for t in range(NT):
                        last = v.bn_stats(out=stats[:, t, :], in_=src[:, t, :])
                    link(last)
                    v.memset(pad[:], 0.0)
                    for t in range(NT):
                        last = v.bn_aggr(out=mv[:, t, :], in_=stats[:, t, :])
                    last.then_inc(var_ready, 1)
                    dve.wait_ge(rstd_ready, b * 4 + n)
                    for t in range(NT):
                        last = v.tensor_scalar(out=out[:, t, :], in0=src[:, t, :], scalar1=mv[:, t, 0:1], scalar2=rstd[:, t:t + 1],
                                               op0=ALU.subtract, op1=ALU.mult)
                    done(last)

                def token_ready(n):
                    def done(ins):
                        ins.then_inc(x_ready, 1)
                        dve.wait_ge(x_ready, b * 3 + n)
                    return done

                tt_evac(0)
                def query_parts(G):
                    dve.wait_ge(qf_ready, b * NG + G + 1)
                    v.tensor_scalar(out=qst[:, G, :], in0=qf[:, G, :], scalar1=rowsel[:, 0:1], scalar2=None,
                                    op0=ALU.mult).then_inc(q_ready, 1)

                for G in range(NG):
                    dve.wait_ge(q_ps, b * NG + G + 1)
                    v.tensor_scalar(out=qf[:, G, :], in0=ps[:, 2 + G, :], scalar1=bq[:, G:G + 1], scalar2=ATT_SCALE,
                                    op0=ALU.add, op1=ALU.mult).then_inc(qf_ready, 1)
                    if G:
                        query_parts(G - 1)
                query_parts(NG - 1)
                for G in range(NG):
                    dve.wait_ge(khi_ready, b * NG + G + 1)
                    v.scalar_tensor_tensor(out=kT[:, 1, G, :], in0=ps[:, (6 + G) % 8, :], scalar=bk[:, G:G + 1],
                                           in1=kT[:, 0, G, :].bitcast(F32), op0=ALU.add, op1=ALU.subtract).then_inc(k_ready, 1)
                dve.wait_ge(stored, b + 1)
                for i in range(2):
                    dve.wait_ge(v_ps, b * 2 + i + 1)
                    for t in range(2):
                        last = v.tensor_tensor(out=vaug[:, 2 * i + t, :, 0:HD],
                                        in0=ps[:, 2 + i, t * D:(t + 1) * D].rearrange("p (h d) -> p h d", h=H),
                                        in1=bv[:].rearrange("p (h d) -> p h d", h=H), op=ALU.add)
                    last.then_inc(v_ready, 1)
                for u in range(UNITS + LAG):
                    if u < UNITS:
                        n = (u % NT + 1) * P
                        dve.wait_ge(s_ps, b * UNITS + u + 1)
                        if u >= 8:
                            dve.wait_ge(exp_ready, b * UNITS + u - 7)
                        v.tensor_reduce(out=nmax[:, u % 8:u % 8 + 1], in_=ps[:, 4 + u % 4, 0:n], axis=AX.X, op=ALU.max,
                                        negate=True).then_inc(max_ready, 1)
                    w = u - LAG
                    if w >= 0 and (w % NT) % 2 == 1:
                        h, qt = divmod(w, NT)
                        dve.wait_ge(t_ps, b * UNITS + w + 1)
                        if h % HG == 0 and qt == 1 and h:
                            dve.wait_ge(ot_ps, b * NG + h // HG)
                        v.tensor_copy(pT[:, h % HG, 0:qt + 1, qt * P:(qt + 1) * P],
                                      ps[:, w % 2, 0:(qt + 1) * P].rearrange("p (k q) -> p k q", q=P)).then_inc(pt_v, 1)
                    if w >= 0 and w % (NT * HG) == 2 and w > 2:
                        G = w // (NT * HG) - 1
                        dve.wait_ge(ot_ps, b * NG + G + 1)
                        v.tensor_copy(oTs[:, G, :], ps[:, 2 + G % 2, :]).then_inc(ot_ready, 1)
                dve.wait_ge(ot_ps, b * NG + NG)
                v.tensor_copy(oTs[:, NG - 1, :], ps[:, 2 + (NG - 1) % 2, :]).then_inc(ot_ready, 1)

                def normalised(layer):
                    for t in range(NT):
                        dve.wait_ge(on_ps, b * 2 * NT + layer * NT + t + 1)
                        heads = ps[:, 4 + t, :].rearrange("p (c a d) -> p c a d", c=NG, a=HG)
                        link(v.reciprocal(out=rden[:, t, :].rearrange("p (c a) -> p c a", c=NG), in_=heads[:, :, :, HD]))
                        dst = o[:, t, :].rearrange("p (c a d) -> p c a d", c=NG, a=HG) if layer == 0 else \
                            o[:, t, :].rearrange("p (a c d) -> p c a d", c=NG, a=HG)
                        scale = rden[:, t, :].rearrange("p (c a) -> p c a", c=NG).unsqueeze(3).to_broadcast([P, NG, HG, HD])
                        v.tensor_tensor(out=dst, in0=heads[:, :, :, 0:HD], in1=scale, op=ALU.mult).then_inc(o_ready, 1)

                normalised(0)
                tt_evac(1)
                dve.wait_ge(y_ps, b * 3 * NT + NT)
                link(v.tensor_tensor(out=z[:], in0=ps[:, 2:4, :].rearrange("p a (t n) -> p (a t) n", t=2),
                                     in1=bo[:].unsqueeze(1).to_broadcast([P, NT, D]), op=ALU.add))
                layer_norm(1, z, z, link)
                link(v.tensor_tensor(out=z[:], in0=z[:], in1=gamma[:].unsqueeze(1).to_broadcast([P, NT, D]), op=ALU.mult))
                dve.wait_ge(x_free, b + 1)
                link(v.tensor_tensor(out=z[:], in0=z[:], in1=xbeta[:], op=ALU.add))
                layer_norm(2, z, x1, token_ready(1))
                tt_evac(2)
                dve.wait_ge(y_ps, b * 3 * NT + 2 * NT)
                link(v.scalar_tensor_tensor(out=z[:].rearrange("p t n -> p (t n)"), in0=ps[:, 2:4, :].rearrange("p a n -> p (a n)"),
                                            scalar=tscale[:, 1:2], in1=x1[:].rearrange("p t n -> p (t n)"),
                                            op0=ALU.mult, op1=ALU.add))
                layer_norm(3, z, x2, token_ready(2))
                tt_evac(3)
                dve.wait_ge(qkv_ready, b * NT + NT)
                qk = qkv[:, :, 0:D + KV * HD]
                link(v.tensor_tensor(out=sq, in0=qk, in1=qk, op=ALU.mult))
                v.tensor_reduce(out=ss[:].rearrange("p (t h) -> p t h", t=NT), in_=sq.rearrange("p t (h d) -> p t h d", d=HD),
                                axis=AX.X, op=ALU.add).then_inc(ss_ready, 1)
                dve.wait_ge(nrm_ready, b + 1)
                link(v.tensor_scalar(out=nrm[:], in0=nrm[:], scalar1=QK_EPS, scalar2=None, op0=ALU.add))
                link(v.reciprocal(out=ss[:], in_=nrm[:]))
                heads = H + KV
                for t in range(NT):
                    last = v.tensor_tensor(out=qn[:, t, :].rearrange("p (h d) -> p h d", d=HD),
                                           in0=qkv[:, t, 0:D + KV * HD].rearrange("p (h d) -> p h d", d=HD),
                                           in1=ss[:, t * heads:(t + 1) * heads].unsqueeze(2).to_broadcast([P, heads, HD]),
                                           op=ALU.mult)
                link(last)
                half = HD // 2
                qnh = qn.rearrange("p t (h d) -> p t h d", d=HD)
                roth = rot.rearrange("p t (h d) -> p t h d", d=HD)
                for t in range(NT):
                    v.tensor_tensor(out=roth[:, t, :, 0:half], in0=qnh[:, t, :, half:HD],
                                    in1=sin[:, t, 0:half].unsqueeze(1).to_broadcast([P, heads, half]), op=ALU.mult)
                    last = v.tensor_tensor(out=roth[:, t, :, half:HD], in0=qnh[:, t, :, 0:half],
                                           in1=sin[:, t, half:HD].unsqueeze(1).to_broadcast([P, heads, half]), op=ALU.mult)
                link(last)
                for t in range(NT):
                    last = v.tensor_tensor(out=qnh[:, t], in0=qnh[:, t],
                                           in1=cos[:, t, :].unsqueeze(1).to_broadcast([P, heads, HD]), op=ALU.mult)
                link(last)
                for t in range(NT):
                    v.tensor_tensor(out=qpad[:, t, :].rearrange("p (j g d) -> p j g d", j=HG, g=KV)[:, :, :, 0:HD],
                                    in0=qn[:, t, 0:D].rearrange("p (g j d) -> p j g d", g=KV, j=HG),
                                    in1=rot[:, t, 0:D].rearrange("p (g j d) -> p j g d", g=KV, j=HG), op=ALU.add)
                    last = v.tensor_tensor(out=kpad[:, t, :].rearrange("p (g d) -> p g d", g=KV)[:, :, 0:HD],
                                           in0=qn[:, t, D:D + KV * HD].rearrange("p (g d) -> p g d", g=KV),
                                           in1=rot[:, t, D:D + KV * HD].rearrange("p (g d) -> p g d", g=KV), op=ALU.add)
                last.then_inc(rope_ready, 1)
                for j in range(HG):
                    dve.wait_ge(qk1_a, b * 8 + j + 1)
                    v.tensor_tensor(out=q1lo[:, j, :], in0=ps[:, j, :], in1=q1hi[:, j, :].bitcast(F32), op=ALU.subtract).then_inc(qk1_v, 1)
                for g in range(KV):
                    rows = slice(g * HP, (g + 1) * HP)
                    dve.wait_ge(qk1_a, b * 8 + 4 + g + 1)
                    v.tensor_tensor(out=alone[rows, KV + g, :], in0=ps[rows, 4, :], in1=alone[rows, g, :].bitcast(F32),
                                    op=ALU.subtract).then_inc(qk1_v, 1)
                for c in range(NG):
                    dve.wait_ge(av1_done, b * NT + NT)
                    v.tensor_copy(oTs[:, c, :], ps[:, c, :]).then_inc(ot_ready, 1)
                normalised(1)
                tt_evac(4)
                dve.wait_ge(y_ps, b * 3 * NT + 3 * NT)
                link(v.tensor_tensor(out=z[:], in0=ps[:, 2:4, :].rearrange("p a (t n) -> p (a t) n", t=2), in1=x2[:], op=ALU.add))
                layer_norm(4, z, x1, token_ready(3))
                tt_evac(5)
                link(v.tensor_copy(kept["acc"][:, bass.ds(b, 1)].rearrange("p o t d -> p (o t) d"), x1[:]))
                dve.wait_ge(xhi_ready, b + 1)
                v.tensor_tensor(out=xhl[:, 1], in0=tT[1][:], in1=xhl[:, 0].bitcast(F32), op=ALU.subtract).then_inc(xlo_ready, 1)
                dve.wait_ge(logit_read, b + 2)
                NGR = NT * 2 * FH
                g3 = [x.rearrange("p (c e) -> p c e", e=E) for x in gw]
                wide = [P, NGR, E]
                ranks = rank[:].unsqueeze(1).to_broadcast(wide)
                link(v.tensor_scalar(out=gw[1], in0=gw[0], scalar1=1.0, scalar2=None, op0=ALU.add))
                link(v.reciprocal(out=gw[0], in_=gw[1]))

                def first_largest(src, top, hot, tmp):
                    link(v.tensor_reduce(out=m12[:, top, :], in_=g3[src], axis=AX.X, op=ALU.max))
                    link(v.tensor_tensor(out=g3[tmp], in0=g3[src], in1=m12[:, top, :].unsqueeze(2).to_broadcast(wide), op=ALU.is_equal))
                    link(v.tensor_tensor(out=g3[tmp], in0=g3[tmp], in1=ranks, op=ALU.mult))
                    link(v.tensor_reduce(out=m12[:, 3, :], in_=g3[tmp], axis=AX.X, op=ALU.max))
                    link(v.tensor_tensor(out=g3[hot], in0=g3[tmp], in1=m12[:, 3, :].unsqueeze(2).to_broadcast(wide), op=ALU.is_equal))

                first_largest(0, 0, 1, 2)
                link(v.scalar_tensor_tensor(out=gw[2], in0=gw[1], scalar=-2.0, in1=gw[0], op0=ALU.mult, op1=ALU.add))
                first_largest(2, 1, 3, 3)
                link(v.tensor_tensor(out=gw[1], in0=gw[1], in1=gw[3], op=ALU.add))
                link(v.tensor_tensor(out=gw[0], in0=gw[0], in1=gw[1], op=ALU.mult))
                link(v.tensor_tensor(out=m12[:, 2, :], in0=m12[:, 0, :], in1=m12[:, 1, :], op=ALU.add))
                link(v.tensor_scalar(out=m12[:, 2, :], in0=m12[:, 2, :], scalar1=1e-9, scalar2=None, op0=ALU.max))
                link(v.reciprocal(out=m12[:, 3, :], in_=m12[:, 2, :]))
                link(v.tensor_scalar(out=m12[:, 3, :], in0=m12[:, 3, :], scalar1=rscale[:, 0:1], scalar2=None, op0=ALU.mult))
                for t in range(NT):
                    n = 2 * FH
                    last = v.tensor_tensor(out=kept["gates"][:, bass.ds(b, 1), :, :, t, :].rearrange("p o h c e -> p c (o h) e"),
                                           in0=g3[0][:, t * n:(t + 1) * n, :].rearrange("p (c h) e -> p c h e", c=2),
                                           in1=m12[:, 3, t * n:(t + 1) * n].rearrange("p (c h) -> p c h", c=2).unsqueeze(3).to_broadcast([P, 2, FH, E]),
                                           op=ALU.mult)
                link(last)
                assert step[0] == DVE_STEPS, step[0]

        @block.tensor
        def _(pe):
            mm = nc.tensor.matmul
            all_loaded(pe)
            pe.wait_ge(const_v, 7)
            mm(ps[:, 7, 0:1], ones[:], tsum[:, 0:1], start=True, stop=True).then_inc(absum_ps, 1)
            pe.wait_ge(const_v, 12)
            pe.wait_ge(const_g, 4)
            pe.wait_ge(act_step, 1)
            pe.sem_inc(logit_read, 1)
            with pe.Fori(0, B) as b:
                def transposition(n, src, per_tile=None):
                    for k in range(DK):
                        for t in range(NT):
                            if per_tile:
                                per_tile(t)
                            last = nc.tensor.transpose(ps[:, k, t * P:(t + 1) * P], src[:, t, k * P:(k + 1) * P], ident[:])
                        last.then_inc(tr_ps, 1)

                def project(n, out, rhs, width, t, done=None):
                    for k in range(DK):
                        last = mm(out, tT[n % 2][:, k, t * P:(t + 1) * P], rhs[:, k, 0:width], start=(k == 0), stop=(k == DK - 1))
                    if done is not None:
                        last.then_inc(done, 1)

                pe.wait_ge(x_loaded, b * 16 + 16)
                transposition(0, x_in)
                pe.wait_ge(tr_sb, b * 12 + 2)
                pe.wait_ge(logit_read, b + 1)
                for w, first, done in ((wq, 2, q_ps), (wk, 6, k_ps)):
                    for G in range(NG):
                        for k in range(DK):
                            last = mm(ps[:, (first + G) % 8, :], w[:, k, G * P:(G + 1) * P], tT[0][:, k, :],
                                      start=(k == 0), stop=(k == DK - 1))
                        last.then_inc(done, 1)
                for i in range(2):
                    pe.wait_ge(qf_ready, b * NG + i + 1)
                    for t in range(2):
                        project(0, ps[:, 2 + i, t * D:(t + 1) * D], wv, D, 2 * i + t, v_ps if t else None)
                pe.wait_ge(k_ready, b * NG + NG)
                pe.wait_ge(v_ready, b * 2 + 2)

                def weighted(G):
                    pe.wait_ge(pt_a, b * 2 * H + 2 * HG * (G + 1))
                    pe.wait_ge(pt_v, b * 2 * H + 2 * HG * (G + 1))
                    if G >= 2:
                        pe.wait_ge(ot_ready, b * 2 * NG + G - 1)
                    for kt in range(NT):
                        for j in range(HG):
                            last = mm(ps[j * HP:(j + 1) * HP, 2 + G % 2, kt * P:T], vaug[:, kt, G * HG + j, :],
                                      pT[:, j, kt, kt * P:T], start=(kt == 0), stop=(kt == NT - 1), skip_group_check=True)
                    last.then_inc(ot_ps, 1)

                for u in range(UNITS + LAG):
                    if u < UNITS:
                        h, qt = divmod(u, NT)
                        G, j = divmod(h, HG)
                        if u >= 4:
                            pe.wait_ge(exp_ready, b * UNITS + u - 3)
                        if j == 0 and qt == 0:
                            pe.wait_ge(alone_ready, b * H + (G + 1) * HG)
                        bank = ps[:, 4 + u % 4, :]
                        n = max(qt + 1, 2) * P
                        for part in range(2):
                            mm(bank[:, 0:n], alone[:, G % 2 * HG + j, qt * P:(qt + 1) * P], kT[:, part, G, 0:n],
                               start=(part == 0), stop=False)
                        mm(bank[:, qt * P:(qt + 1) * P], identb[:], cmask[:], start=False, stop=True).then_inc(s_ps, 1)
                    w = u - LAG
                    if w >= 0:
                        qt = w % NT
                        pe.wait_ge(exp_ready, b * UNITS + w + 1)
                        if w >= 2:
                            pe.wait_ge(pt_v if qt % 2 else pt_a, b * 2 * H + (w - 2) // NT * 2 + (w - 2) % NT // 2 + 1)
                        for k in range(qt + 1):
                            last = nc.tensor.transpose(ps[:, w % 2, k * P:(k + 1) * P], probs[:, w % 4, k * P:(k + 1) * P], ident[:])
                        last.then_inc(t_ps, 1)
                        if w % (NT * HG) == NT * HG - 1:
                            weighted(w // (NT * HG))

                def back(layer):
                    pe.wait_ge(ot_ready, b * 2 * NG + layer * NG + NG)
                    for t in range(NT):
                        for c in range(NG):
                            last = nc.tensor.transpose(ps[:, 4 + t, c * P:(c + 1) * P], oTs[:, c, t * P:(t + 1) * P], ident[:])
                        last.then_inc(on_ps, 1)

                def to_width(n, rhs):
                    pe.wait_ge(tr_sb, b * 12 + 2 * n + 2)
                    for t in range(NT):
                        project(n, ps[:, 2 + t // 2, (t % 2) * D:(t % 2 + 1) * D], rhs, D, t, y_ps)

                back(0)
                transposition(1, o, lambda t: pe.wait_ge(o_ready, b * 2 * NT + t + 1))
                to_width(1, wo)
                pe.wait_ge(x_ready, b * 3 + 1)
                transposition(2, x1)
                to_width(2, tern)
                pe.wait_ge(x_ready, b * 3 + 2)
                transposition(3, x2)
                pe.wait_ge(tr_sb, b * 12 + 8)
                for t in range(NT):
                    project(3, ps[:, 4 + t, 0:QKV], w1, QKV, t, qkv_ps)
                pe.wait_ge(rope_ready, b + 1)
                pe.wait_ge(tr_sb, b * 12 + 8)
                pe.wait_ge(qkv_ready, b * NT + NT)
                for j in range(HG):
                    for t in range(NT):
                        last = nc.tensor.transpose(ps[:, j, t * P:(t + 1) * P], qpad[:, t, j * P:(j + 1) * P], ident[:])
                    last.then_inc(qk1_ps, 1)
                for t in range(NT):
                    last = nc.tensor.transpose(ps[:, 4, t * P:(t + 1) * P], kpad[:, t, :], ident[:])
                last.then_inc(qk1_ps, 1)
                pe.wait_ge(qk1_a, b * 8 + 8)
                pe.wait_ge(qk1_v, b * 8 + 8)
                pe.wait_ge(v1_ready, b * NT + NT)

                def weighted1(kt):
                    pe.wait_ge(exp1_ready, b * KV * NT + (kt + 1) * KV)
                    nq = 2 * P if kt < NT - 1 else P
                    for j in range(HG):
                        for g in range(KV):
                            last = mm(ps[g * HP:(g + 1) * HP, j, kt * P:kt * P + nq], v1aug[:, kt, g, :],
                                      p1T[(kt * KV + g) % (KV + 1)][:, j * nq:(j + 1) * nq],
                                      start=(kt == 0), stop=(kt == NT - 1), skip_group_check=True)
                    last.then_inc(av1_done, 1)

                for w in range(KV * NT + 1):
                    if w < KV * NT:
                        kt, g = divmod(w, KV)
                        if w >= 2:
                            pe.wait_ge(exp1_ready, b * KV * NT + w - 1)
                        bank = 4 + 2 * (w % 2)
                        for i in range(2 if kt < NT - 1 else 1):
                            hs = slice(2 * i, 2 * i + 2) if kt < NT - 1 else slice(0, HG)
                            qs_ = slice(kt * P, min((kt + 2) * P, T))
                            for k, (keys, queries) in enumerate(((0, q1hi), (0, q1lo), (1, q1hi))):
                                mm(ps[:, bank + i, :], alone[:, keys * KV + g, kt * P:(kt + 1) * P], queries[:, hs, qs_],
                                   start=(k == 0), stop=False)
                            last = mm(ps[:, bank + i, :], identb[:], (band if kt < NT - 1 else diag)[:], start=False, stop=True)
                        last.then_inc(s1_ps, 1)
                    if w and w % KV == 0:
                        weighted1(w // KV - 1)

                back(1)
                transposition(4, o, lambda t: pe.wait_ge(o_ready, b * 2 * NT + NT + t + 1))
                to_width(4, wp)
                pe.wait_ge(x_ready, b * 3 + 3)
                transposition(5, x1)
                pe.wait_ge(tr_sb, b * 12 + 12)
                for t in range(NT):
                    project(5, ps[:, 6, t * P:(t + 1) * P], wsel, 2 * SEL, t, logit_ps if t == NT - 1 else None)


def layouts(inputs):
    import numpy as np

    def rows(w):
        return np.ascontiguousarray(w.reshape(-1, P, w.shape[1]).transpose(1, 0, 2))

    def twice(w):
        return np.repeat(w.reshape(-1, H, 1, HD), 2, 2).reshape(-1, H * HP)

    i = {k: np.asarray(v) for k, v in inputs.items()}
    f = np.float32
    theta = 1.0 / 10000.0 ** (np.arange(0, HD, 2, dtype=f) / HD)
    freqs = np.outer(np.arange(T, dtype=f), theta).astype(f)
    cos = np.concatenate([np.cos(freqs)] * 2, 1).astype(f)
    sin = np.concatenate([-np.sin(freqs), np.sin(freqs)], 1).astype(f)
    table = lambda x: np.ascontiguousarray(x.reshape(NT, P, HD).transpose(1, 0, 2))
    return {
        "x": i["L0_attn_x"],
        "wq": rows(twice(i["L0_attn_Wq"])), "wk": rows(twice(i["L0_attn_Wk"])),
        "wv": rows(i["L0_attn_Wv"]), "wo": rows(i["L0_attn_Wo"]),
        "bq": np.ascontiguousarray(twice(i["L0_attn_bq"][None]).reshape(NG, P).T),
        "bk": np.ascontiguousarray(twice(i["L0_attn_bk"][None]).reshape(NG, P).T),
        "bv": i["L0_attn_bv"], "bo": i["L0_attn_bo"],
        "gamma": i["L0_attn_gamma"], "beta": i["L0_attn_beta"],
        "wt": rows(i["L0_ffn_weight"].T),
        "w1": rows(np.concatenate([i["L1_attn_Wq"].T, i["L1_attn_Wkv"].T], 1)),
        "wp": rows(i["L1_attn_Wproj"].T),
        "wsel": rows(np.concatenate([i["L1_ffn_sel_v_w"].T, i["L1_ffn_sel_o_w"].T], 1)),
        "cos": table(cos), "sin": table(sin),
        "rowsel": np.tile(np.repeat(np.array([[0, 1], [1, -1]], f), HD, 0), (HG, 1)),
        "rank": np.arange(E, 0, -1).astype(f),
        "route_scale": i["L1_ffn_route_scale"],
        "ident": np.eye(P, dtype=f),
        "wf": np.concatenate([
            i["L1_ffn_q_w"].reshape(FH, FP, DK, P).transpose(0, 3, 2, 1).reshape(FH, P, -1),
            i["L1_ffn_k_w"].reshape(FH, FP, DK, P).transpose(0, 3, 2, 1).reshape(FH, P, -1),
            i["L1_ffn_v_w"].reshape(FH, E, DK, P, FP).transpose(0, 3, 2, 1, 4).reshape(FH, P, -1),
            i["L1_ffn_o_w"].reshape(FH, E, FP, D).transpose(0, 2, 1, 3).reshape(FH, P, -1)], 2),
    }


def routed_heads(nc, dram, kept):
    ctx = ExitStack()
    with ctx:
        def sb(name, shape, dt=F32):
            return ctx.enter_context(nc.sbuf_tensor(name, shape, dt))

        def sem(name):
            return ctx.enter_context(nc.semaphore(name))

        acc, gates = kept["acc"], kept["gates"]
        QW, VW = DK * FP, DK * E * FP
        WCOLS = 2 * QW + VW + E * D
        SLICE = WCOLS // B
        stage = sb("stage", [P, WCOLS])
        whl = [sb(f"whl{i}", [P, 2, WCOLS], F32R) for i in range(2)]
        xhl = sb("xhlB", [P, 2, DK, T], F32R)
        gs = sb("gs", [P, 2, NT, E])
        go = sb("go", [P, NT, E])
        qhl = sb("qhl", [P, 2, T], F32R)
        khl = sb("khl", [P, 2, T], F32R)
        vacc = sb("vacc", [P, 2, 2, FP])
        vsum = sb("vsum", [P, NT, FP])
        vhl = sb("vhl", [P, 2, NT, FP], F32R)
        probs = sb("probsB", [P, 2, T])
        nmax = sb("nmaxB", [P, NT])
        rowsum = sb("rowsum", [P, NT])
        rinv = sb("rinv", [P, NT])
        pT = sb("pTB", [P, 2, NT, T], F32R)
        cT = sb("cT", [P, 2, T], F32R)
        part = sb("part", [P, NT, 2, D])
        weighted = sb("weighted", [P, 4, D])
        total = sb("total", [P, D])
        ident = sb("identB", [P, P])
        ps = ctx.enter_context(nc.psum_tensor("psB", [P, 8, BANK], F32))
        PROJ, TR, CTX, RING = 0, 2, (4, 2), 5
        HALF = T // 2
        VCH, OCH = 2, E // 2
        CHUNKS = NT * (VCH + OCH)
        NRING = 3
        VOPS, OOPS = E + 1, E // 2 + 1
        GATED = NT * (VOPS + OOPS)
        SCALED = NT * E // 2
        ADDS = E // 2 + 1

        ident_loaded = sem("ident_loadedB")
        w_loaded = sem("w_loaded")
        w_hi0 = sem("w_hi0")
        w_split = sem("w_split")
        w_hi = sem("w_hi")
        x_loaded = sem("x_loadedB")
        proj_ps = sem("proj_ps")
        qk_hi = sem("qk_hi")
        qk_lo = sem("qk_lo")
        chunk_ps = sem("chunk_ps")
        gated = sem("gated")
        scaled = sem("scaled")
        v_hi = sem("v_hi")
        v_lo = sem("v_lo")
        s_ps = sem("s_psB")
        max_ready = sem("max_readyB")
        exp_ready = sem("exp_readyB")
        t_ps = sem("t_psB")
        pt_hi = sem("pt_hi")
        pt_lo = sem("pt_lo")
        ctx_ps = sem("ctx_ps")
        ctx_hi = sem("ctx_hi")
        ctx_lo = sem("ctx_lo")
        go_ready = sem("go_ready")
        added = sem("added")
        dve_step = sem("dve_stepB")
        DVE_STEPS = 2

        block = ctx.enter_context(nc.Block())
        TERMS = ((0, 0), (0, 1), (1, 0))

        @block.sync
        def _(sp):
            sp.dma_start(stage[:], dram["wf"][0]).then_inc(w_loaded, 16)
            sp.dma_start(ident[:], dram["ident"]).then_inc(ident_loaded, 16)
            sp.dma_start(xhl[:].rearrange("p a k t -> p (a k t)").bitcast(F32), dram["xs"][0]).then_inc(x_loaded, 16)
            with sp.Fori(0, FH) as h:
                sp.wait_ge(w_split, h * B + 1)
                sp.dma_start(stage[:], dram["wf"][bass.ds((h + 1) % FH, 1)].rearrange("o p n -> p (o n)")).then_inc(w_loaded, 16)
                with sp.Fori(0, B) as b:
                    sp.wait_ge(chunk_ps, h * (B * CHUNKS) + b * CHUNKS + 2 * NT)
                    sp.dma_start(xhl[:].rearrange("p a k t -> p (a k t)").bitcast(F32),
                                 dram["xs"][bass.ds((b + 1) % B, 1)].rearrange("o p n -> p (o n)")).then_inc(x_loaded, 16)
            sp.wait_ge(x_loaded, 16 * (FH * B + 1))
            sp.wait_ge(w_loaded, 16 * (FH + 1))

        def heads(eng, body):
            with eng.Fori(0, FH // 2) as hh:
                for parity in range(2):
                    h = hh * 2 + parity
                    with eng.Fori(0, B) as b:
                        body(parity, h, b, hh * (2 * B) + b + parity * B)

        @block.gpsimd
        def _(pool):
            g = nc.gpsimd
            pool.sem_inc(added, NT * ADDS)

            def iteration(parity, h, b, i):
                pool.wait_ge(w_loaded, h * 16 + 32)
                part_in = stage[:, bass.ds(b * SLICE, SLICE)]
                hi = whl[1 - parity][:, 0, bass.ds(b * SLICE, SLICE)]
                g.tensor_copy(hi, part_in).then_inc(w_hi, 1)
                pool.wait_ge(w_hi, i + 1)
                g.tensor_tensor(out=whl[1 - parity][:, 1, bass.ds(b * SLICE, SLICE)], in0=part_in, in1=hi.bitcast(F32),
                                op=ALU.subtract).then_inc(w_split, 1)
                for t in range(NT):
                    done = (i + 1) * (NT * ADDS) + t * ADDS
                    for k in range(1, E // 2):
                        pool.wait_ge(scaled, i * SCALED + SCALED + t * (E // 2) + k + 1)
                        pool.wait_ge(added, done + k - 1)
                        g.tensor_tensor(out=total[:], in0=weighted[:, 0, :] if k == 1 else total[:], in1=weighted[:, k, :],
                                        op=ALU.add).then_inc(added, 1)
                    pool.wait_ge(gated, i * GATED + GATED + NT * VOPS + (t + 1) * OOPS)
                    pool.wait_ge(added, done + E // 2 - 1)
                    g.tensor_tensor(out=total[:], in0=total[:], in1=part[:, t, 0, :], op=ALU.add).then_inc(added, 1)
                    pool.wait_ge(added, done + E // 2)
                    dst = acc[:, bass.ds(b, 1), t, :].rearrange("p o n -> p (o n)")
                    g.tensor_tensor(out=dst, in0=dst, in1=total[:], op=ALU.add).then_inc(added, 1)

            heads(pool, iteration)

        @block.scalar
        def _(act):
            a = nc.scalar
            act.wait_ge(w_loaded, 16)
            a.activation(whl[0][:, 0, :], stage[:], ACT.Copy).then_inc(w_hi0, 1)

            def iteration(parity, h, b, i):
                for n, (dst, scale) in enumerate(((qhl, FFN_SCALE), (khl, 1.0))):
                    act.wait_ge(proj_ps, i * 2 + n + 1)
                    a.activation(dst[:, 0, :], ps[:, PROJ + n, :], ACT.Copy, scale=scale).then_inc(qk_hi, 1)

                def value_hi(t):
                    act.wait_ge(gated, i * GATED + GATED + (t + 1) * VOPS)
                    a.activation(vhl[:, 0, t, :], vsum[:, t, :], ACT.Copy).then_inc(v_hi, 1)

                def exp(qt):
                    act.wait_ge(max_ready, i * NT + qt + 1)
                    a.activation(probs[:, qt % 2, :], ps[:, PROJ + qt % 2, :], ACT.Exp, bias=nmax[:, qt:qt + 1],
                                 accum_out=rowsum[:, qt:qt + 1]).then_inc(exp_ready, 1)

                def probs_hi(qt):
                    act.wait_ge(t_ps, i * NT + qt + 1)
                    a.activation(pT[:, 0, :, qt * P:(qt + 1) * P], ps[:, TR + qt % 2, :].rearrange("p (k q) -> p k q", q=P),
                                 ACT.Copy).then_inc(pt_hi, 1)

                value_hi(0)
                value_hi(1)
                exp(0)
                exp(1)
                probs_hi(0)
                exp(2)
                probs_hi(1)
                exp(3)
                value_hi(2)
                probs_hi(2)
                value_hi(3)
                probs_hi(3)
                for half in range(2):
                    act.wait_ge(ctx_ps, i * 2 + half + 1)
                    a.activation(cT[:, 0, half * HALF:(half + 1) * HALF], ps[:, CTX[half], 0:HALF], ACT.Copy).then_inc(ctx_hi, 1)
                act.wait_ge(go_ready, i + 1)
                for t in range(NT):
                    for pair in (1, 3):
                        c = NT * VCH + t * OCH + pair
                        act.wait_ge(chunk_ps, i * CHUNKS + c + 1)
                        for e in range(2):
                            k = pair // 2 * 2 + e
                            act.wait_ge(added, i * (NT * ADDS) + NT * ADDS + (t - 1) * ADDS + max(k, 1))
                            a.activation(weighted[:, k, :], ps[:, RING + c % NRING, e * D:(e + 1) * D], ACT.Copy,
                                         scale=go[:, t, 2 * pair + e:2 * pair + e + 1]).then_inc(scaled, 1)

            heads(act, iteration)

        @block.vector
        def _(dve):
            v = nc.vector
            dve.wait_ge(w_hi0, 1)
            v.tensor_tensor(out=whl[0][:, 1, :], in0=stage[:], in1=whl[0][:, 0, :].bitcast(F32), op=ALU.subtract).then_inc(w_split, 1)

            def iteration(parity, h, b, i):
                step = [0]

                def link(ins):
                    step[0] += 1
                    ins.then_inc(dve_step, 1)
                    dve.wait_ge(dve_step, i * DVE_STEPS + step[0])

                ops = [0]

                def count(ins):
                    ops[0] += 1
                    ins.then_inc(gated, 1)

                def wait_gated(back):
                    dve.wait_ge(gated, i * GATED + GATED + ops[0] - back)

                def weigh(c, out, gate, first, experts, width):
                    dve.wait_ge(chunk_ps, i * CHUNKS + c + 1)
                    for e in range(experts):
                        src = ps[:, RING + c % NRING, e * width:(e + 1) * width]
                        scale = gate[:, first + e:first + e + 1]
                        dst = out[:, e % 2, :]
                        if first + e < 2:
                            count(v.tensor_scalar(out=dst, in0=src, scalar1=scale, scalar2=None, op0=ALU.mult))
                        else:
                            wait_gated(1)
                            count(v.scalar_tensor_tensor(out=dst, in0=src, scalar=scale, in1=dst, op0=ALU.mult, op1=ALU.add))

                def values(t):
                    out = vacc[:, t % 2]
                    for c in range(VCH):
                        weigh(VCH * t + c, out, gs[:, 0, t, :], c * (E // VCH), E // VCH, FP)
                    wait_gated(0)
                    count(v.tensor_tensor(out=vsum[:, t, :], in0=out[:, 0, :], in1=out[:, 1, :], op=ALU.add))

                def value_lo(t):
                    dve.wait_ge(v_hi, i * NT + t + 1)
                    v.tensor_tensor(out=vhl[:, 1, t, :], in0=vsum[:, t, :], in1=vhl[:, 0, t, :].bitcast(F32), op=ALU.subtract).then_inc(v_lo, 1)

                def row_max(qt):
                    dve.wait_ge(s_ps, i * NT + qt + 1)
                    v.tensor_reduce(out=nmax[:, qt:qt + 1], in_=ps[:, PROJ + qt % 2, :], axis=AX.X, op=ALU.max,
                                    negate=True).then_inc(max_ready, 1)

                def probs_lo(qt):
                    dve.wait_ge(pt_hi, i * NT + qt + 1)
                    cols = slice(qt * P, (qt + 1) * P)
                    v.tensor_tensor(out=pT[:, 1, :, cols], in0=ps[:, TR + qt % 2, :].rearrange("p (k q) -> p k q", q=P),
                                    in1=pT[:, 0, :, cols].bitcast(F32), op=ALU.subtract).then_inc(pt_lo, 1)

                link(v.tensor_copy(gs[:].rearrange("p c t e -> p (c t e)"),
                                   gates[:, bass.ds(b, 1), bass.ds(h, 1)].rearrange("p o a c t e -> p (o a c t e)")))
                dve.wait_ge(qk_hi, i * 2 + 1)
                v.scalar_tensor_tensor(out=qhl[:, 1, :], in0=ps[:, PROJ, :], scalar=FFN_SCALE, in1=qhl[:, 0, :].bitcast(F32),
                                       op0=ALU.mult, op1=ALU.subtract).then_inc(qk_lo, 1)
                dve.wait_ge(qk_hi, i * 2 + 2)
                v.tensor_tensor(out=khl[:, 1, :], in0=ps[:, PROJ + 1, :], in1=khl[:, 0, :].bitcast(F32), op=ALU.subtract).then_inc(qk_lo, 1)
                values(0)
                values(1)
                row_max(0)
                row_max(1)
                value_lo(0)
                value_lo(1)
                values(2)
                probs_lo(0)
                row_max(2)
                probs_lo(1)
                row_max(3)
                values(3)
                value_lo(2)
                probs_lo(2)
                value_lo(3)
                probs_lo(3)
                dve.wait_ge(exp_ready, i * NT + NT)
                link(v.reciprocal(out=rinv[:], in_=rowsum[:]))
                v.tensor_tensor(out=go[:], in0=gs[:, 1], in1=rinv[:].unsqueeze(2).to_broadcast([P, NT, E]), op=ALU.mult).then_inc(go_ready, 1)
                for half in range(2):
                    cols = slice(half * HALF, (half + 1) * HALF)
                    dve.wait_ge(ctx_hi, i * 2 + half + 1)
                    v.tensor_tensor(out=cT[:, 1, cols], in0=ps[:, CTX[half], 0:HALF], in1=cT[:, 0, cols].bitcast(F32),
                                    op=ALU.subtract).then_inc(ctx_lo, 1)
                dve.wait_ge(go_ready, i + 1)
                for t in range(NT):
                    dve.wait_ge(added, i * (NT * ADDS) + (t + 1) * ADDS)
                    for pair in (0, 2):
                        weigh(NT * VCH + t * OCH + pair, part[:, t], go[:, t, :], 2 * pair, 2, D)
                    wait_gated(0)
                    count(v.tensor_tensor(out=part[:, t, 0, :], in0=part[:, t, 0, :], in1=part[:, t, 1, :], op=ALU.add))
                assert ops[0] == GATED
                assert step[0] == DVE_STEPS, step[0]

            heads(dve, iteration)

        @block.tensor
        def _(pe):
            mm = nc.tensor.matmul
            pe.sem_inc(gated, GATED)
            pe.sem_inc(scaled, SCALED)
            pe.wait_ge(ident_loaded, 16)

            def split_product(out, pairs):
                n = len(pairs) * len(TERMS)
                k = 0
                for stationary, moving in pairs:
                    for s, m in TERMS:
                        last = mm(out, stationary(s), moving(m), start=(k == 0), stop=(k == n - 1))
                        k += 1
                return last

            def iteration(parity, h, b, i):
                w = whl[parity]

                def weight(s, first, width):
                    return w[:, s, first:first + width]

                pe.wait_ge(w_split, h * B + 1)
                pe.wait_ge(x_loaded, i * 16 + 16)
                for n in range(2):
                    split_product(ps[:, PROJ + n, :],
                                  [(lambda s, k=k: weight(s, n * QW + k * FP, FP), lambda m, k=k: xhl[:, m, k, :])
                                   for k in range(DK)]).then_inc(proj_ps, 1)

                def ring_free(c):
                    was, ago = (c - NRING, 0) if c >= NRING else (c - NRING + CHUNKS, 1)
                    out = was - NT * VCH
                    if out < 0:
                        t, c = divmod(was, VCH)
                        pe.wait_ge(gated, (i + 1 - ago) * GATED + t * VOPS + (c + 1) * (E // VCH))
                    elif out % 2:
                        pe.wait_ge(scaled, (i + 1 - ago) * SCALED + out // 2 * 2 + 2)
                    else:
                        t, pair = divmod(out, OCH)
                        pe.wait_ge(gated, (i + 1 - ago) * GATED + NT * VOPS + t * OOPS + pair + 2)

                def values(t):
                    for half in range(2):
                        c = 2 * t + half
                        ring_free(c)
                        split_product(ps[:, RING + c % NRING, :],
                                      [(lambda s, k=k: xhl[:, s, k, t * P:(t + 1) * P],
                                        lambda m, k=k: weight(m, 2 * QW + k * E * FP + half * BANK, BANK))
                                       for k in range(DK)]).then_inc(chunk_ps, 1)

                def scores(qt):
                    if qt >= 2:
                        pe.wait_ge(exp_ready, i * NT + qt - 1)
                    split_product(ps[:, PROJ + qt % 2, :],
                                  [(lambda s: qhl[:, s, qt * P:(qt + 1) * P], lambda m: khl[:, m, :])]).then_inc(s_ps, 1)

                def transposes(qt):
                    pe.wait_ge(exp_ready, i * NT + qt + 1)
                    if qt >= 2:
                        pe.wait_ge(pt_lo, i * NT + qt - 1)
                    for k in range(NT):
                        last = nc.tensor.transpose(ps[:, TR + qt % 2, k * P:(k + 1) * P], probs[:, qt % 2, k * P:(k + 1) * P], ident[:])
                    last.then_inc(t_ps, 1)

                values(0)
                values(1)
                pe.wait_ge(qk_lo, i * 2 + 2)
                scores(0)
                scores(1)
                values(2)
                transposes(0)
                scores(2)
                transposes(1)
                scores(3)
                values(3)
                transposes(2)
                transposes(3)
                for half in range(2):
                    pe.wait_ge(pt_lo, i * NT + 2 * half + 2)
                    k = 0
                    for kt in range(NT):
                        if not half:
                            pe.wait_ge(v_lo, i * NT + kt + 1)
                        for st, m in TERMS:
                            last = mm(ps[:, CTX[half], 0:HALF], vhl[:, st, kt, :], pT[:, m, kt, half * HALF:(half + 1) * HALF],
                                      start=(k == 0), stop=(k == NT * len(TERMS) - 1))
                            k += 1
                    last.then_inc(ctx_ps, 1)
                for t in range(NT):
                    if t % 2 == 0:
                        pe.wait_ge(ctx_lo, i * 2 + t // 2 + 1)
                    for pair in range(E // 2):
                        c = 2 * NT + t * E // 2 + pair
                        ring_free(c)
                        split_product(ps[:, RING + c % NRING, :],
                                      [(lambda s: cT[:, s, t * P:(t + 1) * P],
                                        lambda m: weight(m, 2 * QW + VW + pair * BANK, BANK))]).then_inc(chunk_ps, 1)

            heads(pe, iteration)


def last_norm(nc, dram, kept):
    ctx = ExitStack()
    with ctx:
        acc = kept["acc"]
        stats = ctx.enter_context(nc.sbuf_tensor("statsC", [P, B, NT, 6], F32))
        mv = ctx.enter_context(nc.sbuf_tensor("mvC", [P, B, NT, 2], F32))
        ve = ctx.enter_context(nc.sbuf_tensor("veC", [P, B, NT], F32))
        rstd = ctx.enter_context(nc.sbuf_tensor("rstdC", [P, B, NT], F32))
        mhalf = ctx.enter_context(nc.sbuf_tensor("mhalfC", [P, NT], F32))
        stats_ready = ctx.enter_context(nc.semaphore("stats_readyC"))
        var_ready = ctx.enter_context(nc.semaphore("var_readyC"))
        pool_step = ctx.enter_context(nc.semaphore("pool_stepC"))
        rstd_ready = ctx.enter_context(nc.semaphore("rstd_readyC"))
        out_ready = ctx.enter_context(nc.semaphore("out_ready"))
        stored = ctx.enter_context(nc.semaphore("storedC"))
        block = ctx.enter_context(nc.Block())

        @block.vector
        def _(dve):
            v = nc.vector

            def normalise(b):
                dve.wait_ge(rstd_ready, b + 1)
                for t in range(NT):
                    last = v.tensor_scalar(out=acc[:, b, t, :], in0=acc[:, b, t, :], scalar1=mv[:, b, t, 0:1],
                                           scalar2=rstd[:, b, t:t + 1], op0=ALU.subtract, op1=ALU.mult)
                last.then_inc(out_ready, 1)

            for b in range(B):
                for t in range(NT):
                    last = v.bn_stats(out=stats[:, b, t, :], in_=acc[:, b, t, :])
                last.then_inc(stats_ready, 1)
                dve.wait_ge(stats_ready, b + 1)
                for t in range(NT):
                    last = v.bn_aggr(out=mv[:, b, t, :], in_=stats[:, b, t, :])
                last.then_inc(var_ready, 1)
                if b:
                    normalise(b - 1)
            normalise(B - 1)

        @block.gpsimd
        def _(pool):
            g = nc.gpsimd
            g.memset(mhalf[:], -0.5).then_inc(pool_step, 1)
            for b in range(B):
                pool.wait_ge(var_ready, b + 1)
                g.tensor_scalar(out=ve[:, b, :], in0=mv[:, b, :, 1], scalar1=LN_EPS, scalar2=None, op0=ALU.add).then_inc(pool_step, 1)
                pool.wait_ge(pool_step, b + 2)
                g.tensor_tensor(out=rstd[:, b, :], in0=ve[:, b, :], in1=mhalf[:], op=ALU.pow).then_inc(rstd_ready, 1)

        @block.sync
        def _(sp):
            for b in range(B):
                sp.wait_ge(out_ready, b + 1)
                sp.dma_start(dram["out"][b].rearrange("(t p) d -> p t d", p=P), acc[:, b]).then_inc(stored, 16)
            sp.wait_ge(stored, 16 * B)


def build(nc, dram):
    with nc.sbuf_tensor("acc", [P, B, NT, D], F32) as acc, nc.sbuf_tensor("gates", [P, B, FH, 2, NT, E], F32) as gates:
        kept = {"acc": acc, "gates": gates}
        layer0_and_layer1_attention(nc, dram, kept)
        routed_heads(nc, dram, kept)
        last_norm(nc, dram, kept)


def kernel(**inputs):
    import concourse.bacc as bacc
    from concourse.bass_utils import run_bass_kernel_spmd

    nc = bacc.Bacc("TRN2", target_bir_lowering=False, num_devices=1)
    arrays = {f"in_{name}": a for name, a in layouts(inputs).items()}
    dram = {name[3:]: nc.dram_tensor(name, a.shape, mybir.dt.from_np(a.dtype), kind="ExternalInput").ap()
            for name, a in arrays.items()}
    dram["xs"] = nc.dram_tensor("routed_input", [B, P, 2 * DK * T], F32, kind="Internal").ap()
    dram["out"] = nc.dram_tensor("out_0", [B, T, D], F32, kind="ExternalOutput").ap()
    build(nc, dram)
    return run_bass_kernel_spmd(nc, [arrays], core_ids=[0]).results[0]["out_0"]
```

```python
import concourse.bass as bass
from concourse import mybir
from contextlib import ExitStack

F32 = mybir.dt.float32
BF16 = mybir.dt.bfloat16
F32R = mybir.dt.float32r
ALU = mybir.AluOpType
ACT = mybir.ActivationFunctionType
AX = mybir.AxisListType

P = 128
B = 8
T = 512
NT = T // P
D = 256
DK = D // P
H = 16
HD = D // H
HP = 32
HG = P // HP
NG = H // HG
KV = 4
QKV = D + 2 * KV * HD
FH = 8
E = 8
FP = 128
SEL = FH * E
BANK = 512
LN_EPS = 1e-5
QK_EPS = 1e-6
MASKED = -1e30
ATT_SCALE = HD ** -0.5
FFN_SCALE = FP ** -0.5
UNITS = H * NT
TINY = 1e-30
LAG = 3
ACT_QT, DVE_QT = (0, 1, 2), (3,)
SLOTS = 6
HOLD1 = 3
HOLD = 2


def layer0_and_layer1_attention(nc, dram, kept):
    ctx = ExitStack()
    with ctx:
        def sb(name, shape, dt=F32):
            return ctx.enter_context(nc.sbuf_tensor(name, shape, dt))

        def sem(name):
            return ctx.enter_context(nc.semaphore(name))

        def in_turn(first, then):
            with ExitStack() as early:
                a = [early.enter_context(nc.sbuf_tensor(*x)) for x in first]
            return a, [sb(*x) for x in then]

        wq = sb("wq", [P, DK, NG * P])
        wk = sb("wk", [P, DK, NG * P])
        wv = sb("wv", [P, DK, D])
        wo = sb("wo", [P, DK, D])
        bq = sb("bq", [P, NG])
        bk = sb("bk", [P, NG])
        bv = sb("bv", [P, D])
        bo = sb("bo", [P, D])
        gamma = sb("gamma", [P, D])
        beta = sb("beta", [P, D])
        wt = sb("wt", [P, DK, D])
        tern = sb("tern", [P, DK, D])
        w1 = sb("w1", [P, DK, QKV])
        wp = sb("wp", [P, DK, D])
        wsel = sb("wsel", [P, DK, 2 * SEL])
        cos = sb("cos", [P, NT, HD])
        sin = sb("sin", [P, NT, HD])
        rank = sb("rank", [P, E])
        rscale = sb("rscale", [P, 1])
        ident = sb("ident", [P, P])
        identb = sb("identb", [P, P], BF16)
        cmask = sb("cmask", [P, P], BF16)
        keep = sb("keep", [P, 2 * P])
        ones = sb("ones", [P, P])
        tscale = sb("tscale", [P, 2])
        tsum = sb("tsum", [P, 2])
        mhalf = sb("mhalf", [P, NT])
        eps = sb("eps", [P, NT])
        pad = sb("pad", [P, 1])
        x_in = sb("x_in", [P, NT, D])
        tT = [sb(f"tT{i}", [P, DK, T]) for i in range(2)]
        (kT,), (o, z, x1, x2) = in_turn([("kT", [P, 2, NG, T], F32R)], [(n, [P, NT, D], F32) for n in ("o", "z", "x1", "x2")])
        (q1lo,), (probs,) = in_turn([("q1lo", [P, HG, T], F32R)], [("probs", [P, 4, T], F32)])
        (xhl,), (oTs,) = in_turn([("xhl", [P, 2, DK, T], F32R)], [("oTs", [P, NG, T], F32)])
        (xbeta,), (qkv,) = in_turn([("xbeta", [P, NT, D], F32)], [("qkv", [P, NT, QKV], F32)])
        (qst,), (qpad,) = in_turn([("qst", [P, NG, T], F32)], [("qpad", [P, NT, HG * P], F32)])
        (q1hi,), (qs,) = in_turn([("q1hi", [P, HG, T], F32R)], [("qs", [P, NG, T], F32)])
        alone = sb("alone", [P, 2 * HG, T], F32R)
        vaug = sb("vaug", [P, NT, H, HP])
        nmax = sb("nmax", [P, 8])
        pT = sb("pT", [P, SLOTS, NT, T])
        gw = sb("gw", [P, 4, NT * 2 * FH * E])
        rden = sb("rden", [P, NT, H])
        stats = sb("stats", [P, NT, 6])
        mv = sb("mv", [P, NT, 2])
        ve = sb("ve", [P, NT])
        rstd = sb("rstd", [P, NT])
        v1aug = sb("v1aug", [P, NT, KV, HP])
        kpad = sb("kpad", [P, NT, P])
        ss = sb("ss", [P, NT * (H + KV)])
        nrm = sb("nrm", [P, NT * (H + KV)])
        spare = sb("spare", [P, 2])
        est = sb("est", [P, NT * (H + KV)])
        rowsel = sb("rowsel", [P, 2])
        qf = pT[:, 0]
        sq = pT[:, 0, :, 0:(H + KV) * HD]
        rot = pT[:, 1, :, 0:(H + KV) * HD]
        qn = pT[:, 2, :, 0:(H + KV) * HD]
        p1T = [pT[:, i, k:k + 2, :].rearrange("p k q -> p (k q)") for i in (1, 2, 3, 4, 5, 0) for k in (0, 2)]
        m12 = sb("m12", [P, 4, NT * 2 * FH])

        ps = ctx.enter_context(nc.psum_tensor("psA", [P, 8, BANK], F32))
        TRB, OTB = (0, 1, 3), 2

        loaded = sem("loaded")
        const_v = sem("const_v")
        const_g = sem("const_g")
        const_p = sem("const_p")
        x_loaded = sem("x_loaded")
        x_free = sem("x_free")
        tr_ps = sem("tr_ps")
        tr_sb = sem("tr_sb")
        q_ps = sem("q_ps")
        k_ps = sem("k_ps")
        absum_ps = sem("absum_ps")
        v_ps = sem("v_ps")
        q_ready = sem("q_ready")
        k_ready = sem("k_ready")
        qf_ready = sem("qf_ready")
        qs_ready = sem("qs_ready")
        khi_ready = sem("khi_ready")
        alone_ready = sem("alone_ready")
        v_ready = sem("v_ready")
        s_ps = sem("s_ps")
        max_ready = sem("max_ready")
        exp_ready = sem("exp_ready")
        t_ps = sem("t_ps")
        pt_a = sem("pt_a")
        pt_v = sem("pt_v")
        ot_ps = sem("ot_ps")
        ot_ready = sem("ot_ready")
        on_ps = sem("on_ps")
        o_ready = sem("o_ready")
        y_ps = sem("y_ps")
        var_ready = sem("var_ready")
        rstd_ready = sem("rstd_ready")
        x_ready = sem("x_ready")
        z_ready = sem("z_ready")
        rden_ready = sem("rden_ready")
        qkv_ps = sem("qkv_ps")
        qkv_ready = sem("qkv_ready")
        ss_ready = sem("ss_ready")
        sq_ready = sem("sq_ready")
        turned = sem("turned")
        nrm_ready = sem("nrm_ready")
        rope_ready = sem("rope_ready")
        v1_ready = sem("v1_ready")
        qk1_ps = sem("qk1_ps")
        qk1_a = sem("qk1_a")
        qk1_v = sem("qk1_v")
        s1_ps = sem("s1_ps")
        exp1_ready = sem("exp1_ready")
        seen_ready = sem("seen_ready")
        av1_done = sem("av1_done")
        logit_ps = sem("logit_ps")
        gw_ready = sem("gw_ready")
        gate_step = sem("gate_step")
        gates_ready = sem("gates_ready")
        xhi_ready = sem("xhi_ready")
        xlo_ready = sem("xlo_ready")
        store_sem = sem("store_sem")
        stored = sem("stored")
        dve_step = sem("dve_step")
        pool_step = sem("pool_step")
        act_step = sem("act_step")
        DVE_STEPS = 11
        POOL_STEPS = 4

        block = ctx.enter_context(nc.Block())

        LOADS = [(wq[:], dram["wq"]), (wk[:], dram["wk"]), (wv[:], dram["wv"]), (wo[:], dram["wo"]),
                 (bq[:], dram["bq"]), (bk[:], dram["bk"]), (bv[:], dram["bv"].partition_broadcast(P)),
                 (bo[:], dram["bo"].partition_broadcast(P)), (gamma[:], dram["gamma"].partition_broadcast(P)),
                 (beta[:], dram["beta"].partition_broadcast(P)), (wt[:], dram["wt"]), (w1[:], dram["w1"]),
                 (wp[:], dram["wp"]), (wsel[:], dram["wsel"]), (cos[:], dram["cos"]), (sin[:], dram["sin"]),
                 (rank[:], dram["rank"].partition_broadcast(P)), (rowsel[:], dram["rowsel"]),
                 (rscale[:], dram["route_scale"].partition_broadcast(P)), (ident[:], dram["ident"])]

        @block.sync
        def _(sp):
            sp.dma_start(x_in[:], dram["x"][0].rearrange("(t p) d -> p t d", p=P)).then_inc(x_loaded, 16)
            for dst, src in LOADS:
                sp.dma_start(dst, src).then_inc(loaded, 16)
            sp.sem_inc(stored, 1)

            def store(b):
                sp.wait_ge(x_ready, b * 3 * NT + 3 * NT)
                sp.dma_start(dram["x3"][bass.ds(b, 1)].rearrange("o p n -> p (o n)"),
                             x1[:].rearrange("p t d -> p (t d)")).then_inc(store_sem, 16)
                sp.wait_ge(xhi_ready, b + 1)
                sp.wait_ge(xlo_ready, b + 1)
                sp.dma_start(dram["xs"][bass.ds(b, 1)].rearrange("o p n -> p (o n)"),
                             xhl[:].rearrange("p a k t -> p (a k t)").bitcast(F32)).then_inc(store_sem, 16)
                sp.wait_ge(store_sem, b * 32 + 32)
                sp.sem_inc(stored, 1)

            with sp.Fori(0, B - 1) as b:
                sp.wait_ge(x_free, b + 1)
                sp.dma_start(x_in[:], dram["x"][bass.ds(b + 1, 1)].rearrange("o (t p) d -> p (o t) d", p=P)).then_inc(x_loaded, 16)
                store(b)
            store(B - 1)

        def all_loaded(eng):
            eng.wait_ge(loaded, 16 * len(LOADS))

        g3 = [gw[:, i].rearrange("p (c e) -> p c e", e=E) for i in range(4)]
        wide = [P, NT * 2 * FH, E]
        GATE_PARTS = 19
        POOL_PARTS = (4, 10, 13, 14, 15)

        def gates(eng, b, part):
            v = nc.gpsimd if part in POOL_PARTS else nc.vector

            def largest(src, out):
                v.tensor_reduce(out=m12[:, out, :], in_=g3[src], axis=AX.X, op=ALU.max).then_inc(gate_step, 1)

            def where(src, value, out):
                v.tensor_tensor(out=g3[out], in0=g3[src], in1=m12[:, value, :].unsqueeze(2).to_broadcast(wide),
                                op=ALU.is_equal).then_inc(gate_step, 1)

            def ranked(n):
                v.tensor_tensor(out=g3[n], in0=g3[n], in1=rank[:].unsqueeze(1).to_broadcast(wide), op=ALU.mult).then_inc(gate_step, 1)

            if part == 0:
                eng.wait_ge(gw_ready, b + 1)
                v.tensor_scalar(out=gw[:, 1], in0=gw[:, 0], scalar1=1.0, scalar2=None, op0=ALU.add).then_inc(gate_step, 1)
                return
            eng.wait_ge(gate_step, b * GATE_PARTS + part)
            if part == 1:
                v.reciprocal(out=gw[:, 0], in_=gw[:, 1]).then_inc(gate_step, 1)
            elif part == 2:
                largest(0, 0)
            elif part == 3:
                where(0, 0, 1)
            elif part == 4:
                ranked(1)
            elif part == 5:
                largest(1, 3)
            elif part == 6:
                where(1, 3, 1)
            elif part == 7:
                v.scalar_tensor_tensor(out=gw[:, 2], in0=gw[:, 1], scalar=-2.0, in1=gw[:, 0], op0=ALU.mult,
                                       op1=ALU.add).then_inc(gate_step, 1)
            elif part == 8:
                largest(2, 1)
            elif part == 9:
                where(2, 1, 3)
            elif part == 10:
                ranked(3)
            elif part == 11:
                largest(3, 3)
            elif part == 12:
                where(3, 3, 3)
            elif part == 13:
                v.tensor_tensor(out=gw[:, 1], in0=gw[:, 1], in1=gw[:, 3], op=ALU.add).then_inc(gate_step, 1)
            elif part == 14:
                v.tensor_tensor(out=gw[:, 0], in0=gw[:, 0], in1=gw[:, 1], op=ALU.mult).then_inc(gate_step, 1)
            elif part == 15:
                v.tensor_tensor(out=m12[:, 2, :], in0=m12[:, 0, :], in1=m12[:, 1, :], op=ALU.add).then_inc(gate_step, 1)
            elif part == 16:
                v.tensor_scalar(out=m12[:, 2, :], in0=m12[:, 2, :], scalar1=1e-9, scalar2=None, op0=ALU.max).then_inc(gate_step, 1)
            elif part == 17:
                v.reciprocal(out=m12[:, 3, :], in_=m12[:, 2, :]).then_inc(gate_step, 1)
            elif part == 18:
                v.tensor_scalar(out=m12[:, 3, :], in0=m12[:, 3, :], scalar1=rscale[:, 0:1], scalar2=None,
                                op0=ALU.mult).then_inc(gate_step, 1)

        @block.gpsimd
        def _(pool):
            g = nc.gpsimd
            g.memset(mhalf[:], -0.5).then_inc(const_p, 1)
            g.memset(alone[:].bitcast(F32), 0.0).then_inc(const_g, 1)
            g.memset(eps[:], LN_EPS).then_inc(const_p, 1)
            g.memset(cmask[:], 0.0).then_inc(const_p, 1)
            g.memset(keep[:], 1.0).then_inc(const_p, 1)
            g.memset(gw[:], 0.0).then_inc(gw_ready, 1)
            pool.wait_ge(const_p, 4)
            g.affine_select(out=cmask[:], in_=cmask[:], compare_op=ALU.is_ge, fill=MASKED, base=0,
                            pattern=[[-1, P]], channel_multiplier=1).then_inc(const_g, 1)
            g.affine_select(out=keep[:], in_=keep[:], compare_op=ALU.is_ge, fill=0.0, base=0,
                            pattern=[[1, 2 * P]], channel_multiplier=-1).then_inc(const_p, 1)
            pool.wait_ge(const_p, 5)
            g.affine_select(out=keep[:], in_=keep[:], compare_op=ALU.is_ge, fill=0.0, base=P - 1,
                            pattern=[[-1, 2 * P]], channel_multiplier=1).then_inc(const_g, 1)
            all_loaded(pool)
            pool.wait_ge(const_g, 3)
            with pool.Fori(0, B) as b:
                step = [0]

                def link(ins):
                    step[0] += 1
                    ins.then_inc(pool_step, 1)
                    pool.wait_ge(pool_step, b * POOL_STEPS + step[0])

                pool.wait_ge(x_loaded, b * 16 + 16)
                pool.wait_ge(tr_ps, b * 12 + 2)
                g.tensor_tensor(out=xbeta[:], in0=x_in[:], in1=beta[:].unsqueeze(1).to_broadcast([P, NT, D]),
                                op=ALU.add).then_inc(x_free, 1)

                def root(n):
                    pool.wait_ge(var_ready, b * 4 + n)
                    link(g.tensor_tensor(out=ve[:], in0=mv[:, :, 1], in1=eps[:], op=ALU.add))
                    g.tensor_tensor(out=rstd[:], in0=ve[:], in1=mhalf[:, 0:NT], op=ALU.pow).then_inc(rstd_ready, 1)

                for G in range(NG):
                    pool.wait_ge(q_ready, b * NG + G + 1)
                    pool.wait_ge(qs_ready, b * NG + G + 1)
                    if G >= 2:
                        pool.wait_ge(alone_ready, b * H + G * HG)
                        gates(pool, b, POOL_PARTS[G - 2])
                        pool.wait_ge(s_ps, b * UNITS + (G - 1) * HG * NT)
                        pool.wait_ge(gate_step, b * GATE_PARTS + POOL_PARTS[G - 2] + 1)
                    elif G:
                        pool.wait_ge(alone_ready, b * H + G * HG)
                    else:
                        pool.wait_ge(x_free, b + 1)
                    for j in range(HG):
                        rows = slice(j * HP, (j + 1) * HP)
                        g.tensor_tensor(out=alone[rows, G % 2 * HG + j, :], in0=qst[rows, G, :], in1=qs[rows, G, :],
                                        op=ALU.add).then_inc(alone_ready, 1)
                pool.wait_ge(alone_ready, b * H + H)
                for part in POOL_PARTS[2:]:
                    gates(pool, b, part)
                pool.wait_ge(gate_step, b * GATE_PARTS + POOL_PARTS[-1] + 1)
                root(1)
                root(2)
                root(3)
                root(4)
                assert step[0] == POOL_STEPS
            for part in POOL_PARTS:
                gates(pool, B, part)

        @block.scalar
        def _(act):
            a = nc.scalar
            all_loaded(act)
            a.activation(identb[:], ident[:], ACT.Copy).then_inc(act_step, 1)
            with act.Fori(0, B) as b:
                def tt_evac(n):
                    act.wait_ge(tr_ps, b * 12 + 2 * n + 1)
                    a.activation(tT[n % 2][:, 0, :], ps[:, 0, :], ACT.Copy).then_inc(tr_sb, 1)

                tt_evac(0)
                for G in range(NG):
                    act.wait_ge(qf_ready, b * NG + G + 1)
                    a.activation(qs[:, G, :].bitcast(F32R), qf[:, G, :], ACT.Copy, scale=rowsel[:, 1:2]).then_inc(qs_ready, 1)
                act.wait_ge(stored, b + 1)
                for G in range(NG):
                    act.wait_ge(k_ps, b * NG + G + 1)
                    a.activation(kT[:, 0, G, :], ps[:, (6 + G) % 8, :], ACT.Identity, bias=bk[:, G:G + 1]).then_inc(khi_ready, 1)
                for u in range(UNITS + LAG):
                    if u < UNITS:
                        n = (u % NT + 1) * P
                        act.wait_ge(max_ready, b * UNITS + u + 1)
                        a.activation(probs[:, u % 4, 0:n], ps[:, 4 + u % 4, 0:n], ACT.Exp,
                                     bias=nmax[:, u % 8:u % 8 + 1]).then_inc(exp_ready, 1)
                    w = u - LAG
                    if w >= 0 and w % NT in ACT_QT:
                        h, qt = divmod(w, NT)
                        act.wait_ge(t_ps, b * UNITS + w + 1)
                        if h >= SLOTS and qt == ACT_QT[0]:
                            act.wait_ge(ot_ps, b * NG + (h - SLOTS) // HG + 1)
                        a.activation(pT[:, h % SLOTS, 0:qt + 1, qt * P:(qt + 1) * P],
                                     ps[:, TRB[w % len(TRB)], 0:(qt + 1) * P].rearrange("p (k q) -> p k q", q=P), ACT.Copy).then_inc(pt_a, 1)
                tt_evac(1)
                tt_evac(2)
                tt_evac(3)
                a.activation(spare[:, 0:1], ones[:, 0:1], ACT.Sqrt)
                for t in range(NT):
                    act.wait_ge(qkv_ps, b * NT + t + 1)
                    a.activation(qkv[:, t, :], ps[:, 4 + t, 0:QKV], ACT.Copy).then_inc(qkv_ready, 1)
                    a.activation(sq[:, t, :], ps[:, 4 + t, 0:D + KV * HD], ACT.Square).then_inc(sq_ready, 1)
                act.wait_ge(ss_ready, b * NT + NT)
                a.activation(nrm[:], ss[:], ACT.Sqrt).then_inc(nrm_ready, 1)
                a.activation(spare[:, 1:2], ones[:, 0:1], ACT.Exp)
                act.wait_ge(qkv_ready, b * NT + NT)
                for t in range(NT):
                    a.activation(v1aug[:, t, :, 0:HD], qkv[:, t, D + KV * HD:QKV].rearrange("p (g d) -> p g d", g=KV),
                                 ACT.Copy).then_inc(v1_ready, 1)
                for j in range(HG):
                    act.wait_ge(qk1_ps, b * 5 + j + 1)
                    a.activation(q1hi[:, j, :], ps[:, j, :], ACT.Copy).then_inc(qk1_a, 1)
                act.wait_ge(qk1_ps, b * 5 + 5)
                for g in range(KV):
                    rows = slice(g * HP, (g + 1) * HP)
                    a.activation(alone[rows, g, :], ps[rows, 4, :], ACT.Copy).then_inc(qk1_a, 1)
                for w in range(KV * NT):
                    kt = w // KV
                    act.wait_ge(s1_ps, b * KV * NT + w + 1)
                    if w >= len(p1T):
                        act.wait_ge(av1_done, b * NT + (w - len(p1T)) // KV + 1)
                    bank = 6 - 2 * (w % 2)
                    n = 1024 if kt < NT - 1 else BANK
                    src = ps[:, bank:bank + 2, :].rearrange("p a n -> p (a n)") if n == 1024 else ps[:, bank, :]
                    a.activation(p1T[w % len(p1T)][:, 0:n], src, ACT.Exp, scale=ATT_SCALE).then_inc(exp1_ready, 1)
                for c in range(1, NG, 2):
                    act.wait_ge(av1_done, b * NT + NT)
                    a.activation(oTs[:, c, :], ps[:, c, :], ACT.Copy).then_inc(ot_ready, 1)
                tt_evac(4)
                tt_evac(5)
                act.wait_ge(tr_sb, b * 12 + 12)
                act.wait_ge(stored, b + 1)
                a.activation(xhl[:, 0], tT[1][:], ACT.Copy).then_inc(xhi_ready, 1)
                act.wait_ge(logit_ps, b + 1)
                act.wait_ge(gates_ready, b + 1)
                a.activation(gw[:, 0], ps[:, 6, :], ACT.Exp, scale=-1.0).then_inc(gw_ready, 1)

        @block.vector
        def _(dve):
            v = nc.vector
            v.memset(vaug[:], 0.0).then_inc(const_v, 1)
            v.memset(v1aug[:], 0.0).then_inc(const_v, 1)
            v.memset(kpad[:], 0.0).then_inc(const_v, 1)
            v.memset(ones[:], 1.0).then_inc(const_v, 1)
            dve.wait_ge(const_v, 4)
            v.memset(vaug[:, :, :, HD:HD + 1], 1.0).then_inc(const_v, 1)
            v.memset(v1aug[:, :, :, HD:HD + 1], 1.0).then_inc(const_v, 1)
            all_loaded(dve)
            v.tensor_reduce(out=tsum[:, 0:1], in_=wt[:].rearrange("p k n -> p (k n)"), axis=AX.X, op=ALU.add,
                            apply_absolute_value=True).then_inc(const_v, 1)
            dve.wait_ge(absum_ps, 1)
            v.tensor_scalar(out=tscale[:, 1:2], in0=ps[:, 7, 0:1], scalar1=1.0 / (D * D), scalar2=LN_EPS,
                            op0=ALU.mult, op1=ALU.max).then_inc(const_v, 1)
            dve.wait_ge(const_v, 8)
            v.tensor_scalar(out=tscale[:, 0:1], in0=tscale[:, 1:2], scalar1=0.5, scalar2=None, op0=ALU.mult).then_inc(const_v, 1)
            v.tensor_scalar(out=tsum[:, 1:2], in0=tscale[:, 1:2], scalar1=-0.5, scalar2=None, op0=ALU.mult).then_inc(const_v, 1)
            dve.wait_ge(const_v, 10)
            v.tensor_scalar(out=tern[:], in0=wt[:], scalar1=tsum[:, 1:2], scalar2=None, op0=ALU.is_lt).then_inc(const_v, 1)
            dve.wait_ge(const_v, 11)
            v.scalar_tensor_tensor(out=tern[:], in0=wt[:], scalar=tscale[:, 0:1], in1=tern[:], op0=ALU.is_gt,
                                   op1=ALU.subtract).then_inc(const_v, 1)

            def gates_end(b, batch):
                dve.wait_ge(gate_step, (b + 1) * GATE_PARTS)
                for t in range(NT):
                    n = 2 * FH
                    last = v.tensor_tensor(out=kept["gates"][:, bass.ds(batch, 1), :, :, t, :].rearrange("p o h c e -> p c (o h) e"),
                                           in0=gw[:, 0, t * n * E:(t + 1) * n * E].rearrange("p (c h e) -> p c h e", c=2, e=E),
                                           in1=m12[:, 3, t * n:(t + 1) * n].rearrange("p (c h) -> p c h", c=2).unsqueeze(3).to_broadcast([P, 2, FH, E]),
                                           op=ALU.mult)
                last.then_inc(gates_ready, 1)

            with dve.Fori(0, B) as b:
                step = [0]

                def link(ins):
                    step[0] += 1
                    ins.then_inc(dve_step, 1)
                    dve.wait_ge(dve_step, b * DVE_STEPS + step[0])

                def tt_evac(n):
                    dve.wait_ge(tr_ps, b * 12 + 2 * n + 2)
                    v.tensor_copy(tT[n % 2][:, 1, :], ps[:, 1, :]).then_inc(tr_sb, 1)

                def variances(n, make):
                    for t in range(NT + 1):
                        if t < NT:
                            make(t).then_inc(z_ready, 1)
                        if t:
                            dve.wait_ge(z_ready, b * 4 * NT + (n - 1) * NT + t)
                            last = v.bn_stats(out=stats[:, t - 1, :], in_=z[:, t - 1, :])
                    link(last)
                    v.memset(pad[:], 0.0)
                    for t in range(NT):
                        last = v.bn_aggr(out=mv[:, t, :], in_=stats[:, t, :])
                    last.then_inc(var_ready, 1)

                def normalise(n, out):
                    dve.wait_ge(rstd_ready, b * 4 + n)
                    for t in range(NT):
                        v.tensor_scalar(out=out[:, t, :], in0=z[:, t, :], scalar1=mv[:, t, 0:1], scalar2=rstd[:, t:t + 1],
                                        op0=ALU.subtract, op1=ALU.mult).then_inc(x_ready, 1)

                def width_ps(k, t):
                    dve.wait_ge(y_ps, b * 3 * NT + k * NT + t + 1)
                    return ps[:, 2 + t, 0:D]

                tt_evac(0)
                def query_parts(G):
                    dve.wait_ge(qf_ready, b * NG + G + 1)
                    v.tensor_scalar(out=qst[:, G, :], in0=qf[:, G, :], scalar1=rowsel[:, 0:1], scalar2=None,
                                    op0=ALU.mult).then_inc(q_ready, 1)

                for G in range(NG):
                    dve.wait_ge(q_ps, b * NG + G + 1)
                    v.tensor_scalar(out=qf[:, G, :], in0=ps[:, 2 + G, :], scalar1=bq[:, G:G + 1], scalar2=ATT_SCALE,
                                    op0=ALU.add, op1=ALU.mult).then_inc(qf_ready, 1)
                    if G:
                        query_parts(G - 1)
                query_parts(NG - 1)
                for G in range(NG):
                    dve.wait_ge(khi_ready, b * NG + G + 1)
                    v.scalar_tensor_tensor(out=kT[:, 1, G, :], in0=ps[:, (6 + G) % 8, :], scalar=bk[:, G:G + 1],
                                           in1=kT[:, 0, G, :].bitcast(F32), op0=ALU.add, op1=ALU.subtract).then_inc(k_ready, 1)
                dve.wait_ge(stored, b + 1)
                for i in range(2):
                    dve.wait_ge(v_ps, b * 2 + i + 1)
                    for t in range(2):
                        last = v.tensor_tensor(out=vaug[:, 2 * i + t, :, 0:HD],
                                        in0=ps[:, 2 + i, t * D:(t + 1) * D].rearrange("p (h d) -> p h d", h=H),
                                        in1=bv[:].rearrange("p (h d) -> p h d", h=H), op=ALU.add)
                    last.then_inc(v_ready, 1)
                for u in range(UNITS + LAG):
                    if u % 3 == 2 and u // 3 < GATE_PARTS and u // 3 not in POOL_PARTS:
                        gates(dve, b, u // 3)
                    if u < UNITS:
                        n = (u % NT + 1) * P
                        dve.wait_ge(s_ps, b * UNITS + u + 1)
                        if u >= 8:
                            dve.wait_ge(exp_ready, b * UNITS + u - 7)
                        v.tensor_reduce(out=nmax[:, u % 8:u % 8 + 1], in_=ps[:, 4 + u % 4, 0:n], axis=AX.X, op=ALU.max,
                                        negate=True).then_inc(max_ready, 1)
                    w = u - LAG
                    if w >= 0 and w % NT in DVE_QT:
                        h, qt = divmod(w, NT)
                        dve.wait_ge(t_ps, b * UNITS + w + 1)
                        if h >= SLOTS and qt == DVE_QT[0]:
                            dve.wait_ge(ot_ps, b * NG + (h - SLOTS) // HG + 1)
                        v.tensor_copy(pT[:, h % SLOTS, 0:qt + 1, qt * P:(qt + 1) * P],
                                      ps[:, TRB[w % len(TRB)], 0:(qt + 1) * P].rearrange("p (k q) -> p k q", q=P)).then_inc(pt_v, 1)
                    if w >= NT * HG and w % (NT * HG) == HOLD + 2:
                        G = w // (NT * HG) - 1
                        dve.wait_ge(ot_ps, b * NG + G + 1)
                        v.tensor_copy(oTs[:, G, :], ps[:, OTB, :]).then_inc(ot_ready, 1)
                gates_end(b, (b + B - 1) % B)
                dve.wait_ge(ot_ps, b * NG + NG)
                v.tensor_copy(oTs[:, NG - 1, :], ps[:, OTB, :]).then_inc(ot_ready, 1)

                def normalised(layer):
                    for t in range(NT + 1):
                        if t < NT:
                            dve.wait_ge(on_ps, b * 2 * NT + layer * NT + t + 1)
                            heads = ps[:, 4 + t, :].rearrange("p (c a d) -> p c a d", c=NG, a=HG)
                            v.reciprocal(out=rden[:, t, :].rearrange("p (c a) -> p c a", c=NG), in_=heads[:, :, :, HD]).then_inc(rden_ready, 1)
                        if t:
                            w = t - 1
                            dve.wait_ge(rden_ready, b * 2 * NT + layer * NT + t)
                            dst = o[:, w, :].rearrange("p (c a d) -> p c a d", c=NG, a=HG) if layer == 0 else \
                                o[:, w, :].rearrange("p (a c d) -> p c a d", c=NG, a=HG)
                            scale = rden[:, w, :].rearrange("p (c a) -> p c a", c=NG).unsqueeze(3).to_broadcast([P, NG, HG, HD])
                            v.tensor_tensor(out=dst, in0=ps[:, 4 + w, :].rearrange("p (c a d) -> p c a d", c=NG, a=HG)[:, :, :, 0:HD],
                                            in1=scale, op=ALU.mult).then_inc(o_ready, 1)

                normalised(0)
                tt_evac(1)
                variances(1, lambda t: v.tensor_tensor(out=z[:, t, :], in0=width_ps(0, t), in1=bo[:], op=ALU.add))
                dve.wait_ge(var_ready, b * 4 + 1)
                for t in range(NT):
                    last = v.scalar_tensor_tensor(out=z[:, t, :], in0=z[:, t, :], scalar=mv[:, t, 0:1], in1=gamma[:],
                                                  op0=ALU.subtract, op1=ALU.mult)
                link(last)
                dve.wait_ge(rstd_ready, b * 4 + 1)
                dve.wait_ge(x_free, b + 1)
                variances(2, lambda t: v.scalar_tensor_tensor(out=z[:, t, :], in0=z[:, t, :], scalar=rstd[:, t:t + 1],
                                                                 in1=xbeta[:, t, :], op0=ALU.mult, op1=ALU.add))
                normalise(2, x1)
                tt_evac(2)
                dve.wait_ge(x_ready, b * 3 * NT + NT)
                variances(3, lambda t: v.scalar_tensor_tensor(out=z[:, t, :], in0=width_ps(1, t), scalar=tscale[:, 1:2],
                                                                 in1=x1[:, t, :], op0=ALU.mult, op1=ALU.add))
                normalise(3, x2)
                tt_evac(3)
                heads = H + KV
                half = HD // 2
                QK = D + KV * HD
                roth = rot.rearrange("p t (h d) -> p t h d", d=HD)
                qnh = qn.rearrange("p t (h d) -> p t h d", d=HD)
                for t in range(NT):
                    qk = qkv[:, t, 0:QK].rearrange("p (h d) -> p h d", d=HD)
                    dve.wait_ge(qkv_ready, b * NT + t + 1)
                    v.tensor_tensor(out=roth[:, t, :, 0:half], in0=qk[:, :, half:HD],
                                    in1=sin[:, t, 0:half].unsqueeze(1).to_broadcast([P, heads, half]), op=ALU.mult)
                    v.tensor_tensor(out=roth[:, t, :, half:HD], in0=qk[:, :, 0:half],
                                    in1=sin[:, t, half:HD].unsqueeze(1).to_broadcast([P, heads, half]), op=ALU.mult)
                    v.tensor_tensor(out=qnh[:, t], in0=qk,
                                    in1=cos[:, t, :].unsqueeze(1).to_broadcast([P, heads, HD]), op=ALU.mult).then_inc(turned, 1)
                    dve.wait_ge(sq_ready, b * NT + t + 1)
                    v.tensor_reduce(out=ss[:, t * heads:(t + 1) * heads], in_=sq[:, t, :].rearrange("p (h d) -> p h d", d=HD),
                                    axis=AX.X, op=ALU.add).then_inc(ss_ready, 1)
                    dve.wait_ge(turned, b * NT + t + 1)
                    last = v.tensor_tensor(out=qn[:, t, :], in0=qn[:, t, :], in1=rot[:, t, :], op=ALU.add)
                dve.wait_ge(nrm_ready, b + 1)
                link(v.tensor_scalar(out=nrm[:], in0=nrm[:], scalar1=TINY, scalar2=None, op0=ALU.max))
                link(v.reciprocal(out=est[:], in_=nrm[:]))
                link(v.tensor_tensor(out=est[:], in0=est[:], in1=ss[:], op=ALU.mult))
                link(v.tensor_tensor(out=est[:], in0=est[:], in1=nrm[:], op=ALU.add))
                link(v.tensor_scalar(out=nrm[:], in0=est[:], scalar1=0.5, scalar2=QK_EPS, op0=ALU.mult, op1=ALU.add))
                link(v.reciprocal(out=est[:], in_=nrm[:]))
                for t in range(NT):
                    over = est[:, t * heads:(t + 1) * heads]
                    v.tensor_tensor(out=qpad[:, t, :].rearrange("p (j g d) -> p j g d", j=HG, g=KV)[:, :, :, 0:HD],
                                    in0=qn[:, t, 0:D].rearrange("p (g j d) -> p j g d", g=KV, j=HG),
                                    in1=over[:, 0:H].rearrange("p (g j) -> p j g", g=KV).unsqueeze(3).to_broadcast([P, HG, KV, HD]),
                                    op=ALU.mult)
                    last = v.tensor_tensor(out=kpad[:, t, :].rearrange("p (g d) -> p g d", g=KV)[:, :, 0:HD],
                                           in0=qn[:, t, D:QK].rearrange("p (g d) -> p g d", g=KV),
                                           in1=over[:, H:heads].unsqueeze(2).to_broadcast([P, KV, HD]), op=ALU.mult)
                last.then_inc(rope_ready, 1)
                for j in range(HG):
                    dve.wait_ge(qk1_a, b * 8 + j + 1)
                    v.tensor_tensor(out=q1lo[:, j, :], in0=ps[:, j, :], in1=q1hi[:, j, :].bitcast(F32), op=ALU.subtract).then_inc(qk1_v, 1)
                for g in range(KV):
                    rows = slice(g * HP, (g + 1) * HP)
                    dve.wait_ge(qk1_a, b * 8 + 4 + g + 1)
                    v.tensor_tensor(out=alone[rows, KV + g, :], in0=ps[rows, 4, :], in1=alone[rows, g, :].bitcast(F32),
                                    op=ALU.subtract).then_inc(qk1_v, 1)
                for w in range(KV * NT):
                    nq = 2 * P if w < KV * (NT - 1) else P
                    seen = p1T[w % len(p1T)][:, 0:HG * nq].rearrange("p (j q) -> p j q", q=nq)
                    dve.wait_ge(exp1_ready, b * KV * NT + w + 1)
                    v.tensor_tensor(out=seen, in0=seen, in1=keep[:, 0:nq].unsqueeze(1).to_broadcast([P, HG, nq]),
                                    op=ALU.mult).then_inc(seen_ready, 1)
                for c in range(0, NG, 2):
                    dve.wait_ge(av1_done, b * NT + NT)
                    v.tensor_copy(oTs[:, c, :], ps[:, c, :]).then_inc(ot_ready, 1)
                normalised(1)
                tt_evac(4)
                variances(4, lambda t: v.tensor_tensor(out=z[:, t, :], in0=width_ps(2, t), in1=x2[:, t, :], op=ALU.add))
                normalise(4, x1)
                tt_evac(5)
                dve.wait_ge(xhi_ready, b + 1)
                v.tensor_tensor(out=xhl[:, 1], in0=tT[1][:], in1=xhl[:, 0].bitcast(F32), op=ALU.subtract).then_inc(xlo_ready, 1)
                assert step[0] == DVE_STEPS, step[0]
            for part in range(GATE_PARTS):
                if part not in POOL_PARTS:
                    gates(dve, B, part)
            gates_end(B, B - 1)

        @block.tensor
        def _(pe):
            mm = nc.tensor.matmul
            all_loaded(pe)
            pe.wait_ge(const_v, 7)
            mm(ps[:, 7, 0:1], ones[:], tsum[:, 0:1], start=True, stop=True).then_inc(absum_ps, 1)
            pe.wait_ge(const_v, 12)
            pe.wait_ge(const_g, 3)
            pe.wait_ge(act_step, 1)
            with pe.Fori(0, B) as b:
                def transposition(n, src, per_tile=None):
                    for k in range(DK):
                        for t in range(NT):
                            if per_tile:
                                per_tile(t)
                            last = nc.tensor.transpose(ps[:, k, t * P:(t + 1) * P], src[:, t, k * P:(k + 1) * P], ident[:])
                        last.then_inc(tr_ps, 1)

                def project(n, out, rhs, width, t, done=None):
                    for k in range(DK):
                        last = mm(out, tT[n % 2][:, k, t * P:(t + 1) * P], rhs[:, k, 0:width], start=(k == 0), stop=(k == DK - 1))
                    if done is not None:
                        last.then_inc(done, 1)

                pe.wait_ge(x_loaded, b * 16 + 16)
                transposition(0, x_in)
                pe.wait_ge(tr_sb, b * 12 + 2)
                pe.wait_ge(gw_ready, b + 1)
                for w, first, done in ((wq, 2, q_ps), (wk, 6, k_ps)):
                    for G in range(NG):
                        for k in range(DK):
                            last = mm(ps[:, (first + G) % 8, :], w[:, k, G * P:(G + 1) * P], tT[0][:, k, :],
                                      start=(k == 0), stop=(k == DK - 1))
                        last.then_inc(done, 1)
                for i in range(2):
                    pe.wait_ge(qf_ready, b * NG + i + 1)
                    for t in range(2):
                        project(0, ps[:, 2 + i, t * D:(t + 1) * D], wv, D, 2 * i + t, v_ps if t else None)
                pe.wait_ge(k_ready, b * NG + NG)
                pe.wait_ge(v_ready, b * 2 + 2)

                def weighted(G):
                    pe.wait_ge(pt_a, b * len(ACT_QT) * H + len(ACT_QT) * HG * (G + 1))
                    pe.wait_ge(pt_v, b * len(DVE_QT) * H + len(DVE_QT) * HG * (G + 1))
                    if G:
                        pe.wait_ge(ot_ready, b * 2 * NG + G)
                    for kt in range(NT):
                        for j in range(HG):
                            last = mm(ps[j * HP:(j + 1) * HP, OTB, kt * P:T], vaug[:, kt, G * HG + j, :],
                                      pT[:, (G * HG + j) % SLOTS, kt, kt * P:T], start=(kt == 0), stop=(kt == NT - 1), skip_group_check=True)
                    last.then_inc(ot_ps, 1)

                for u in range(UNITS + LAG):
                    if u < UNITS:
                        h, qt = divmod(u, NT)
                        G, j = divmod(h, HG)
                        if u >= 4:
                            pe.wait_ge(exp_ready, b * UNITS + u - 3)
                        if j == 0 and qt == 0:
                            pe.wait_ge(alone_ready, b * H + (G + 1) * HG)
                        bank = ps[:, 4 + u % 4, :]
                        n = max(qt + 1, 2) * P
                        for part in range(2):
                            mm(bank[:, 0:n], alone[:, G % 2 * HG + j, qt * P:(qt + 1) * P], kT[:, part, G, 0:n],
                               start=(part == 0), stop=False)
                        mm(bank[:, qt * P:(qt + 1) * P], identb[:], cmask[:], start=False, stop=True).then_inc(s_ps, 1)
                    w = u - LAG
                    if w >= 0:
                        qt = w % NT
                        pe.wait_ge(exp_ready, b * UNITS + w + 1)
                        if w >= len(TRB):
                            was_h, was_qt = divmod(w - len(TRB), NT)
                            done, tiles = (pt_v, DVE_QT) if was_qt in DVE_QT else (pt_a, ACT_QT)
                            pe.wait_ge(done, b * len(tiles) * H + was_h * len(tiles) + tiles.index(was_qt) + 1)
                        for k in range(qt + 1):
                            last = nc.tensor.transpose(ps[:, TRB[w % len(TRB)], k * P:(k + 1) * P], probs[:, w % 4, k * P:(k + 1) * P], ident[:])
                        last.then_inc(t_ps, 1)
                        if w >= NT * HG and w % (NT * HG) == HOLD - 1:
                            weighted(w // (NT * HG) - 1)
                weighted(NG - 1)

                def back(layer):
                    pe.wait_ge(ot_ready, b * 2 * NG + layer * NG + NG)
                    for t in range(NT):
                        for c in range(NG):
                            last = nc.tensor.transpose(ps[:, 4 + t, c * P:(c + 1) * P], oTs[:, c, t * P:(t + 1) * P], ident[:])
                        last.then_inc(on_ps, 1)

                def to_width(n, rhs):
                    pe.wait_ge(tr_sb, b * 12 + 2 * n + 2)
                    for t in range(NT):
                        project(n, ps[:, 2 + t, 0:D], rhs, D, t, y_ps)

                back(0)
                transposition(1, o, lambda t: pe.wait_ge(o_ready, b * 2 * NT + t + 1))
                to_width(1, wo)
                transposition(2, x1, lambda t: pe.wait_ge(x_ready, b * 3 * NT + t + 1))
                to_width(2, tern)
                transposition(3, x2, lambda t: pe.wait_ge(x_ready, b * 3 * NT + NT + t + 1))
                pe.wait_ge(tr_sb, b * 12 + 8)
                for t in range(NT):
                    project(3, ps[:, 4 + t, 0:QKV], w1, QKV, t, qkv_ps)
                pe.wait_ge(rope_ready, b + 1)
                pe.wait_ge(tr_sb, b * 12 + 8)
                pe.wait_ge(qkv_ready, b * NT + NT)
                for j in range(HG):
                    for t in range(NT):
                        last = nc.tensor.transpose(ps[:, j, t * P:(t + 1) * P], qpad[:, t, j * P:(j + 1) * P], ident[:])
                    last.then_inc(qk1_ps, 1)
                for t in range(NT):
                    last = nc.tensor.transpose(ps[:, 4, t * P:(t + 1) * P], kpad[:, t, :], ident[:])
                last.then_inc(qk1_ps, 1)
                pe.wait_ge(qk1_a, b * 8 + HG + 1)
                pe.wait_ge(qk1_v, b * 8 + HG + 1)
                pe.wait_ge(v1_ready, b * NT + NT)

                def weighted1(kt):
                    pe.wait_ge(seen_ready, b * KV * NT + (kt + 1) * KV)
                    nq = 2 * P if kt < NT - 1 else P
                    for j in range(HG):
                        for g in range(KV):
                            last = mm(ps[g * HP:(g + 1) * HP, j, kt * P:kt * P + nq], v1aug[:, kt, g, :],
                                      p1T[(kt * KV + g) % len(p1T)][:, j * nq:(j + 1) * nq],
                                      start=(kt == 0), stop=(kt == NT - 1), skip_group_check=True)
                    last.then_inc(av1_done, 1)

                for w in range(KV * NT + HOLD1 + 1):
                    if w < KV * NT:
                        kt, g = divmod(w, KV)
                        if w == 1:
                            pe.wait_ge(qk1_a, b * 8 + HG + KV)
                            pe.wait_ge(qk1_v, b * 8 + HG + KV)
                        if w >= 2:
                            pe.wait_ge(exp1_ready, b * KV * NT + w - 1)
                        bank = 6 - 2 * (w % 2)
                        for i in range(2 if kt < NT - 1 else 1):
                            hs = slice(2 * i, 2 * i + 2) if kt < NT - 1 else slice(0, HG)
                            qs_ = slice(kt * P, min((kt + 2) * P, T))
                            for k, (keys, queries) in enumerate(((0, q1hi), (0, q1lo), (1, q1hi))):
                                last = mm(ps[:, bank + i, :], alone[:, keys * KV + g, kt * P:(kt + 1) * P], queries[:, hs, qs_],
                                          start=(k == 0), stop=(k == 2))
                        last.then_inc(s1_ps, 1)
                    if w >= KV + HOLD1 and (w - HOLD1) % KV == 0:
                        weighted1((w - HOLD1) // KV - 1)

                back(1)
                transposition(4, o, lambda t: pe.wait_ge(o_ready, b * 2 * NT + NT + t + 1))
                to_width(4, wp)
                transposition(5, x1, lambda t: pe.wait_ge(x_ready, b * 3 * NT + 2 * NT + t + 1))
                pe.wait_ge(tr_sb, b * 12 + 12)
                for t in range(NT):
                    project(5, ps[:, 6, t * P:(t + 1) * P], wsel, 2 * SEL, t, logit_ps if t == NT - 1 else None)


def layouts(inputs):
    import numpy as np

    def rows(w):
        return np.ascontiguousarray(w.reshape(-1, P, w.shape[1]).transpose(1, 0, 2))

    def twice(w):
        return np.repeat(w.reshape(-1, H, 1, HD), 2, 2).reshape(-1, H * HP)

    i = {k: np.asarray(v) for k, v in inputs.items()}
    f = np.float32
    theta = 1.0 / 10000.0 ** (np.arange(0, HD, 2, dtype=f) / HD)
    freqs = np.outer(np.arange(T, dtype=f), theta).astype(f)
    cos = np.concatenate([np.cos(freqs)] * 2, 1).astype(f)
    sin = np.concatenate([-np.sin(freqs), np.sin(freqs)], 1).astype(f)
    table = lambda x: np.ascontiguousarray(x.reshape(NT, P, HD).transpose(1, 0, 2))
    return {
        "x": i["L0_attn_x"],
        "wq": rows(twice(i["L0_attn_Wq"])), "wk": rows(twice(i["L0_attn_Wk"])),
        "wv": rows(i["L0_attn_Wv"]), "wo": rows(i["L0_attn_Wo"]),
        "bq": np.ascontiguousarray(twice(i["L0_attn_bq"][None]).reshape(NG, P).T),
        "bk": np.ascontiguousarray(twice(i["L0_attn_bk"][None]).reshape(NG, P).T),
        "bv": i["L0_attn_bv"], "bo": i["L0_attn_bo"],
        "gamma": i["L0_attn_gamma"], "beta": i["L0_attn_beta"],
        "wt": rows(i["L0_ffn_weight"].T),
        "w1": rows(np.concatenate([i["L1_attn_Wq"].T, i["L1_attn_Wkv"].T], 1)),
        "wp": rows(i["L1_attn_Wproj"].T),
        "wsel": rows(np.concatenate([i["L1_ffn_sel_v_w"].T, i["L1_ffn_sel_o_w"].T], 1)),
        "cos": table(cos), "sin": table(sin),
        "rowsel": np.tile(np.repeat(np.array([[0, 1], [1, -1]], f), HD, 0), (HG, 1)),
        "rank": np.arange(E, 0, -1).astype(f),
        "route_scale": i["L1_ffn_route_scale"],
        "ident": np.eye(P, dtype=f),
        "wf": np.concatenate([
            i["L1_ffn_q_w"].reshape(FH, FP, DK, P).transpose(0, 3, 2, 1).reshape(FH, P, -1),
            i["L1_ffn_k_w"].reshape(FH, FP, DK, P).transpose(0, 3, 2, 1).reshape(FH, P, -1),
            i["L1_ffn_v_w"].reshape(FH, E, DK, P, FP).transpose(0, 3, 2, 1, 4).reshape(FH, P, -1),
            i["L1_ffn_o_w"].reshape(FH, E, FP, D).transpose(0, 2, 1, 3).reshape(FH, P, -1)], 2),
    }


def routed_heads(nc, dram, kept):
    ctx = ExitStack()
    with ctx:
        def sb(name, shape, dt=F32):
            return ctx.enter_context(nc.sbuf_tensor(name, shape, dt))

        def sem(name):
            return ctx.enter_context(nc.semaphore(name))

        acc, gates = kept["acc"], kept["gates"]
        QW, VW = DK * FP, DK * E * FP
        WCOLS = 2 * QW + VW + E * D
        SLICE = WCOLS // B
        FIRST = (slice(0, 2 * QW), slice(2 * QW, 2 * QW + VW), slice(2 * QW + VW, WCOLS))
        stage = sb("stage", [P, WCOLS])
        whl = [sb(f"whl{i}", [P, 2, WCOLS], F32R) for i in range(2)]
        xhl = sb("xhlB", [P, 2, DK, T], F32R)
        gs = sb("gs", [P, 2, NT, E])
        go = sb("go", [P, NT, E])
        qhl = sb("qhl", [P, 2, T], F32R)
        khl = sb("khl", [P, 2, T], F32R)
        vacc = sb("vacc", [P, 2, 2, FP])
        vsum = sb("vsum", [P, NT, FP])
        vhl = sb("vhl", [P, 2, NT, FP], F32R)
        probs = sb("probsB", [P, 2, T])
        nmax = sb("nmaxB", [P, NT])
        rowsum = sb("rowsum", [P, NT])
        rinv = sb("rinv", [P, NT])
        pT = sb("pTB", [P, 2, NT, T], F32R)
        cT = sb("cT", [P, 2, T], F32R)
        part = sb("part", [P, NT, 2, D])
        weighted = sb("weighted", [P, 4, D])
        total = sb("total", [P, D])
        ident = sb("identB", [P, P])
        ps = ctx.enter_context(nc.psum_tensor("psB", [P, 8, BANK], F32))
        PROJ, TR, CTX, RING = 0, 2, (0, 2), 4
        HALF = T // 2
        VCH, OCH = 2, E // 2
        CHUNKS = NT * (VCH + OCH)
        NRING = 4
        SCALAR_PAIRS, VECTOR_PAIRS = (1, 3), (0, 2)
        VOPS, OOPS = E + 1, E // 2 + 1
        GATED = NT * (VOPS + OOPS)
        SCALED = NT * E // 2
        ADDS = E // 2 + 1

        ident_loaded = sem("ident_loadedB")
        w_loaded = sem("w_loaded")
        acc_loaded = sem("acc_loaded")
        zeroed = sem("zeroed")
        w_hi0 = sem("w_hi0")
        w_split = sem("w_split")
        first_loaded = sem("first_loaded")
        values_loaded = sem("values_loaded")
        first_split = sem("first_split")
        w_hi = sem("w_hi")
        x_loaded = sem("x_loadedB")
        proj_ps = sem("proj_ps")
        qk_hi = sem("qk_hi")
        qk_lo = sem("qk_lo")
        chunk_ps = sem("chunk_ps")
        gated = sem("gated")
        scaled = sem("scaled")
        v_hi = sem("v_hi")
        v_lo = sem("v_lo")
        s_ps = sem("s_psB")
        max_ready = sem("max_readyB")
        exp_ready = sem("exp_readyB")
        t_ps = sem("t_psB")
        pt_hi = sem("pt_hi")
        pt_lo = sem("pt_lo")
        ctx_ps = sem("ctx_ps")
        ctx_hi = sem("ctx_hi")
        ctx_lo = sem("ctx_lo")
        go_ready = sem("go_ready")
        added = sem("added")
        dve_step = sem("dve_stepB")
        DVE_STEPS = 2

        block = ctx.enter_context(nc.Block())
        TERMS = ((0, 0), (0, 1), (1, 0))

        STEP = VOPS + OOPS

        def value_chunk(t, half):
            return t * (VCH + OCH) + half

        def output_chunk(t, pair, last):
            return t * OCH + pair if last else t * (VCH + OCH) + VCH + pair

        def output_gated(t, ops, last):
            return t * OOPS + ops if last else t * STEP + VOPS + ops

        def heads(eng, body, last_outputs):
            with eng.Fori(0, FH // 2) as hh:
                for parity in range(2):
                    h = hh * 2 + parity
                    first = hh * (2 * B) + parity * B
                    body(parity, 1 - parity, h, 0, B - 1, first)
                    with eng.Fori(1, B) as b:
                        body(parity, parity, h, b, b - 1, first + b)
            last_outputs(FH * B)

        @block.sync
        def _(sp):
            sp.dma_start(stage[:, FIRST[0]], dram["wf"][0, :, FIRST[0]]).then_inc(first_loaded, 16)
            sp.dma_start(xhl[:].rearrange("p a k t -> p (a k t)").bitcast(F32), dram["xs"][0]).then_inc(x_loaded, 16)
            sp.dma_start(stage[:, FIRST[1]], dram["wf"][0, :, FIRST[1]]).then_inc(values_loaded, 16)
            sp.dma_start(ident[:], dram["ident"]).then_inc(ident_loaded, 16)
            sp.dma_start(stage[:, FIRST[2]], dram["wf"][0, :, FIRST[2]]).then_inc(w_loaded, 16)
            for b in range(B):
                sp.dma_start(acc[:, b].rearrange("p t d -> p (t d)"), dram["x3"][b]).then_inc(acc_loaded, 16)
            sp.wait_ge(first_split, len(FIRST))
            with sp.Fori(0, FH) as h:
                sp.wait_ge(w_split, h * B + 1)
                sp.dma_start(stage[:], dram["wf"][bass.ds((h + 1) % FH, 1)].rearrange("o p n -> p (o n)")).then_inc(w_loaded, 16)
                with sp.Fori(0, B) as b:
                    sp.wait_ge(chunk_ps, h * (B * CHUNKS) + b * CHUNKS + value_chunk(NT - 1, VCH - 1) + 1)
                    sp.dma_start(xhl[:].rearrange("p a k t -> p (a k t)").bitcast(F32),
                                 dram["xs"][bass.ds((b + 1) % B, 1)].rearrange("o p n -> p (o n)")).then_inc(x_loaded, 16)
            sp.wait_ge(x_loaded, 16 * (FH * B + 1))
            sp.wait_ge(w_loaded, 16 * (FH + 1))

        @block.gpsimd
        def _(pool):
            g = nc.gpsimd
            pool.sem_inc(added, NT * ADDS)
            g.memset(whl[1][:, :, 2 * QW + VW:].bitcast(F32), 0.0).then_inc(zeroed, 1)
            pool.wait_ge(acc_loaded, 16 * B)

            def outputs(batch, i, last=False):
                for t in range(NT):
                    done = (i + 1) * (NT * ADDS) + t * ADDS
                    for k in range(1, E // 2):
                        pool.wait_ge(scaled, i * SCALED + SCALED + t * (E // 2) + k + 1)
                        pool.wait_ge(added, done + k - 1)
                        g.tensor_tensor(out=total[:], in0=weighted[:, 0, :] if k == 1 else total[:], in1=weighted[:, k, :],
                                        op=ALU.add).then_inc(added, 1)
                    pool.wait_ge(gated, i * GATED + GATED + output_gated(t, OOPS, last))
                    pool.wait_ge(added, done + E // 2 - 1)
                    g.tensor_tensor(out=total[:], in0=total[:], in1=part[:, t, 0, :], op=ALU.add).then_inc(added, 1)
                    pool.wait_ge(added, done + E // 2)
                    if isinstance(batch, int):
                        dst = acc[:, batch, t, :]
                    else:
                        dst = acc[:, bass.ds(batch, 1), t, :].rearrange("p o n -> p (o n)")
                    g.tensor_tensor(out=dst, in0=dst, in1=total[:], op=ALU.add).then_inc(added, 1)

            def iteration(parity, before, h, b, previous, i):
                pool.wait_ge(w_loaded, h * 16 + 32)
                if isinstance(b, int):
                    outputs(previous, i)
                cols = slice(0, SLICE) if isinstance(b, int) else bass.ds(b * SLICE, SLICE)
                hi = whl[1 - parity][:, 0, cols]
                g.tensor_copy(hi, stage[:, cols]).then_inc(w_hi, 1)
                pool.wait_ge(w_hi, i + 1)
                g.tensor_tensor(out=whl[1 - parity][:, 1, cols], in0=stage[:, cols], in1=hi.bitcast(F32),
                                op=ALU.subtract).then_inc(w_split, 1)
                if not isinstance(b, int):
                    outputs(previous, i)

            heads(pool, iteration, lambda i: outputs(B - 1, i, last=True))

        @block.scalar
        def _(act):
            a = nc.scalar
            for loaded, cols in zip((first_loaded, values_loaded, w_loaded), FIRST):
                act.wait_ge(loaded, 16)
                a.activation(whl[0][:, 0, cols], stage[:, cols], ACT.Copy).then_inc(w_hi0, 1)

            def outputs(t, i, last=False):
                if t == 0:
                    act.wait_ge(go_ready, i + 1)
                for n, pair in enumerate(SCALAR_PAIRS):
                    c = output_chunk(t, pair, last)
                    act.wait_ge(chunk_ps, i * CHUNKS + c + 1)
                    for e in range(2):
                        k = 2 * n + e
                        act.wait_ge(added, i * (NT * ADDS) + NT * ADDS + (t - 1) * ADDS + max(k, 1))
                        a.activation(weighted[:, k, :], ps[:, RING + c % NRING, e * D:(e + 1) * D], ACT.Copy,
                                     scale=go[:, t, 2 * pair + e:2 * pair + e + 1]).then_inc(scaled, 1)

            def iteration(parity, before, h, b, previous, i):
                for n, (dst, scale) in enumerate(((qhl, FFN_SCALE), (khl, 1.0))):
                    act.wait_ge(proj_ps, i * 2 + n + 1)
                    a.activation(dst[:, 0, :], ps[:, PROJ + 1 - n, :], ACT.Copy, scale=scale).then_inc(qk_hi, 1)

                def value_hi(t):
                    act.wait_ge(gated, i * GATED + GATED + t * STEP + VOPS)
                    a.activation(vhl[:, 0, t, :], vsum[:, t, :], ACT.Copy).then_inc(v_hi, 1)

                def exp(qt):
                    act.wait_ge(max_ready, i * NT + qt + 1)
                    a.activation(probs[:, qt % 2, :], ps[:, PROJ + qt % 2, :], ACT.Exp, bias=nmax[:, qt:qt + 1],
                                 accum_out=rowsum[:, qt:qt + 1]).then_inc(exp_ready, 1)

                def probs_hi(qt):
                    act.wait_ge(t_ps, i * NT + qt + 1)
                    a.activation(pT[:, 0, :, qt * P:(qt + 1) * P], ps[:, TR + qt % 2, :].rearrange("p (k q) -> p k q", q=P),
                                 ACT.Copy).then_inc(pt_hi, 1)

                def context_hi(half):
                    act.wait_ge(ctx_ps, i * 2 + half + 1)
                    a.activation(cT[:, 0, half * HALF:(half + 1) * HALF], ps[:, CTX[half], 0:HALF], ACT.Copy).then_inc(ctx_hi, 1)

                outputs(0, i)
                value_hi(0)
                value_hi(1)
                exp(0)
                outputs(1, i)
                exp(1)
                value_hi(2)
                probs_hi(0)
                probs_hi(1)
                exp(2)
                outputs(2, i)
                exp(3)
                value_hi(3)
                probs_hi(2)
                probs_hi(3)
                outputs(3, i)
                context_hi(0)
                context_hi(1)

            def last_outputs(i):
                for t in range(NT):
                    outputs(t, i, last=True)

            heads(act, iteration, last_outputs)

        @block.vector
        def _(dve):
            v = nc.vector
            for n, cols in enumerate(FIRST):
                dve.wait_ge(w_hi0, n + 1)
                v.tensor_tensor(out=whl[0][:, 1, cols], in0=stage[:, cols], in1=whl[0][:, 0, cols].bitcast(F32),
                                op=ALU.subtract).then_inc(first_split, 1)

            def weigh(i, ops, c, out, gate, first, experts, width, begin):
                dve.wait_ge(chunk_ps, i * CHUNKS + c + 1)
                for e in range(experts):
                    src = ps[:, RING + c % NRING, e * width:(e + 1) * width]
                    scale = gate[:, first + e:first + e + 1]
                    dst = out[:, e % 2, :]
                    if begin and e < 2:
                        v.tensor_scalar(out=dst, in0=src, scalar1=scale, scalar2=None, op0=ALU.mult).then_inc(gated, 1)
                    else:
                        dve.wait_ge(gated, i * GATED + GATED + ops - 1)
                        v.scalar_tensor_tensor(out=dst, in0=src, scalar=scale, in1=dst, op0=ALU.mult, op1=ALU.add).then_inc(gated, 1)
                    ops += 1
                return ops

            def outputs(t, i, last=False):
                if t == 0:
                    dve.wait_ge(go_ready, i + 1)
                dve.wait_ge(added, i * (NT * ADDS) + (t + 1) * ADDS)
                ops = output_gated(t, 0, last)
                for pair in VECTOR_PAIRS:
                    ops = weigh(i, ops, output_chunk(t, pair, last), part[:, t], go[:, t, :], 2 * pair, 2, D, pair == VECTOR_PAIRS[0])
                dve.wait_ge(gated, i * GATED + GATED + ops)
                v.tensor_tensor(out=part[:, t, 0, :], in0=part[:, t, 0, :], in1=part[:, t, 1, :], op=ALU.add).then_inc(gated, 1)

            for half in range(2):
                v.memset(cT[:, half, :].bitcast(F32), 0.0).then_inc(ctx_lo, 1)
            v.memset(go[:], 0.0).then_inc(go_ready, 1)

            def iteration(parity, before, h, b, previous, i):
                step = [0]

                def link(ins):
                    step[0] += 1
                    ins.then_inc(dve_step, 1)
                    dve.wait_ge(dve_step, i * DVE_STEPS + step[0])

                def values(t):
                    out = vacc[:, t % 2]
                    ops = t * STEP
                    for half in range(VCH):
                        ops = weigh(i, ops, value_chunk(t, half), out, gs[:, 0, t, :], half * (E // VCH), E // VCH, FP, half == 0)
                    dve.wait_ge(gated, i * GATED + GATED + ops)
                    v.tensor_tensor(out=vsum[:, t, :], in0=out[:, 0, :], in1=out[:, 1, :], op=ALU.add).then_inc(gated, 1)

                def value_lo(t):
                    dve.wait_ge(v_hi, i * NT + t + 1)
                    v.tensor_tensor(out=vhl[:, 1, t, :], in0=vsum[:, t, :], in1=vhl[:, 0, t, :].bitcast(F32), op=ALU.subtract).then_inc(v_lo, 1)

                def row_max(qt):
                    dve.wait_ge(s_ps, i * NT + qt + 1)
                    v.tensor_reduce(out=nmax[:, qt:qt + 1], in_=ps[:, PROJ + qt % 2, :], axis=AX.X, op=ALU.max,
                                    negate=True).then_inc(max_ready, 1)

                def probs_lo(qt):
                    dve.wait_ge(pt_hi, i * NT + qt + 1)
                    cols = slice(qt * P, (qt + 1) * P)
                    v.tensor_tensor(out=pT[:, 1, :, cols], in0=ps[:, TR + qt % 2, :].rearrange("p (k q) -> p k q", q=P),
                                    in1=pT[:, 0, :, cols].bitcast(F32), op=ALU.subtract).then_inc(pt_lo, 1)

                dve.wait_ge(go_ready, i + 1)
                batch = slice(b, b + 1) if isinstance(b, int) else bass.ds(b, 1)
                link(v.tensor_copy(gs[:].rearrange("p c t e -> p (c t e)"),
                                   gates[:, batch, bass.ds(h, 1)].rearrange("p o a c t e -> p (o a c t e)")))
                dve.wait_ge(qk_hi, i * 2 + 1)
                v.scalar_tensor_tensor(out=qhl[:, 1, :], in0=ps[:, PROJ + 1, :], scalar=FFN_SCALE, in1=qhl[:, 0, :].bitcast(F32),
                                       op0=ALU.mult, op1=ALU.subtract).then_inc(qk_lo, 1)
                dve.wait_ge(qk_hi, i * 2 + 2)
                v.tensor_tensor(out=khl[:, 1, :], in0=ps[:, PROJ, :], in1=khl[:, 0, :].bitcast(F32), op=ALU.subtract).then_inc(qk_lo, 1)
                def context_lo(half):
                    cols = slice(half * HALF, (half + 1) * HALF)
                    dve.wait_ge(ctx_hi, i * 2 + half + 1)
                    v.tensor_tensor(out=cT[:, 1, cols], in0=ps[:, CTX[half], 0:HALF], in1=cT[:, 0, cols].bitcast(F32),
                                    op=ALU.subtract).then_inc(ctx_lo, 1)

                values(0)
                outputs(0, i)
                values(1)
                row_max(0)
                outputs(1, i)
                row_max(1)
                value_lo(0)
                value_lo(1)
                values(2)
                row_max(2)
                outputs(2, i)
                row_max(3)
                probs_lo(0)
                probs_lo(1)
                value_lo(2)
                values(3)
                outputs(3, i)
                value_lo(3)
                probs_lo(2)
                probs_lo(3)
                context_lo(0)
                context_lo(1)
                dve.wait_ge(exp_ready, i * NT + NT)
                link(v.reciprocal(out=rinv[:], in_=rowsum[:]))
                dve.wait_ge(scaled, i * SCALED + SCALED + SCALED)
                v.tensor_tensor(out=go[:], in0=gs[:, 1], in1=rinv[:].unsqueeze(2).to_broadcast([P, NT, E]), op=ALU.mult).then_inc(go_ready, 1)
                assert step[0] == DVE_STEPS, step[0]

            def last_outputs(i):
                for t in range(NT):
                    outputs(t, i, last=True)

            heads(dve, iteration, last_outputs)

        @block.tensor
        def _(pe):
            mm = nc.tensor.matmul
            pe.sem_inc(gated, GATED)
            pe.sem_inc(scaled, SCALED)
            pe.sem_inc(w_split, 1)
            pe.wait_ge(ident_loaded, 16)

            def split_product(out, pairs):
                n = len(pairs) * len(TERMS)
                k = 0
                for stationary, moving in pairs:
                    for s, m in TERMS:
                        last = mm(out, stationary(s), moving(m), start=(k == 0), stop=(k == n - 1))
                        k += 1
                return last

            def ring_free(i, c, last=False):
                was, ago = c - NRING, 0
                if was < 0:
                    was, ago, last = was + CHUNKS, 1, False
                t, part_ = divmod(was, OCH if last else VCH + OCH)
                pair = part_ if last else part_ - VCH
                if pair < 0:
                    pe.wait_ge(gated, (i + 1 - ago) * GATED + t * STEP + (part_ + 1) * (E // VCH))
                elif pair in SCALAR_PAIRS:
                    pe.wait_ge(scaled, (i + 1 - ago) * SCALED + t * (E // 2) + 2 * SCALAR_PAIRS.index(pair) + 2)
                else:
                    pe.wait_ge(gated, (i + 1 - ago) * GATED + output_gated(t, 2 * VECTOR_PAIRS.index(pair) + 2, last))

            def outputs(t, i, w, last=False):
                if t == 0:
                    pe.wait_ge(ctx_lo, i * 2 + 2)
                for pair in range(OCH):
                    c = output_chunk(t, pair, last)
                    ring_free(i, c, last)
                    first = 2 * QW + VW + pair * BANK
                    split_product(ps[:, RING + c % NRING, :],
                                  [(lambda s: cT[:, s, t * P:(t + 1) * P],
                                    lambda m: w[:, m, first:first + BANK])]).then_inc(chunk_ps, 1)

            pe.wait_ge(first_split, 2)
            pe.wait_ge(zeroed, 1)

            def iteration(parity, before, h, b, previous, i):
                w = whl[parity]

                def weight(s, first, width):
                    return w[:, s, first:first + width]

                pe.wait_ge(w_split, h * B + 1)
                pe.wait_ge(x_loaded, i * 16 + 16)
                for n in range(2):
                    if n:
                        pe.wait_ge(ctx_lo, i * 2 + 1)
                    split_product(ps[:, PROJ + 1 - n, :],
                                  [(lambda s, k=k: weight(s, n * QW + k * FP, FP), lambda m, k=k: xhl[:, m, k, :])
                                   for k in range(DK)]).then_inc(proj_ps, 1)

                def values(t):
                    for half in range(2):
                        c = value_chunk(t, half)
                        ring_free(i, c)
                        split_product(ps[:, RING + c % NRING, :],
                                      [(lambda s, k=k: xhl[:, s, k, t * P:(t + 1) * P],
                                        lambda m, k=k: weight(m, 2 * QW + k * E * FP + half * BANK, BANK))
                                       for k in range(DK)]).then_inc(chunk_ps, 1)

                def scores(qt):
                    if qt >= 2:
                        pe.wait_ge(exp_ready, i * NT + qt - 1)
                    split_product(ps[:, PROJ + qt % 2, :],
                                  [(lambda s: qhl[:, s, qt * P:(qt + 1) * P], lambda m: khl[:, m, :])]).then_inc(s_ps, 1)

                def transposes(qt):
                    pe.wait_ge(exp_ready, i * NT + qt + 1)
                    if qt >= 2:
                        pe.wait_ge(pt_lo, i * NT + qt - 1)
                    for k in range(NT):
                        last = nc.tensor.transpose(ps[:, TR + qt % 2, k * P:(k + 1) * P], probs[:, qt % 2, k * P:(k + 1) * P], ident[:])
                    last.then_inc(t_ps, 1)

                def context(half):
                    pe.wait_ge(pt_lo, i * NT + 2 * half + 2)
                    k = 0
                    for kt in range(NT):
                        if not half:
                            pe.wait_ge(v_lo, i * NT + kt + 1)
                        for st, m in TERMS:
                            last = mm(ps[:, CTX[half], 0:HALF], vhl[:, st, kt, :], pT[:, m, kt, half * HALF:(half + 1) * HALF],
                                      start=(k == 0), stop=(k == NT * len(TERMS) - 1))
                            k += 1
                    last.then_inc(ctx_ps, 1)

                wo = whl[before]
                values(0)
                outputs(0, i, wo)
                values(1)
                pe.wait_ge(qk_lo, i * 2 + 2)
                scores(0)
                scores(1)
                outputs(1, i, wo)
                values(2)
                transposes(0)
                transposes(1)
                scores(2)
                scores(3)
                outputs(2, i, wo)
                values(3)
                transposes(2)
                transposes(3)
                outputs(3, i, wo)
                context(0)
                context(1)

            def last_outputs(i):
                for t in range(NT):
                    outputs(t, i, whl[(FH - 1) % 2], last=True)

            heads(pe, iteration, last_outputs)


def last_norm(nc, dram, kept):
    ctx = ExitStack()
    with ctx:
        acc = kept["acc"]
        stats = ctx.enter_context(nc.sbuf_tensor("statsC", [P, B, NT, 6], F32))
        mv = ctx.enter_context(nc.sbuf_tensor("mvC", [P, B, NT, 2], F32))
        ve = ctx.enter_context(nc.sbuf_tensor("veC", [P, B, NT], F32))
        rstd = ctx.enter_context(nc.sbuf_tensor("rstdC", [P, B, NT], F32))
        mhalf = ctx.enter_context(nc.sbuf_tensor("mhalfC", [P, NT], F32))
        zero = ctx.enter_context(nc.sbuf_tensor("zeroC", [P, NT], F32))
        shift = ctx.enter_context(nc.sbuf_tensor("shiftC", [P, B, NT], F32))
        stats_ready = ctx.enter_context(nc.semaphore("stats_readyC"))
        var_ready = ctx.enter_context(nc.semaphore("var_readyC"))
        pool_step = ctx.enter_context(nc.semaphore("pool_stepC"))
        rstd_ready = ctx.enter_context(nc.semaphore("rstd_readyC"))
        out_ready = ctx.enter_context(nc.semaphore("out_ready"))
        stored = ctx.enter_context(nc.semaphore("storedC"))
        block = ctx.enter_context(nc.Block())

        @block.vector
        def _(dve):
            v = nc.vector

            for b in range(B):
                for t in range(NT):
                    last = v.bn_stats(out=stats[:, b, t, :], in_=acc[:, b, t, :])
                last.then_inc(stats_ready, 1)
                dve.wait_ge(stats_ready, b + 1)
                for t in range(NT):
                    last = v.bn_aggr(out=mv[:, b, t, :], in_=stats[:, b, t, :])
                last.then_inc(var_ready, 1)

        @block.scalar
        def _(act):
            for b in range(B):
                act.wait_ge(rstd_ready, b + 1)
                for t in range(NT):
                    last = nc.scalar.activation(acc[:, b, t, :], acc[:, b, t, :], ACT.Identity, bias=shift[:, b, t:t + 1],
                                                scale=rstd[:, b, t:t + 1])
                last.then_inc(out_ready, 1)

        @block.gpsimd
        def _(pool):
            g = nc.gpsimd
            g.memset(mhalf[:], -0.5).then_inc(pool_step, 1)
            g.memset(zero[:], 0.0).then_inc(pool_step, 1)
            for b in range(B):
                pool.wait_ge(var_ready, b + 1)
                g.tensor_scalar(out=ve[:, b, :], in0=mv[:, b, :, 1], scalar1=LN_EPS, scalar2=None, op0=ALU.add).then_inc(pool_step, 1)
                pool.wait_ge(pool_step, 3 * b + 3)
                g.tensor_tensor(out=rstd[:, b, :], in0=ve[:, b, :], in1=mhalf[:], op=ALU.pow).then_inc(pool_step, 1)
                pool.wait_ge(pool_step, 3 * b + 4)
                g.tensor_tensor(out=shift[:, b, :], in0=mv[:, b, :, 0], in1=rstd[:, b, :], op=ALU.mult).then_inc(pool_step, 1)
                pool.wait_ge(pool_step, 3 * b + 5)
                g.tensor_tensor(out=shift[:, b, :], in0=zero[:], in1=shift[:, b, :], op=ALU.subtract).then_inc(rstd_ready, 1)

        @block.sync
        def _(sp):
            for b in range(B):
                sp.wait_ge(out_ready, b + 1)
                sp.dma_start(dram["out"][b].rearrange("(t p) d -> p t d", p=P), acc[:, b]).then_inc(stored, 16)
            sp.wait_ge(stored, 16 * B)


def build(nc, dram):
    with nc.sbuf_tensor("gates", [P, B, FH, 2, NT, E], F32) as gates:
        kept = {"gates": gates}
        layer0_and_layer1_attention(nc, dram, kept)
        with nc.sbuf_tensor("acc", [P, B, NT, D], F32) as acc:
            kept["acc"] = acc
            routed_heads(nc, dram, kept)
            last_norm(nc, dram, kept)


def kernel(**inputs):
    import concourse.bacc as bacc
    from concourse.bass_utils import run_bass_kernel_spmd

    nc = bacc.Bacc("TRN2", target_bir_lowering=False, num_devices=1)
    arrays = {f"in_{name}": a for name, a in layouts(inputs).items()}
    dram = {name[3:]: nc.dram_tensor(name, a.shape, mybir.dt.from_np(a.dtype), kind="ExternalInput").ap()
            for name, a in arrays.items()}
    dram["xs"] = nc.dram_tensor("routed_input", [B, P, 2 * DK * T], F32, kind="Internal").ap()
    dram["x3"] = nc.dram_tensor("routed_residual", [B, P, NT * D], F32, kind="Internal").ap()
    dram["out"] = nc.dram_tensor("out_0", [B, T, D], F32, kind="ExternalOutput").ap()
    build(nc, dram)
    return run_bass_kernel_spmd(nc, [arrays], core_ids=[0]).results[0]["out_0"]
```
